# Optimizing a Trainium2 kernel written in Bass

```python
import numpy as np
import jax
import jax.numpy as jnp

def _softmax(x, axis=-1):
    return jax.nn.softmax(x, axis=axis)

def _gelu(x):
    return jax.nn.gelu(x, approximate=True)

def _silu(x):
    return jax.nn.silu(x)

def _sigmoid(x):
    return jax.nn.sigmoid(x)

def _layernorm(x, axis=-1, eps=1e-05):
    m = jnp.mean(x, axis=axis, keepdims=True)
    v = jnp.var(x, axis=axis, keepdims=True)
    return (x - m) / jnp.sqrt(v + eps)

def _scatter_add(tgt, idx, src, axis=0):
    return tgt.at[idx].add(src)

def _segment_sum(src, seg, n):
    return jax.ops.segment_sum(src, seg, n)
kernel_name = 'mk_early_fusion_embed_d1_tok_img768_r4_87c1d6'

def setup_inputs(seed: int=0):
    np.random.seed(seed)
    _w = jnp.asarray

    def _rec_inputs():
        import jax
        import jax.numpy as jnp
        _rk = jax.random.key(seed)
        x = -0.00016672 + 0.999947 * jax.random.normal(jax.random.fold_in(_rk, 1), (32, 3, 96, 96), jnp.float32)
        x_txt = jax.random.randint(jax.random.fold_in(_rk, 51), (32, 128), 0, 119, jnp.int32)
        return (x, x_txt)
    x, x_txt = _rec_inputs()

    def _L0_tok_setup():
        import jax, jax.numpy as jnp
        import numpy as np
        B, C, H, W = (64, 3, 96, 96)
        P = 16
        NH, NW = (H // P, W // P)
        N = NH * NW
        PATCH_DIM = C * P * P
        DIM = 192

        def _layernorm(x, g, b, eps=1e-05):
            mu = jnp.mean(x, axis=-1, keepdims=True)
            var = jnp.var(x, axis=-1, keepdims=True)
            return (x - mu) * jax.lax.rsqrt(var + eps) * g + b
        key = jax.random.key(seed)
        ks = jax.random.split(key, 8)
        img = jax.random.normal(ks[0], (B, C, H, W), dtype=jnp.float32)
        ln1_g = jnp.ones((PATCH_DIM,), jnp.float32)
        ln1_b = jnp.zeros((PATCH_DIM,), jnp.float32)
        W_lin = jax.random.normal(ks[1], (PATCH_DIM, DIM), jnp.float32) / np.sqrt(PATCH_DIM)
        b_lin = jnp.zeros((DIM,), jnp.float32)
        ln2_g = jnp.ones((DIM,), jnp.float32)
        ln2_b = jnp.zeros((DIM,), jnp.float32)
        pos_embedding = jax.random.normal(ks[2], (1, N + 1, DIM), jnp.float32)
        cls_token = jax.random.normal(ks[3], (1, 1, DIM), jnp.float32)
        return {'img': img, 'ln1_g': ln1_g, 'ln1_b': ln1_b, 'W_lin': W_lin, 'b_lin': b_lin, 'ln2_g': ln2_g, 'ln2_b': ln2_b, 'pos_embedding': pos_embedding, 'cls_token': cls_token}
    _L0_tok_all = _L0_tok_setup()
    _L0_tok_in = {k: v for k, v in _L0_tok_all.items() if k in ('ln1_g', 'ln1_b', 'W_lin', 'b_lin', 'ln2_g', 'ln2_b', 'pos_embedding', 'cls_token')}
    del _L0_tok_all

    def _L0_txt_setup():
        import jax, jax.numpy as jnp
        import numpy as np
        B, S = (64, 128)
        K = 7 * 4
        D = 192
        N_ATOMS = 118
        key = jax.random.key(seed)
        k1, k2, k3, k4 = jax.random.split(key, 4)
        configs = jax.random.randint(k1, (N_ATOMS, K), 0, 4).astype(jnp.float32)
        atom_configs = jnp.concatenate([jnp.zeros((1, K), jnp.float32), configs], axis=0)
        atom_indices = jax.random.randint(k2, (B, S), 0, N_ATOMS + 1)
        subshell_embeds = jax.random.normal(k3, (K, D), jnp.float32)
        occupancy_embeds = jax.random.normal(k4, (K, D), jnp.float32)
        return {'atom_indices': atom_indices, 'atom_configs': atom_configs, 'subshell_embeds': subshell_embeds, 'occupancy_embeds': occupancy_embeds}
    _L0_txt_all = _L0_txt_setup()
    _L0_txt_in = {k: v for k, v in _L0_txt_all.items() if k in ('atom_configs', 'subshell_embeds', 'occupancy_embeds')}
    del _L0_txt_all

    def _L0_attn_setup():
        import jax, jax.numpy as jnp
        import numpy as np
        N_HEADS = 12
        key = jax.random.key(seed)
        k1, k2, k3 = jax.random.split(key, 3)
        B, S, W = (8, 256, 192)
        x = jax.random.normal(k1, (B, S, W), dtype=jnp.float32)
        w_qkv = jax.random.normal(k2, (W, 3 * W), dtype=jnp.float32) * W ** (-0.5)
        w_out = jax.random.normal(k3, (W, W), dtype=jnp.float32) * W ** (-0.5)
        return {'x': x, 'w_qkv': w_qkv, 'w_out': w_out}
    _L0_attn_all = _L0_attn_setup()
    _L0_attn_in = {k: v for k, v in _L0_attn_all.items() if k in ('w_qkv', 'w_out')}
    del _L0_attn_all

    def _L0_ffn_setup():
        import jax, jax.numpy as jnp
        import numpy as np
        B, S, D, F, E = (4, 512, 192, 768, 8)
        key = jax.random.key(seed)
        ks = jax.random.split(key, 5)
        return {'x': jax.random.normal(ks[0], (B, S, D), dtype=jnp.float32), 'Ws': jax.random.normal(ks[1], (D, E), dtype=jnp.float32) * 0.02, 'bs': jnp.zeros((E,), dtype=jnp.float32), 'W1': jax.random.normal(ks[2], (E, D, F), dtype=jnp.float32) * 0.02, 'b1': jnp.zeros((E, F), dtype=jnp.float32), 'W2': jax.random.normal(ks[3], (E, F, D), dtype=jnp.float32) * 0.02, 'b2': jnp.zeros((E, D), dtype=jnp.float32)}
    _L0_ffn_all = _L0_ffn_setup()
    _L0_ffn_in = {k: v for k, v in _L0_ffn_all.items() if k in ('Ws', 'bs', 'W1', 'b1', 'W2', 'b2')}
    del _L0_ffn_all
    return {'x': x, 'x_txt': x_txt, 'L0_tok_ln1_g': _L0_tok_in['ln1_g'], 'L0_tok_ln1_b': _L0_tok_in['ln1_b'], 'L0_tok_W_lin': _L0_tok_in['W_lin'], 'L0_tok_b_lin': _L0_tok_in['b_lin'], 'L0_tok_ln2_g': _L0_tok_in['ln2_g'], 'L0_tok_ln2_b': _L0_tok_in['ln2_b'], 'L0_tok_pos_embedding': _L0_tok_in['pos_embedding'], 'L0_tok_cls_token': _L0_tok_in['cls_token'], 'L0_txt_atom_configs': _L0_txt_in['atom_configs'], 'L0_txt_subshell_embeds': _L0_txt_in['subshell_embeds'], 'L0_txt_occupancy_embeds': _L0_txt_in['occupancy_embeds'], 'L0_attn_w_qkv': _L0_attn_in['w_qkv'], 'L0_attn_w_out': _L0_attn_in['w_out'], 'L0_ffn_Ws': _L0_ffn_in['Ws'], 'L0_ffn_bs': _L0_ffn_in['bs'], 'L0_ffn_W1': _L0_ffn_in['W1'], 'L0_ffn_b1': _L0_ffn_in['b1'], 'L0_ffn_W2': _L0_ffn_in['W2'], 'L0_ffn_b2': _L0_ffn_in['b2']}

def reference(x, x_txt, L0_tok_ln1_g, L0_tok_ln1_b, L0_tok_W_lin, L0_tok_b_lin, L0_tok_ln2_g, L0_tok_ln2_b, L0_tok_pos_embedding, L0_tok_cls_token, L0_txt_atom_configs, L0_txt_subshell_embeds, L0_txt_occupancy_embeds, L0_attn_w_qkv, L0_attn_w_out, L0_ffn_Ws, L0_ffn_bs, L0_ffn_W1, L0_ffn_b1, L0_ffn_W2, L0_ffn_b2):
    import jax
    import jax.numpy as jnp

    def _L0_tok_ref(img, ln1_g, ln1_b, W_lin, b_lin, ln2_g, ln2_b, pos_embedding, cls_token):
        import jax, jax.numpy as jnp
        import numpy as np
        B, C, H, W = (64, 3, 96, 96)
        P = 16
        NH, NW = (H // P, W // P)
        N = NH * NW
        PATCH_DIM = C * P * P
        DIM = 192

        def _layernorm(x, g, b, eps=1e-05):
            mu = jnp.mean(x, axis=-1, keepdims=True)
            var = jnp.var(x, axis=-1, keepdims=True)
            return (x - mu) * jax.lax.rsqrt(var + eps) * g + b
        b = img.shape[0]
        x = img.reshape(b, C, NH, P, NW, P)
        x = jnp.transpose(x, (0, 2, 4, 3, 5, 1))
        x = x.reshape(b, N, PATCH_DIM)
        x = _layernorm(x, ln1_g, ln1_b)
        x = jnp.einsum('bnp,pd->bnd', x, W_lin) + b_lin
        x = _layernorm(x, ln2_g, ln2_b)
        cls = jnp.broadcast_to(cls_token, (b, 1, DIM))
        x = jnp.concatenate([cls, x], axis=1)
        x = x + pos_embedding[:, :N + 1]
        return x

    def _L0_txt_ref(atom_indices, atom_configs, subshell_embeds, occupancy_embeds):
        import jax, jax.numpy as jnp
        import numpy as np
        B, S = (64, 128)
        K = 7 * 4
        D = 192
        N_ATOMS = 118
        atom_repr = atom_configs[atom_indices]
        base_repr = (atom_repr != 0).astype(subshell_embeds.dtype)
        occ_repr = jnp.maximum(atom_repr - 1.0, 0.0)
        base_vec = jnp.einsum('bsk,kd->bsd', base_repr, subshell_embeds)
        occ_vec = jnp.einsum('bsk,kd->bsd', occ_repr, occupancy_embeds)
        return base_vec + occ_vec

    def _L0_attn_ref(x, w_qkv, w_out):
        import jax, jax.numpy as jnp
        import numpy as np
        N_HEADS = 12
        B, S, W = x.shape
        H = N_HEADS
        D = W // H
        scale = W ** (-0.5)
        qkv = x @ w_qkv
        q, k, v = jnp.split(qkv, 3, axis=2)
        q = q.reshape(B, S, H, D)
        k = k.reshape(B, S, H, D)
        attn_score = jnp.einsum('binh,bjnh->bijn', q, k) * scale
        attn_weight = jax.nn.softmax(attn_score, axis=2)
        out = jnp.einsum('bijn,bjnh->binh', attn_weight, k)
        out = out.reshape(B, S, W)
        return out @ w_out

    def _L0_ffn_ref(x, Ws, bs, W1, b1, W2, b2):
        import jax, jax.numpy as jnp
        import numpy as np
        B, S, D, F, E = (4, 512, 192, 768, 8)
        b, s, d = x.shape
        xt = x.reshape(-1, d)
        logits = xt @ Ws + bs
        probs = jax.nn.softmax(logits, axis=-1)
        routes = jnp.argmax(probs, axis=-1)
        prob_max = jnp.max(probs, axis=-1)
        h = jax.nn.gelu(jnp.einsum('td,edf->etf', xt, W1) + b1[:, None, :], approximate=False)
        y = jnp.einsum('etf,efd->etd', h, W2) + b2[:, None, :]
        out = jnp.take_along_axis(y, routes[None, :, None], axis=0)[0]
        out = out * prob_max[:, None]
        return out.reshape(b, s, d)
    h = _L0_tok_ref(x, L0_tok_ln1_g, L0_tok_ln1_b, L0_tok_W_lin, L0_tok_b_lin, L0_tok_ln2_g, L0_tok_ln2_b, L0_tok_pos_embedding, L0_tok_cls_token)
    h = jnp.concatenate([h, _L0_txt_ref(x_txt, L0_txt_atom_configs, L0_txt_subshell_embeds, L0_txt_occupancy_embeds)], axis=1)
    h = h + _L0_attn_ref(_layernorm(h, axis=-1), L0_attn_w_qkv, L0_attn_w_out)
    h = h + _L0_ffn_ref(_layernorm(h, axis=-1), L0_ffn_Ws, L0_ffn_bs, L0_ffn_W1, L0_ffn_b1, L0_ffn_W2, L0_ffn_b2)
    return h

_drawn_inputs = setup_inputs


def setup_inputs(seed=0):
    import zlib

    import numpy as np

    out = dict(_drawn_inputs(seed))
    spreads = {'L0_tok_ln1_g': (1.0, 0.6),
     'L0_tok_ln1_b': (0.0, 0.8),
     'L0_tok_b_lin': (0.0, 0.8),
     'L0_tok_ln2_g': (1.0, 0.6),
     'L0_tok_ln2_b': (0.0, 0.8),
     'L0_ffn_bs': (0.0, 0.8),
     'L0_ffn_b1': (0.0, 0.8),
     'L0_ffn_b2': (0.0, 0.8)}
    factors = {'L0_tok_cls_token': 5.076, 'L0_ffn_Ws': 8.0, 'L0_ffn_W1': 8.0, 'L0_ffn_W2': 8.0}
    for name, (base, spread) in spreads.items():
        noise = np.random.default_rng([zlib.crc32(name.encode()), seed]).standard_normal(out[name].shape)
        drawn = base * np.exp(spread * noise) if base else spread * noise
        out[name] = jnp.asarray(drawn.astype(out[name].dtype))
    for name, factor in factors.items():
        out[name] = (out[name] * factor).astype(out[name].dtype)
    return out
```

```python
from contextlib import ExitStack

import numpy as np

import concourse.bass as bass
from concourse import mybir

F32 = mybir.dt.float32
F16 = mybir.dt.float16
BF16 = mybir.dt.bfloat16
I32 = mybir.dt.int32
ALU = mybir.AluOpType
ACT = mybir.ActivationFunctionType
AX = mybir.AxisListType

P = 128
B, C, IMG, PATCH = 32, 3, 96, 16
G = IMG // PATCH
NPATCH = G * G
NIMG = NPATCH + 1
TXT = 128
S = NIMG + TXT
SP = TXT + 64
D = 192
DK = D // 2
H, DH = 12, 16
HG, HJ = 3, 4
NAT, NCFG = 119, 28
E, F = 8, 768
FC = F // P
T = B * S
CAP = (T + P + 31) // 32 * 32
ROW = 196
C_MEAN, C_RSTD, C_PROB, C_ID = 192, 193, 194, 195
NT = T // P + E
EPS = 1e-5
QK_SCALE = 8.0
MAX_SCALE = 16.0
W_SCALE = 64.0
PAD_ID = 1 << 20

K_ID, K_TRI, K_KLO, K_K2M, K_K2A, K_VALID, K_IDS, K_BASE, K_FIRST, K_TILE, K_PART, K_PADID, K_HALF = (
    0, 128, 256, 257, 258, 259, 261, 263, 271, 287, 287 + NT, 288 + NT, 289 + NT)
K_END = 291 + NT


def shape_constants():
    k = np.zeros((P, K_END), np.float32)
    p = np.arange(P)
    r = p % 32
    k[:, K_ID:K_ID + P] = np.eye(P)
    k[:, K_TRI:K_TRI + P] = p[:, None] < p[None, :]
    k[:, K_KLO] = -(r >= DH).astype(np.float32)
    k[:, K_K2M] = r < DH
    k[:, K_K2A] = MAX_SCALE * (r == DH)
    k[:, K_VALID] = 1
    k[:, K_VALID + 1] = p < NIMG
    k[:, K_IDS] = NIMG + p
    k[:, K_IDS + 1] = p
    k[:, K_BASE:K_BASE + E] = CAP * np.arange(E)
    k[:, K_FIRST:K_FIRST + 2 * E] = np.tile(E - np.arange(E), 2)
    k[:, K_TILE:K_TILE + NT] = np.arange(NT)
    k[:, K_PART] = p
    k[:, K_PADID] = PAD_ID
    k[:, K_HALF] = p < NIMG
    k[:, K_HALF + 1] = (p >= 64) & (p < 64 + NIMG)
    return k


def spread(ap, axis, n):
    shape = list(ap.shape)
    shape[axis] = n
    return ap.broadcast_to(shape)


class Turn:

    def __init__(self, c, r=None, n=1):
        self.c, self.r, self.n = c, r, n

    def plus(self, d):
        return Turn(self.c + d, self.r, self.n)

    def lin(self, a, k=0):
        return a * self.c + k if self.r is None else self.r * (a * self.n) + (a * self.c + k)

    def of(self, m):
        return self.c // m if self.r is None else self.r * (self.n // m) + self.c // m

    def slot(self, m):
        return self.c % m

    def exists(self, count):
        return self.r is not None or 0 <= self.c < count


class Event:

    def __init__(self, sem, per=1):
        self.sem, self.per = sem, per

    def wait(self, eng, item, k=None):
        if item.r is None and item.c < 0:
            return
        eng.wait_ge(self.sem, item.lin(self.per, self.per if k is None else k))


def build(nc, x, x_txt, ln1_g, ln1_b, W_lin, b_lin, ln2_g, ln2_b, pos, cls_tok, cfg, sub_e, occ_e,
          w_qkv, w_out, Ws, bs, W1, b1, W2, b2, consts, out):
    ctx = ExitStack()
    with ctx:
        def sb(name, shape, dt=F32):
            return ctx.enter_context(nc.sbuf_tensor(name, shape, dt))

        def sem(name):
            return ctx.enter_context(nc.semaphore(name))

        def ev(name, per=1):
            return Event(sem(name), per)

        bank = [ctx.enter_context(nc.psum_tensor(f"bank{i}", [P, 512], F32)) for i in range(8)]

        himg = nc.dram_tensor("himg", (B, NIMG, D), F32, kind="Internal").ap()
        atoms = nc.dram_tensor("atoms", (NAT, D), F32, kind="Internal").ap()
        routed = nc.dram_tensor("routed", (E * CAP + P, ROW), F32, kind="Internal").ap()

        con = sb("con", [P, K_END])
        neg_id = sb("neg_id", [P, P], BF16)
        tri = sb("tri", [P, P], BF16)
        ones = sb("ones", [P, P], BF16)
        one16 = sb("one16", [1, P], F16)
        halfs = sb("halfs", [P, 2 * G])
        ident = con[:, K_ID:K_ID + P]
        wqk_hi = sb("wqk_hi", [DK, 2, 2, HG * P], F16)
        wqk_lo = sb("wqk_lo", [DK, 2, 2, HG * P], F16)
        wo = sb("wo", [P, HG, D])
        ws = sb("ws", [DK, 2, E])
        bs_all = sb("bs_all", [P, 2, E])
        w2_hi = sb("w2_hi", [P, E * FC * D], F16)
        w2_lo = sb("w2_lo", [P, E * FC * D], F16)
        b1T = sb("b1T", [P, E * FC])
        b2_hi = sb("b2_hi", [1, E * D], F16)
        b2_lo = sb("b2_lo", [1, E * D], F16)
        wstage1 = sb("wstage1", [DK, F])
        wstage2 = sb("wstage2", [P, 3 * D])

        X = [sb(f"x{i}", [P, 2, D]) for i in range(4)]
        txt_i = sb("txt_i", [P, B + 1], I32)
        txt_now = [sb(f"txt_now{i}", [P, 1], I32) for i in range(2)]
        padrow = sb("padrow", [P, ROW])
        st1 = sb("st1", [P, 2, 6])
        mv1 = sb("mv1", [P, 2, 2])
        var1 = sb("var1", [P, 2])
        rstd1 = sb("rstd1", [P, 2])
        xn = sb("xn", [P, 2, D])
        xh = [sb(f"xh{i}", [DK, 2, SP], F16) for i in range(2)]
        xl = [sb(f"xl{i}", [DK, 2, SP], F16) for i in range(2)]
        kh = sb("kh", [P, HG, S], F16)
        k1 = [sb(f"k1_{i}", [P, HG, SP], F16) for i in range(2)]
        k2 = [sb(f"k2_{i}", [P, HG, SP], F16) for i in range(2)]
        q1 = [sb(f"q1_{i}", [P, HG, SP], F16) for i in range(2)]
        q2 = [sb(f"q2_{i}", [P, HG, S], F16) for i in range(2)]
        qlo = sb("qlo", [P, HG, S], F16)
        V = [sb(f"v{i}", [P, 2, H, 32]) for i in range(2)]
        mxa = sb("mxa", [P, HG, P], BF16)
        mxb = sb("mxb", [P, 2, P], BF16)
        pa = [sb(f"pa{i}", [P, HG * S]) for i in range(2)]
        pb = [sb(f"pb{i}", [P, 2 * S]) for i in range(2)]
        den = sb("den", [P, HG * S])
        ot = sb("ot", [P, HG, S])
        hrow = [sb(f"hrow{i}", [P, 2, ROW]) for i in range(2)]
        st2 = sb("st2", [P, 2, 6])
        mv2 = sb("mv2", [P, 2, 2])
        var2 = sb("var2", [P, 2])
        xn2 = sb("xn2", [P, 2, D])
        xT2 = sb("xT2", [DK, 2, 2 * P])
        lg = sb("lg", [P, 2, E])
        lgm = sb("lgm", [P, 2])
        lgd = sb("lgd", [P, 2, E])
        lge = sb("lge", [P, 2, E])
        esum = sb("esum", [P, 2])
        first = sb("first", [P, 2, E])
        firstm = sb("firstm", [P, 2])
        oh = sb("oh", [P, 2, E])
        ohb = sb("ohb", [P, 2, E], BF16)
        count = sb("count", [P, E])
        rank = sb("rank", [P, 2, E])
        slotf = sb("slotf", [P, 2])
        slot_i = [sb(f"slot_i{i}", [P, 2], I32) for i in range(2)]
        ids = sb("ids", [P, 2])

        embed_ctx = ExitStack()

        def sbe(name, shape, dt=F32):
            return embed_ctx.enter_context(nc.sbuf_tensor(name, shape, dt))

        IH = B // 2
        PR = IH * G
        xi = [sbe(f"xi{i}", [PR, C, PATCH * IMG]) for i in range(2)]
        sti = sbe("sti", [PR, 2 * G, C, 6])
        mvi = sbe("mvi", [PR, 2 * G, 2])
        vari = sbe("vari", [PR, 2 * G])
        rstdi = sbe("rstdi", [PR, 2 * G])
        xni = [sbe(f"xni{i}", [PR, C * 2, P]) for i in range(2)]
        xTi = [sbe(f"xTi{i}", [P, C * 2, PR]) for i in range(2)]
        wl = sbe("wl", [P, 2, C, D])
        wlg = sbe("wlg", [P, 2, C, D])
        g1 = sbe("g1", [P, 2, C])
        b1v = sbe("b1v", [P, 2, C])
        bl_all = sbe("bl_all", [P, D])
        bias_all = sbe("bias_all", [P, D])
        g2_all = sbe("g2_all", [P, D])
        b2_all = sbe("b2_all", [P, D])
        posr = sbe("posr", [PR, G * D])
        clsr = sbe("clsr", [B, D])
        posc = sbe("posc", [B, D])
        yi = sbe("yi", [PR, G, D])
        sty = sbe("sty", [PR, G, 6])
        mvy = sbe("mvy", [PR, G, 2])
        vary = sbe("vary", [PR, G])
        rstdy = sbe("rstdy", [PR, G])
        img = [sbe(f"img{i}", [PR, G, D]) for i in range(2)]
        cfg_s = sbe("cfg_s", [NAT, NCFG])
        cfg2 = sbe("cfg2", [NAT, 2, 32])
        cfgT = sbe("cfgT", [32, 2, NAT])
        emb = sbe("emb", [NCFG, 2, D])
        tab = sbe("tab", [NAT, D])

        wqkv = sbe("wqkv", [DK, 2, 2 * D])
        wdup = sbe("wdup", [DK, 2, 2 * H, 2, DH])
        b1r = sbe("b1r", [E * FC, P])
        b2r = sbe("b2r", [1, E * D])
        txt = sbe("txt", [B, P], I32)
        txt_f = sbe("txt_f", [B, P])
        txt_neg = sbe("txt_neg", [B, P])
        embed_ctx.close()

        w1_hi = sb("w1_hi", [DK, E * 2 * F], F16)
        w1_lo = sb("w1_lo", [DK, E * 2 * F], F16)
        pad_f = sb("pad_f", [P, E])
        pad_i = sb("pad_i", [P, E], I32)
        cnt_f = sb("cnt_f", [1, E])
        cnt_i = sb("cnt_i", [1, E], I32)
        ntile = sb("ntile", [1, E])
        cum = sb("cum", [1, E])
        skip = sb("skip", [1, E])
        reached = sb("reached", [1, NT])
        tl_f = sb("tl_f", [1, 2, NT])
        tl = sb("tl", [1, 2, NT], I32)
        R = [sb(f"r{i}", [P, ROW]) for i in range(4)]
        xe = sb("xe", [P, D])
        xeh = [sb(f"xeh{i}", [DK, 2, P], F16) for i in range(2)]
        xel = [sb(f"xel{i}", [DK, 2, P], F16) for i in range(2)]
        hf = [sb(f"hf{i}", [P, FC, P]) for i in range(2)]
        hh = [sb(f"hh{i}", [P, FC, P], F16) for i in range(2)]
        hl = [sb(f"hl{i}", [P, FC, P], F16) for i in range(2)]
        res = [sb(f"res{i}", [P, D]) for i in range(4)]

        con_in = sem("con_in")
        patch_w_in = sem("patch_w_in")
        image_in = [sem(f"image_in{i}") for i in range(2)]
        atom_in = sem("atom_in")
        attn_w_in = sem("attn_w_in")
        route_w_in = sem("route_w_in")
        atoms_out = sem("atoms_out")
        himg_out = sem("himg_out")
        pool_zeroed = sem("pool_zeroed")
        pool_setup = sem("pool_setup")
        dve_setup = sem("dve_setup")
        pe_setup = sem("pe_setup")
        act_setup = sem("act_setup")
        dve_patch = sem("dve_patch")
        patch_stats = sem("patch_stats")
        patch_norm = sem("patch_norm")
        pe_patchT = sem("pe_patchT")
        act_patchT = sem("act_patchT")
        pe_patchY = sem("pe_patchY")
        patch_y = sem("patch_y")
        y_stats = sem("y_stats")
        img_ready = sem("img_ready")
        pool_patch = sem("pool_patch")
        img_step = sem("img_step")
        w_ready = sem("w_ready")
        list_step = sem("list_step")
        pool_apart, dve_apart = sem("pool_apart"), sem("dve_apart")

        xi_in = [sem(f"xi_in{i}") for i in range(4)]
        xt_in = [sem(f"xt_in{i}") for i in range(4)]
        w1_in, w2_in = ev("w1_in", 16), ev("w2_in", 16)
        w_split = ev("w_split", 6)
        ln_stats = ev("ln_stats", 4)
        ln_rstd = ev("ln_rstd", 2)
        x_norm = ev("x_norm")
        x_T = ev("x_T")
        x_hi = ev("x_hi")
        x_lo = ev("x_lo")
        k_proj, q_proj, v_proj = ev("k_proj"), ev("q_proj"), ev("v_proj")
        k_hi, q_hi, v_out = ev("k_hi"), ev("q_hi"), ev("v_out")
        k_st1, k_st2, q_rest, q_st2 = ev("k_st1"), ev("k_st2"), ev("q_rest"), ev("q_st2")
        max_scores = ev("max_scores", 8)
        max_taken = ev("max_taken", 8)
        max_rows = ev("max_rows")
        sc_a, sc_b = ev("sc_a", 4), ev("sc_b", 4)
        exp_a, exp_b = ev("exp_a", 4), ev("exp_b", 4)
        pv = ev("pv", 4)
        o_norm = ev("o_norm", 3)
        o_proj = ev("o_proj")
        h_sum = ev("h_sum", 2)
        ln2_stats = ev("ln2_stats", 4)
        ln2_rstd = ev("ln2_rstd", 3)
        x2_norm = ev("x2_norm")
        x2_T = ev("x2_T")
        x2_out = ev("x2_out")
        logits = ev("logits")
        onehot = ev("onehot", 7)
        lg_exp = ev("lg_exp")
        prob = ev("prob", 3)
        ranks = ev("ranks")
        slots = ev("slots", 5)
        id_put = ev("id_put", 2)
        idx_put = ev("idx_put")
        scattered = [sem(f"scattered{i}") for i in range(2)]

        pads_i = sem("pads_i")
        pads_out = sem("pads_out")
        tiles = sem("tiles")
        r_in = [sem(f"r_in{i}") for i in range(4)]
        e_norm, e_T, e_hi, e_lo = ev("e_norm"), ev("e_T"), ev("e_hi"), ev("e_lo")
        e_h = ev("e_h", 2)
        e_gelu = ev("e_gelu", 2)
        e_hh = ev("e_hh", 2)
        e_hl = ev("e_hl", 2)
        e_y = ev("e_y")
        e_res = ev("e_res")
        e_out = [sem(f"e_out{i}") for i in range(4)]

        w1_pieces = W1.rearrange("e (k p) f -> (e k) p f", k=2)
        w2_pieces = W2.rearrange("e (c p) d -> p (e c) d", p=P)

        HEAD, TAIL, UN = 4, 3, 4
        TH = 2

        def apart(eng, mark):
            eng.sem_inc(mark, 1)

        def attend_steps(eng, step):
            def at(i):
                step(i, i.plus(-1), i.plus(-2), i.plus(-3))
            for i in range(HEAD):
                at(Turn(i))
            with eng.Fori(HEAD // UN, B // UN) as r:
                for u in range(UN):
                    at(Turn(u, r, UN))
            for i in range(B, B + TAIL):
                at(Turn(i))

        def expert_steps(eng, step):
            def at(i):
                step(i, i.plus(-1), i.plus(-2))
            for i in range(4):
                at(Turn(i))
            with eng.Fori(1, NT // 4) as r:
                for u in range(4):
                    at(Turn(u, r, 4))
            for i in range(NT // 4 * 4, NT + 2):
                at(Turn(i))

        block = ctx.enter_context(nc.Block())

        @block.sync
        def _(sp):
            sp.dma_start(con[:], consts).then_inc(con_in, 16)
            for h in range(2):
                for i in range(IH):
                    sp.dma_start(xi[h][i * G:(i + 1) * G, :, :],
                                 x[h * IH + i].rearrange("c (n r) w -> n c (r w)", n=G)).then_inc(image_in[h], 16)
            sp.dma_start(wqkv[:], w_qkv.rearrange("(k p) n -> p k n", k=2)[:, :, 0:2 * D]).then_inc(attn_w_in, 16)
            sp.wait_ge(pool_zeroed, 1)
            for j in range(HJ):
                sp.dma_start(wo[32 * j:32 * j + DH, :, :],
                             w_out.rearrange("(g j r) d -> j r g d", g=HG, j=HJ)[j]).then_inc(attn_w_in, 16)
            sp.dma_start(ws[:], Ws.rearrange("(k p) e -> p k e", k=2)).then_inc(route_w_in, 16)
            for t in range(2):
                sp.dma_start(bs_all[:, t, :], spread(bs.rearrange("(a e) -> a e", a=1), 0, P)).then_inc(route_w_in, 16)
            sp.dma_start(b1r[:], b1.rearrange("e (c p) -> (e c) p", p=P)).then_inc(route_w_in, 16)
            sp.dma_start(b2r[:], b2.rearrange("(a e) d -> a (e d)", a=1)).then_inc(route_w_in, 16)
            sp.wait_ge(dve_setup, 7)
            sp.dma_start(himg[:, 0, :], clsr[:]).then_inc(himg_out, 16)
            for h in range(2):
                sp.wait_ge(img_ready, h + 1)
                for i in range(IH):
                    sp.dma_start(himg[h * IH + i, 1:NIMG, :].rearrange("(n w) d -> n (w d)", n=G),
                                 img[h][i * G:(i + 1) * G, :, :].rearrange("p w d -> p (w d)")).then_inc(himg_out, 16)
            sp.wait_ge(himg_out, 16 * (1 + B))
            sp.dma_start(X[0][0:NIMG, 1, :], himg[0]).then_inc(xi_in[0], 16)

            def step(l, f, a, p):
                if l.exists(B) and l.slot(2) == 0:
                    w_split.wait(sp, Turn(l.c // 2 - 1, l.r, l.n // 2))
                    sp.dma_start(wstage1[:], w1_pieces[l.of(2)]).then_inc(w1_in.sem, 16)
                    piece = l.of(2)
                    sp.dma_start(wstage2[:].rearrange("p (c d) -> p c d", d=D),
                                 w2_pieces[:, bass.ds(piece * 3, 3), :]).then_inc(w2_in.sem, 16)
                if l.exists(B) and not (l.r is None and l.c == 0):
                    h_sum.wait(sp, l.plus(-4))
                    src = l.c if l.r is None else l.lin(1)
                    sp.dma_start(X[l.slot(4)][0:NIMG, 1, :], himg[src]).then_inc(xi_in[l.slot(4)], 16)

            attend_steps(sp, step)

            def estep(t, h, y):
                if t.exists(NT):
                    if t.r is None and t.c == 0:
                        for i in range(2):
                            sp.wait_ge(scattered[i], 32 * (B // 2))
                        sp.wait_ge(pads_out, 16 * (E + 1))
                        sp.wait_ge(tiles, 1)
                    e_res.wait(sp, t.plus(-4))
                    if t.plus(-4).exists(NT):
                        sp.wait_ge(e_out[t.slot(4)], t.plus(-4).of(4) * 16 + 16)
                    row = sp.value_load(tl[0:1, 0, bass.ds(t.lin(1), 1)] if t.r is not None
                                        else tl[0:1, 0, t.c:t.c + 1], min_val=0, max_val=E * CAP)
                    sp.dma_start(R[t.slot(4)][:], routed[bass.ds(row, P), :]).then_inc(r_in[t.slot(4)], 16)

            expert_steps(sp, estep)

        @block.gpsimd
        def _(pool):
            pool.memset(wo[:], 0.0).then_inc(pool_zeroed, 1)
            pool.memset(halfs[:], -0.5)
            pool.memset(one16[:], 1.0)
            pool.memset(ones[:], 1.0)
            for i in range(4):
                pool.memset(X[i][:, 1, :], 0.0)
            for i in range(2):
                for t in (k1[i], k2[i], q1[i], hrow[i], V[i]):
                    pool.memset(t[:], 0.0)
            pool.memset(mxa[:], 0.0)
            pool.memset(mxb[:], 0.0)
            pool.memset(xT2[:], 0.0)
            pool.memset(padrow[:], 0.0)
            pool.memset(cfg2[:], 0.0).then_inc(pool_zeroed, 1)
            pool.wait_ge(pool_zeroed, 2)
            pool.wait_ge(con_in, 16)
            for i in range(2):
                pool.memset(V[i][:, 0, :, DH:DH + 1], 1.0)
                for h in range(H):
                    g = h // HJ
                    pool.tensor_copy(V[i][:, 1, h, DH:DH + 1], con[:, K_HALF + g % 2:K_HALF + g % 2 + 1])
            pool.wait_ge(con_in, 16)
            pool.tensor_copy(padrow[:, C_ID:C_ID + 1].bitcast(I32), con[:, K_PADID:K_PADID + 1])
            pool.tensor_copy(count[:], con[:, K_BASE:K_BASE + E])
            pool.tensor_copy(ids[:], con[:, K_IDS:K_IDS + 2]).then_inc(pool_setup, 1)
            for h in range(2):
                pool.wait_ge(patch_stats, h + 1)
                v = slice(h * G, (h + 1) * G)
                pool.tensor_scalar(vari[:, v], mvi[:, v, 1], EPS, None, ALU.add).then_inc(pool_patch, 1)
                pool.wait_ge(pool_patch, 4 * h + 1)
                pool.tensor_tensor(rstdi[:, v], vari[:, v], halfs[0:PR, 0:G], ALU.pow).then_inc(pool_patch, 1)
                pool.wait_ge(y_stats, h + 1)
                pool.tensor_scalar(vary[:], mvy[:, :, 1], EPS, None, ALU.add).then_inc(pool_patch, 1)
                pool.wait_ge(pool_patch, 4 * h + 3)
                pool.tensor_tensor(rstdy[:], vary[:], halfs[0:PR, 0:G], ALU.pow).then_inc(pool_patch, 1)
            pool.wait_ge(atoms_out, 16)
            pool.wait_ge(dve_setup, 13)
            pool.indirect_dma_start(X[0][:, 0, :], None, atoms,
                                    bass.IndirectOffsetOnAxis(txt_i[:, 0:1], 0)).then_inc(xt_in[0], 16)

            def step(l, f, a, p):
                n = l.plus(1)
                if n.r is not None or n.c < B:
                    h_sum.wait(pool, p)
                    if n.c >= 2 or n.r is not None:
                        o = n.plus(-2)
                        if o.r is not None or o.c >= 0:
                            pool.wait_ge(xt_in[o.slot(4)], o.of(4) * 16 + 16)
                    idx = txt_i[:, n.c:n.c + 1] if n.r is None else txt_i[:, bass.ds(n.lin(1), 1)]
                    apart(pool, pool_apart)
                    pool.tensor_copy(txt_now[n.slot(2)][:], idx).then_inc(idx_put.sem, 1)
                    idx_put.wait(pool, n.plus(-1))
                    apart(pool, pool_apart)
                    pool.indirect_dma_start(X[n.slot(4)][:, 0, :], None, atoms,
                                            bass.IndirectOffsetOnAxis(txt_now[n.slot(2)][:], 0)).then_inc(xt_in[n.slot(4)], 16)
                if f.exists(B):
                    s = f.slot(2)
                    k_hi.wait(pool, f)
                    apart(pool, pool_apart)
                    pool.tensor_scalar(k2[s][:, :, 0:S], kh[:], con[:, K_K2M:K_K2M + 1], con[:, K_K2A:K_K2A + 1],
                                       ALU.mult, ALU.add).then_inc(k_st2.sem, 1)
                if p.exists(B):
                    s = p.slot(2)
                    ln2_stats.wait(pool, p)
                    apart(pool, pool_apart)
                    pool.tensor_scalar(var2[:], mv2[:, :, 1], EPS, None, ALU.add).then_inc(ln2_rstd.sem, 1)
                    ln2_rstd.wait(pool, p, 1)
                    pool.tensor_tensor(hrow[s][:, :, C_RSTD], var2[:], halfs[:, 0:2], ALU.pow).then_inc(ln2_rstd.sem, 1)
                    pool.tensor_copy(hrow[s][:, :, C_MEAN], mv2[:, :, 0]).then_inc(ln2_rstd.sem, 1)
                if l.exists(B):
                    ln_stats.wait(pool, l)
                    apart(pool, pool_apart)
                    pool.tensor_scalar(var1[:], mv1[:, :, 1], EPS, None, ALU.add).then_inc(ln_rstd.sem, 1)
                    ln_rstd.wait(pool, l, 1)
                    pool.tensor_tensor(rstd1[:], var1[:], halfs[:, 0:2], ALU.pow).then_inc(ln_rstd.sem, 1)
                if l.r is None and l.c == 0:
                    pool.wait_ge(himg_out, 16 * (1 + B))
                    pool.wait_ge(w_ready, 12)
                if l.exists(B) and l.slot(2) == 0:
                    w = Turn(l.c // 2, l.r, l.n // 2)
                    if l.r is None:
                        d1, d2 = slice(w.c * F, w.c * F + F), slice(w.c * 3 * D, (w.c + 1) * 3 * D)
                    else:
                        d1, d2 = bass.ds(l.of(2) * F, F), bass.ds(l.of(2) * (3 * D), 3 * D)
                    w1_in.wait(pool, w)
                    apart(pool, pool_apart)
                    pool.tensor_scalar(wstage1[:], wstage1[:], W_SCALE, None, ALU.mult).then_inc(w_split.sem, 1)
                    w2_in.wait(pool, w)
                    apart(pool, pool_apart)
                    pool.tensor_scalar(wstage2[:], wstage2[:], W_SCALE, None, ALU.mult).then_inc(w_split.sem, 1)
                    w_split.wait(pool, w, 2)
                    apart(pool, pool_apart)
                    pool.tensor_copy(w1_hi[:, d1], wstage1[:]).then_inc(w_split.sem, 1)
                    pool.tensor_copy(w2_hi[:, d2], wstage2[:]).then_inc(w_split.sem, 1)
                    w_split.wait(pool, w, 4)
                    pool.tensor_tensor(w1_lo[:, d1], wstage1[:], w1_hi[:, d1], ALU.subtract).then_inc(w_split.sem, 1)
                    pool.tensor_tensor(w2_lo[:, d2], wstage2[:], w2_hi[:, d2], ALU.subtract).then_inc(w_split.sem, 1)
                if p.exists(B):
                    s = p.slot(2)
                    id_put.wait(pool, p.plus(-1))
                    apart(pool, pool_apart)
                    pool.tensor_copy(hrow[s][:, :, C_ID].bitcast(I32), ids[:]).then_inc(id_put.sem, 1)
                    pool.tensor_scalar(ids[:], ids[:], float(S), None, ALU.add).then_inc(id_put.sem, 1)
                    id_put.wait(pool, p)
                    slots.wait(pool, p)
                    prob.wait(pool, p)
                    ln2_rstd.wait(pool, p)
                    apart(pool, pool_apart)
                    pool.indirect_dma_start(routed, bass.IndirectOffsetOnAxis(slot_i[s][:, 0:1], 0),
                                            hrow[s][:, 0, :], None).then_inc(scattered[s], 16)
                    pool.indirect_dma_start(routed, bass.IndirectOffsetOnAxis(slot_i[s][0:NIMG, 1:2], 0),
                                            hrow[s][0:NIMG, 1, :], None).then_inc(scattered[s], 16)

            attend_steps(pool, step)
            pool.wait_ge(pads_i, 2)
            for e in range(E):
                pool.indirect_dma_start(routed, bass.IndirectOffsetOnAxis(pad_i[:, e:e + 1], 0),
                                        padrow[:], None).then_inc(pads_out, 16)
            pool.dma_start(routed[E * CAP:E * CAP + P, :], padrow[:]).then_inc(pads_out, 16)

            def estep(t, h, y):
                if y.exists(NT):
                    e_res.wait(pool, y)
                    s = y.slot(4)
                    apart(pool, pool_apart)
                    pool.indirect_dma_start(out, bass.IndirectOffsetOnAxis(R[s][:, C_ID:C_ID + 1].bitcast(I32), 0),
                                            res[s][:], None, bounds_check=T - 1, oob_is_err=False).then_inc(e_out[s], 16)

            expert_steps(pool, estep)
            pool.wait_ge(xt_in[0], 16 * (B // 4 + 1))
            for s in range(4):
                pool.wait_ge(e_out[s], 16 * ((NT - s + 3) // 4))

        @block.scalar
        def _(act):
            act.dma_start(wl[:], W_lin.rearrange("(f p c) d -> p f c d", f=2, c=C)).then_inc(patch_w_in, 16)
            act.dma_start(g1[:], ln1_g.rearrange("(f p c) -> p f c", f=2, c=C)).then_inc(patch_w_in, 16)
            act.dma_start(b1v[:], ln1_b.rearrange("(f p c) -> p f c", f=2, c=C)).then_inc(patch_w_in, 16)
            for t, src in ((bl_all, b_lin), (g2_all, ln2_g), (b2_all, ln2_b)):
                act.dma_start(t[:], spread(src.rearrange("(a d) -> a d", a=1), 0, P)).then_inc(patch_w_in, 16)
            for i in range(IH):
                act.dma_start(posr[i * G:(i + 1) * G, :],
                              pos[0, 1:NIMG, :].rearrange("(n w) d -> n (w d)", n=G)).then_inc(patch_w_in, 16)
            act.dma_start(clsr[:], spread(cls_tok[0], 0, B)).then_inc(patch_w_in, 16)
            act.dma_start(posc[:], spread(pos[0, 0:1, :], 0, B)).then_inc(patch_w_in, 16)
            act.dma_start(cfg_s[:], cfg).then_inc(atom_in, 16)
            act.dma_start(emb[:, 0, :], sub_e).then_inc(atom_in, 16)
            act.dma_start(emb[:, 1, :], occ_e).then_inc(atom_in, 16)
            act.dma_start(txt[:], x_txt).then_inc(atom_in, 16)
            act.wait_ge(dve_setup, 6)
            act.wait_ge(dve_setup, 12)
            act.dma_start(atoms, tab[:]).then_inc(atoms_out, 16)
            for i in range(2 * G):
                act.wait_ge(pe_patchT, i + 1)
                if i >= 2:
                    act.wait_ge(pe_patchY, i - 1)
                for c in range(2):
                    last = act.activation(xTi[i % 2][:, 3 * c:3 * c + 3, :],
                                          bank[2 * (i % 2) + c][:, 0:3 * PR].rearrange("p (c n) -> p c n", c=3),
                                          ACT.Copy)
                last.then_inc(act_patchT, 1)

            def k_q_hi(f):
                s = f.slot(2)
                k_proj.wait(act, f)
                k_st1.wait(act, f.plus(-1))
                k_st2.wait(act, f.plus(-1))
                act.activation(kh[:].rearrange("p g n -> p (g n)"), bank[2][:, 0:HG * S], ACT.Copy).then_inc(k_hi.sem, 1)
                q_proj.wait(act, f)
                pv.wait(act, f.plus(-2))
                act.activation(q1[s][:, :, 0:S], bank[3][:, 0:HG * S].rearrange("p (g n) -> p g n", g=HG),
                               ACT.Copy).then_inc(q_hi.sem, 1)

            def exps(a, j):
                s = j % 2
                sc_a.wait(act, a, j + 1)
                if j >= 2:
                    pv.wait(act, a, j - 1)
                else:
                    pv.wait(act, a.plus(-1), j + 3)
                act.activation(pa[s][:], bank[4][:, 0:HG * S], ACT.Exp,
                               scale=float(D) ** -0.5 / QK_SCALE ** 2).then_inc(exp_a.sem, 1)
                sc_b.wait(act, a, j + 1)
                act.activation(pb[s][:], bank[5][:, 0:2 * S], ACT.Exp,
                               scale=float(D) ** -0.5 / QK_SCALE ** 2).then_inc(exp_b.sem, 1)

            def step(l, f, a, p):
                if f.exists(B):
                    k_q_hi(f)
                if a.exists(B):
                    exps(a, 0)
                    exps(a, 1)
                if f.exists(B):
                    v_proj.wait(act, f)
                    pv.wait(act, f.plus(-2))
                    pv_out = bank[2][:, 0:2 * D].rearrange("p (t h d) -> p t h d", t=2, h=H)
                    vs = V[f.slot(2)]
                    act.activation(vs[:, 0, :, 0:DH], pv_out[:, 0], ACT.Copy, scale=1.0 / QK_SCALE)
                    act.activation(vs[64:P, 1, HJ:2 * HJ, 0:DH], pv_out[64:P, 1, HJ:2 * HJ], ACT.Copy, scale=1.0 / QK_SCALE)
                    act.activation(vs[0:64, 1].rearrange("p (g j) d -> p g j d", j=HJ)[:, 0:HG:2, :, 0:DH],
                                   pv_out[0:64, 1].rearrange("p (g j) d -> p g j d", j=HJ)[:, 0:HG:2], ACT.Copy,
                                   scale=1.0 / QK_SCALE).then_inc(v_out.sem, 1)
                if p.exists(B):
                    x2_T.wait(act, p)
                    logits.wait(act, p.plus(-1))
                    act.activation(xT2[:, :, 0:SP], bank[1][0:DK, 0:2 * SP].rearrange("p (k n) -> p k n", k=2),
                                   ACT.Copy).then_inc(x2_out.sem, 1)
                if a.exists(B):
                    exps(a, 2)
                if l.exists(B):
                    x_T.wait(act, l)
                    v_proj.wait(act, l.plus(-2))
                    act.activation(xh[l.slot(2)][:], bank[0][0:DK, 0:2 * SP].rearrange("p (k n) -> p k n", k=2),
                                   ACT.Copy).then_inc(x_hi.sem, 1)
                if a.exists(B):
                    exps(a, 3)
                if p.exists(B):
                    onehot.wait(act, p, 3)
                    prob.wait(act, p.plus(-1), 1)
                    act.activation(lge[:], lgd[:], ACT.Exp).then_inc(lg_exp.sem, 1)

            attend_steps(act, step)

            def estep(t, h, y):
                if t.exists(NT):
                    e_T.wait(act, t)
                    e_h.wait(act, t.plus(-2))
                    act.activation(xeh[t.slot(2)][:], bank[0][0:DK, 0:2 * P].rearrange("p (k n) -> p k n", k=2),
                                   ACT.Copy).then_inc(e_hi.sem, 1)
                if h.exists(NT):
                    s = h.slot(2)
                    ex = act.value_load(tl[0:1, 1, bass.ds(h.lin(1), 1)] if h.r is not None
                                        else tl[0:1, 1, h.c:h.c + 1], min_val=0, max_val=E - 1)
                    if h.exists(NT):
                        e_hl.wait(act, h.plus(-2))
                    for c in range(2):
                        e_h.wait(act, h, c + 1)
                        for m in range(3):
                            fc = 3 * c + m
                            last = act.activation(hf[s][:, fc, :], bank[2 + 2 * s + c][:, m * P:(m + 1) * P], ACT.Gelu,
                                                  bias=b1T[:, bass.ds(ex * FC + fc, 1)], scale=1.0 / W_SCALE)
                        last.then_inc(e_gelu.sem, 1)

            act.wait_ge(tiles, 1)
            expert_steps(act, estep)

        @block.vector
        def _(dve):
            dve.wait_ge(con_in, 16)
            dve.tensor_scalar(neg_id[:], ident, -1.0 / MAX_SCALE, None, ALU.mult).then_inc(dve_setup, 1)
            dve.tensor_copy(tri[:], con[:, K_TRI:K_TRI + P]).then_inc(dve_setup, 1)
            dve.wait_ge(atom_in, 64)
            dve.wait_ge(pool_zeroed, 2)
            dve.tensor_scalar(cfg2[:, 0, 0:NCFG], cfg_s[:], 0.0, None, ALU.not_equal).then_inc(dve_setup, 1)
            dve.tensor_scalar(cfg2[:, 1, 0:NCFG], cfg_s[:], -1.0, 0.0, ALU.add, ALU.max).then_inc(dve_setup, 1)
            dve.wait_ge(patch_w_in, 16 * (8 + IH))
            for f2 in range(2):
                for c in range(C):
                    last = dve.tensor_scalar(wlg[:, f2, c, :], wl[:, f2, c, :], g1[:, f2, c:c + 1], None, ALU.mult)
            last.then_inc(dve_setup, 1)
            dve.tensor_tensor(posr[:].rearrange("p (w d) -> p w d", d=D), posr[:].rearrange("p (w d) -> p w d", d=D),
                              spread(b2_all[0:PR, :].unsqueeze(1), 1, G), ALU.add).then_inc(dve_setup, 1)
            dve.tensor_tensor(clsr[:], clsr[:], posc[:], ALU.add).then_inc(dve_setup, 1)
            dve.tensor_scalar(txt_neg[:], txt[:], 0.0, float(NAT), ALU.is_lt, ALU.mult)
            dve.tensor_copy(txt_f[:], txt[:]).then_inc(dve_setup, 1)
            dve.wait_ge(dve_setup, 8)
            dve.tensor_tensor(txt_f[:], txt_f[:], txt_neg[:], ALU.add).then_inc(dve_patch, 1)
            dve.wait_ge(dve_patch, 1)
            dve.tensor_scalar(txt_f[:], txt_f[:], 0.0, float(NAT - 1), ALU.max, ALU.min).then_inc(dve_setup, 1)
            dve.wait_ge(pe_setup, 1)
            dve.tensor_tensor(bias_all[:], bank[7][:, 0:D], bl_all[:], ALU.add).then_inc(dve_setup, 1)
            dve.wait_ge(pe_setup, 2)
            dve.tensor_copy(cfgT[:], bank[6][0:32, 0:2 * NAT].rearrange("p (t n) -> p t n", t=2)).then_inc(dve_setup, 1)
            dve.wait_ge(pe_setup, 3)
            dve.tensor_copy(tab[:], bank[7][0:NAT, 0:D]).then_inc(dve_setup, 1)
            dve.memset(txt_i[:, B:B + 1], 0)
            dve.tensor_copy(txt_i[:, 0:B], bank[6][:, 256:256 + B]).then_inc(dve_setup, 1)
            for h in range(2):
                dve.wait_ge(image_in[h], 16 * IH)
                for w in range(G):
                    for c in range(C):
                        last = dve.bn_stats(sti[:, h * G + w, c, :],
                                            xi[h][:, c, :].rearrange("p (r w) -> p r w", r=PATCH)[:, :, w * PATCH:(w + 1) * PATCH])
                last.then_inc(dve_patch, 1)
                dve.wait_ge(dve_patch, 1 + 2 * h + 1)
                for w in range(G):
                    last = dve.bn_aggr(mvi[:, h * G + w, :], sti[:, h * G + w, :, :])
                last.then_inc(patch_stats, 1)
                dve.wait_ge(pool_patch, 4 * h + 2)
                dve.wait_ge(patch_stats, h + 1)

                def y_out(i):
                    dve.wait_ge(pe_patchY, i + 1)
                    dve.tensor_tensor(yi[:, i % G, :], bank[4 + i % 2][0:PR, 0:D], bias_all[0:PR, :],
                                      ALU.add).then_inc(patch_y, 1)

                if h == 0:
                    dve.wait_ge(dve_setup, 10)
                for w in range(G):
                    i = h * G + w
                    if i >= 2:
                        dve.wait_ge(pe_patchT, i - 1)
                    dve.tensor_scalar(xni[i % 2][:].rearrange("p c (r q) -> p c r q", q=PATCH),
                                      xi[h][:].rearrange("p c (r w) -> p c r w", r=PATCH)[:, :, :, w * PATCH:(w + 1) * PATCH]
                                      .rearrange("p c (f r) q -> p (c f) r q", f=2),
                                      mvi[:, i, 0:1], rstdi[:, i:i + 1], ALU.subtract, ALU.mult).then_inc(patch_norm, 1)
                    if w >= 1:
                        y_out(i - 1)
                y_out(h * G + G - 1)
                dve.wait_ge(patch_y, G * (h + 1))
                for w in range(G):
                    last = dve.bn_stats(sty[:, w, :], yi[:, w, :])
                last.then_inc(dve_patch, 1)
                dve.wait_ge(dve_patch, 1 + 2 * h + 2)
                for w in range(G):
                    last = dve.bn_aggr(mvy[:, w, :], sty[:, w, :])
                last.then_inc(y_stats, 1)
                dve.wait_ge(pool_patch, 4 * h + 4)
                dve.wait_ge(y_stats, h + 1)
                for w in range(G):
                    last = dve.tensor_scalar(img[h][:, w, :], yi[:, w, :], mvy[:, w, 0:1], rstdy[:, w:w + 1],
                                             ALU.subtract, ALU.mult)
                last.then_inc(img_step, 1)
                dve.wait_ge(img_step, 2 * h + 1)
                dve.tensor_tensor(img[h][:], img[h][:], spread(g2_all[0:PR, :].unsqueeze(1), 1, G),
                                  ALU.mult).then_inc(img_step, 1)
                dve.wait_ge(img_step, 2 * h + 2)
                dve.tensor_tensor(img[h][:], img[h][:], posr[:].rearrange("p (w d) -> p w d", d=D),
                                  ALU.add).then_inc(img_ready, 1)
            dve.wait_ge(attn_w_in, 16 * (1 + HJ))
            for k in range(2):
                for t in range(2):
                    dve.tensor_scalar(wdup[:, k, :, t, :], wqkv[:, k, :].rearrange("p (h d) -> p h d", d=DH),
                                      QK_SCALE, None, ALU.mult).then_inc(w_ready, 1)
            dve.wait_ge(w_ready, 4)
            wflat = wdup[:].rearrange("p k (q n) t d -> p k q (n t d)", q=2)
            for k in range(2):
                dve.tensor_copy(wqk_hi[:, k], wflat[:, k]).then_inc(w_ready, 1)
            dve.wait_ge(w_ready, 6)
            for k in range(2):
                dve.tensor_tensor(wqk_lo[:, k], wflat[:, k], wqk_hi[:, k], ALU.subtract).then_inc(w_ready, 1)
            dve.wait_ge(route_w_in, 80)
            dve.wait_ge(pe_setup, 4)
            dve.tensor_copy(b1T[:], bank[6][:, 0:E * FC]).then_inc(w_ready, 1)
            dve.tensor_scalar(b2r[:], b2r[:], W_SCALE, None, ALU.mult).then_inc(w_ready, 1)
            dve.wait_ge(w_ready, 10)
            dve.tensor_copy(b2_hi[:], b2r[:]).then_inc(w_ready, 1)
            dve.wait_ge(w_ready, 11)
            dve.tensor_tensor(b2_lo[:], b2r[:], b2_hi[:], ALU.subtract).then_inc(w_ready, 1)
            dve.wait_ge(pool_setup, 1)

            def take_max(f, m):
                j, images = m // 2, m % 2
                if m == 0:
                    max_rows.wait(dve, f.plus(-1))
                max_scores.wait(dve, f, m + 1)
                if images:
                    dve.tensor_reduce(mxb[:, :, 32 * j + DH], bank[7][:, 0:2 * S].rearrange("p (g n) -> p g n", g=2),
                                      AX.X, ALU.max).then_inc(max_taken.sem, 1)
                else:
                    dve.tensor_reduce(mxa[:, :, 32 * j + DH], bank[7][:, 0:HG * S].rearrange("p (g n) -> p g n", g=HG),
                                      AX.X, ALU.max).then_inc(max_taken.sem, 1)

            def step(l, f, a, p):
                if f.exists(B):
                    s = f.slot(2)
                    k_hi.wait(dve, f)
                    pv.wait(dve, f.plus(-2))
                    dve.scalar_tensor_tensor(out=k1[s][:, :, 0:S], in0=kh[:], scalar=con[:, K_KLO:K_KLO + 1],
                                             in1=bank[2][:, 0:HG * S].rearrange("p (g n) -> p g n", g=HG),
                                             op0=ALU.mult, op1=ALU.add).then_inc(k_st1.sem, 1)
                    q_hi.wait(dve, f)
                    dve.tensor_tensor(qlo[:], bank[3][:, 0:HG * S].rearrange("p (g n) -> p g n", g=HG),
                                      q1[s][:, :, 0:S], ALU.subtract).then_inc(q_rest.sem, 1)
                if p.exists(B):
                    s = p.slot(2)
                    o_proj.wait(dve, p)
                    if p.plus(-2).exists(B):
                        dve.wait_ge(scattered[s], p.plus(-2).of(2) * 32 + 32)
                    dve.tensor_tensor(hrow[s][:, 0, 0:D], bank[1][:, 0:D], X[p.slot(4)][:, 0, :],
                                      ALU.add).then_inc(h_sum.sem, 1)
                    dve.tensor_tensor(hrow[s][0:NIMG, 1, 0:D], bank[1][0:NIMG, D:2 * D], X[p.slot(4)][0:NIMG, 1, :],
                                      ALU.add).then_inc(h_sum.sem, 1)
                    h_sum.wait(dve, p)
                    for t in range(2):
                        dve.bn_stats(st2[:, t, :], hrow[s][:, t, 0:D]).then_inc(ln2_stats.sem, 1)
                    ln2_stats.wait(dve, p, 2)
                    ln2_rstd.wait(dve, p.plus(-1))
                    for t in range(2):
                        apart(dve, dve_apart)
                        dve.bn_aggr(mv2[:, t, :], st2[:, t, :]).then_inc(ln2_stats.sem, 1)
                if l.exists(B):
                    n = l.slot(4)
                    dve.wait_ge(xi_in[n], l.of(4) * 16 + 16)
                    dve.wait_ge(xt_in[n], l.of(4) * 16 + 16)
                    for t in range(2):
                        dve.bn_stats(st1[:, t, :], X[n][:, t, :]).then_inc(ln_stats.sem, 1)
                    ln_stats.wait(dve, l, 2)
                    for t in range(2):
                        apart(dve, dve_apart)
                        dve.bn_aggr(mv1[:, t, :], st1[:, t, :]).then_inc(ln_stats.sem, 1)
                if f.exists(B):
                    take_max(f, 0)
                    take_max(f, 1)
                if p.exists(B):
                    s = p.slot(2)
                    ln2_rstd.wait(dve, p)
                    x2_T.wait(dve, p.plus(-1))
                    for t in range(2):
                        last = dve.tensor_scalar(xn2[:, t, :], hrow[s][:, t, 0:D], hrow[s][:, t, C_MEAN:C_MEAN + 1],
                                                 hrow[s][:, t, C_RSTD:C_RSTD + 1], ALU.subtract, ALU.mult)
                    last.then_inc(x2_norm.sem, 1)
                if l.exists(B):
                    ln_rstd.wait(dve, l)
                    ln_stats.wait(dve, l)
                    x_T.wait(dve, l.plus(-1))
                    for t in range(2):
                        last = dve.tensor_scalar(xn[:, t, :], X[l.slot(4)][:, t, :], mv1[:, t, 0:1], rstd1[:, t:t + 1],
                                                 ALU.subtract, ALU.mult)
                    last.then_inc(x_norm.sem, 1)
                if f.exists(B):
                    for m in range(2, 6):
                        take_max(f, m)
                if l.exists(B):
                    x_hi.wait(dve, l)
                    dve.tensor_tensor(xl[l.slot(2)][:], bank[0][0:DK, 0:2 * SP].rearrange("p (k n) -> p k n", k=2),
                                      xh[l.slot(2)][:], ALU.subtract).then_inc(x_lo.sem, 1)
                if p.exists(B):
                    logits.wait(dve, p)
                    dve.tensor_tensor(lg[:], bank[1][:, 0:2 * E].rearrange("p (t e) -> p t e", t=2), bs_all[:],
                                      ALU.add).then_inc(onehot.sem, 1)
                    onehot.wait(dve, p, 1)
                    dve.tensor_reduce(lgm[:], lg[:], AX.X, ALU.max).then_inc(onehot.sem, 1)
                    onehot.wait(dve, p, 2)
                    lg_exp.wait(dve, p.plus(-1))
                    dve.tensor_tensor(lgd[:], lg[:], spread(lgm[:].unsqueeze(2), 2, E), ALU.subtract).then_inc(onehot.sem, 1)
                    onehot.wait(dve, p, 3)
                    dve.scalar_tensor_tensor(out=first[:], in0=lgd[:], scalar=0.0,
                                             in1=con[:, K_FIRST:K_FIRST + 2 * E].rearrange("p (t e) -> p t e", t=2),
                                             op0=ALU.is_equal, op1=ALU.mult).then_inc(onehot.sem, 1)
                    onehot.wait(dve, p, 4)
                    dve.tensor_reduce(firstm[:], first[:], AX.X, ALU.max).then_inc(onehot.sem, 1)
                    onehot.wait(dve, p, 5)
                    dve.tensor_tensor(oh[:], first[:], spread(firstm[:].unsqueeze(2), 2, E), ALU.is_equal).then_inc(onehot.sem, 1)
                    onehot.wait(dve, p, 6)
                    dve.tensor_tensor(ohb[:], oh[:], spread(con[:, K_VALID:K_VALID + 2].unsqueeze(2), 2, E),
                                      ALU.mult).then_inc(onehot.sem, 1)
                if f.exists(B):
                    take_max(f, 6)
                    take_max(f, 7)
                if a.exists(B):
                    pv.wait(dve, a)
                    apart(dve, dve_apart)
                    dve.stream_shuffle(den[:], bank[6][:, 0:HG * S], [DH] * 32).then_inc(o_norm.sem, 1)
                    o_norm.wait(dve, a, 1)
                    dve.reciprocal(den[:], den[:]).then_inc(o_norm.sem, 1)
                    o_norm.wait(dve, a, 2)
                    o_proj.wait(dve, a.plus(-1))
                    dve.tensor_tensor(ot[:].rearrange("p g n -> p (g n)"), bank[6][:, 0:HG * S], den[:],
                                      ALU.mult).then_inc(o_norm.sem, 1)
                if f.exists(B):
                    max_rows.wait(dve, f)
                    q_rest.wait(dve, f)
                    pv.wait(dve, f.plus(-2))
                    dve.scalar_tensor_tensor(out=q2[f.slot(2)][:], in0=qlo[:], scalar=con[:, K_K2M:K_K2M + 1],
                                             in1=bank[3][:, 0:HG * S].rearrange("p (g n) -> p g n", g=HG),
                                             op0=ALU.mult, op1=ALU.add).then_inc(q_st2.sem, 1)
                if p.exists(B):
                    s = p.slot(2)
                    lg_exp.wait(dve, p)
                    dve.tensor_reduce(esum[:], lge[:], AX.X, ALU.add).then_inc(prob.sem, 1)
                    prob.wait(dve, p, 1)
                    dve.tensor_scalar(esum[:], esum[:], W_SCALE, None, ALU.mult).then_inc(prob.sem, 1)
                    prob.wait(dve, p, 2)
                    dve.reciprocal(hrow[s][:, :, C_PROB], esum[:]).then_inc(prob.sem, 1)
                    ranks.wait(dve, p)
                    slots.wait(dve, p.plus(-1))
                    rk = bank[1][:, 2 * E:5 * E].rearrange("p (t e) -> p t e", t=3)
                    dve.tensor_tensor(rank[:], rk[:, 0:2, :], spread(count[:].unsqueeze(1), 1, 2), ALU.add).then_inc(slots.sem, 1)
                    slots.wait(dve, p, 1)
                    dve.tensor_tensor(count[:], count[:], rk[:, 2, :], ALU.add).then_inc(slots.sem, 1)
                    dve.tensor_tensor(rank[:], rank[:], ohb[:], ALU.mult).then_inc(slots.sem, 1)
                    slots.wait(dve, p, 3)
                    dve.tensor_reduce(slotf[:], rank[:], AX.X, ALU.add).then_inc(slots.sem, 1)
                    slots.wait(dve, p, 4)
                    dve.tensor_copy(slot_i[s][:], slotf[:]).then_inc(slots.sem, 1)

            attend_steps(dve, step)

            last_b = Turn(B - 1)
            slots.wait(dve, last_b)
            dve.tensor_scalar(pad_f[:], count[:], con[:, K_PART:K_PART + 1], None, ALU.add).then_inc(pads_i, 1)
            dve.wait_ge(pads_i, 1)
            dve.tensor_copy(pad_i[:], pad_f[:]).then_inc(pads_i, 1)
            chain = [0]

            def link(ins):
                chain[0] += 1
                ins.then_inc(list_step, 1)
                dve.wait_ge(list_step, chain[0])

            link(dve.tensor_tensor(cnt_f[:], count[0:1, :], con[0:1, K_BASE:K_BASE + E], ALU.subtract))
            link(dve.tensor_scalar(cnt_i[:], cnt_f[:], float(P - 1), None, ALU.add))
            link(dve.tensor_scalar(cnt_i[:], cnt_i[:], P.bit_length() - 1, None, ALU.logical_shift_right))
            link(dve.tensor_copy(ntile[:], cnt_i[:]))
            link(dve.tensor_scalar(skip[:], ntile[:], -float(P), float(CAP), ALU.mult, ALU.add))
            link(dve.tensor_copy(cum[:], ntile[:]))
            for e in range(1, E):
                link(dve.tensor_tensor(cum[:, e:e + 1], cum[:, e:e + 1], cum[:, e - 1:e], ALU.add))
            link(dve.memset(tl_f[:, 1, :], 0.0))
            link(dve.tensor_scalar(tl_f[:, 0, :], con[0:1, K_TILE:K_TILE + NT], float(P), None, ALU.mult))
            for e in range(E):
                link(dve.tensor_scalar(reached[:], con[0:1, K_TILE:K_TILE + NT], cum[:, e:e + 1], None, ALU.is_ge))
                link(dve.tensor_tensor(tl_f[:, 1, :], tl_f[:, 1, :], reached[:], ALU.add))
                link(dve.scalar_tensor_tensor(out=tl_f[:, 0, :], in0=reached[:], scalar=skip[:, e:e + 1],
                                              in1=tl_f[:, 0, :], op0=ALU.mult, op1=ALU.add))
            link(dve.tensor_scalar(tl_f[:, 0, :], tl_f[:, 0, :], float(E * CAP), None, ALU.min))
            link(dve.tensor_scalar(tl_f[:, 1, :], tl_f[:, 1, :], float(E - 1), None, ALU.min))
            dve.tensor_copy(tl[:], tl_f[:]).then_inc(tiles, 1)

            def estep(t, h, y):
                if t.exists(NT):
                    s = t.slot(4)
                    dve.wait_ge(r_in[s], t.of(4) * 16 + 16)
                    e_T.wait(dve, t.plus(-1))
                    dve.tensor_scalar(xe[:], R[s][:, 0:D], R[s][:, C_MEAN:C_MEAN + 1], R[s][:, C_RSTD:C_RSTD + 1],
                                      ALU.subtract, ALU.mult).then_inc(e_norm.sem, 1)
                if y.exists(NT):
                    s = y.slot(4)
                    e_y.wait(dve, y)
                    if y.plus(-4).exists(NT):
                        dve.wait_ge(e_out[s], y.plus(-4).of(4) * 16 + 16)
                    dve.scalar_tensor_tensor(out=res[s][:], in0=bank[6 + y.slot(2)][:, 0:D],
                                             scalar=R[s][:, C_PROB:C_PROB + 1], in1=R[s][:, 0:D],
                                             op0=ALU.mult, op1=ALU.add).then_inc(e_res.sem, 1)
                if t.exists(NT):
                    e_hi.wait(dve, t)
                    dve.tensor_tensor(xel[t.slot(2)][:], bank[0][0:DK, 0:2 * P].rearrange("p (k n) -> p k n", k=2),
                                      xeh[t.slot(2)][:], ALU.subtract).then_inc(e_lo.sem, 1)
                if h.exists(NT):
                    s = h.slot(2)
                    for c in range(2):
                        e_gelu.wait(dve, h, c + 1)
                        e_y.wait(dve, h.plus(-2))
                        m = slice(3 * c, 3 * c + 3)
                        dve.tensor_copy(hh[s][:, m, :], hf[s][:, m, :]).then_inc(e_hh.sem, 1)
                        e_hh.wait(dve, h, c + 1)
                        dve.tensor_tensor(hl[s][:, m, :], hf[s][:, m, :], hh[s][:, m, :], ALU.subtract).then_inc(e_hl.sem, 1)

            expert_steps(dve, estep)

        @block.tensor
        def _(pe):
            pe.wait_ge(con_in, 16)
            pe.wait_ge(patch_w_in, 16 * (8 + IH))
            n = 0
            for f2 in range(2):
                for c in range(C):
                    last = pe.matmul(bank[7][:, 0:D], spread(b1v[:, f2, c:c + 1], 1, P), wl[:, f2, c, :],
                                     start=(n == 0), stop=(n == 2 * C - 1))
                    n += 1
            last.then_inc(pe_setup, 1)
            pe.wait_ge(dve_setup, 4)
            for t in range(2):
                last = pe.transpose(bank[6][0:32, t * NAT:(t + 1) * NAT], cfg2[:, t, :], ident[0:NAT, 0:NAT])
            last.then_inc(pe_setup, 1)
            pe.wait_ge(dve_setup, 11)
            pe.transpose(bank[6][:, 256:256 + B], txt_f[:], ident[0:B, 0:B])
            for t in range(2):
                last = pe.matmul(bank[7][0:NAT, 0:D], cfgT[0:NCFG, t, :], emb[:, t, :], start=(t == 0), stop=(t == 1))
            last.then_inc(pe_setup, 1)
            def patch_transpose(i):
                pe.wait_ge(patch_norm, i + 1)
                if i >= 2:
                    pe.wait_ge(act_patchT, i - 1)
                for c in range(2 * C):
                    last = pe.transpose(bank[2 * (i % 2) + c // 3][:, (c % 3) * PR:(c % 3 + 1) * PR], xni[i % 2][:, c, :],
                                        ident[0:PR, 0:PR])
                last.then_inc(pe_patchT, 1)

            def patch_embed(k):
                pe.wait_ge(act_patchT, k + 1)
                if k >= 2:
                    pe.wait_ge(patch_y, k - 1)
                for c in range(2 * C):
                    last = pe.matmul(bank[4 + k % 2][0:PR, 0:D], xTi[k % 2][:, c, :], wlg[:, c % 2, c // 2, :],
                                     start=(c == 0), stop=(c == 2 * C - 1))
                last.then_inc(pe_patchY, 1)

            pe.wait_ge(dve_setup, 5)
            for h in range(2):
                patch_transpose(h * G)
                for w in range(1, G):
                    patch_transpose(h * G + w)
                    patch_embed(h * G + w - 1)
                patch_embed(h * G + G - 1)
            pe.wait_ge(route_w_in, 80)
            pe.wait_ge(dve_setup, 13)
            pe.transpose(bank[6][:, 0:E * FC], b1r[:], ident[0:E * FC, 0:E * FC]).then_inc(pe_setup, 1)
            pe.wait_ge(w_ready, 12)
            pe.wait_ge(attn_w_in, 16 * (1 + HJ))

            def project(dst, which, f):
                s = f.slot(2)
                for g in range(HG):
                    cols = slice(g * P, (g + 1) * P)
                    n = 0
                    for k in range(2):
                        for w, v in ((wqk_hi, xh), (wqk_lo, xh), (wqk_hi, xl)):
                            last = pe.matmul(dst[:, g * S:(g + 1) * S], w[:, k, which, cols], v[s][:, k, 0:S],
                                             start=(n == 0), stop=(n == 5))
                            n += 1
                return last

            def project_values(f):
                s = f.slot(2)
                wv_hi = wqk_hi[:].rearrange("p k q (h t d) -> p k q h t d", h=H, t=2)
                wv_lo = wqk_lo[:].rearrange("p k q (h t d) -> p k q h t d", h=H, t=2)
                for c0, c1, r0, r1, h0, h1, o in ((0, TXT, 0, P, 0, H, 0), (TXT, SP, 0, 64, 0, H, D),
                                                  (TXT, SP, 64, P, HJ, 2 * HJ, D)):
                    n = 0
                    for k in range(2):
                        for w, v in ((wv_hi, xh), (wv_lo, xh), (wv_hi, xl)):
                            last = pe.matmul(bank[2][r0:r1, o + h0 * DH:o + h1 * DH].rearrange("p (h d) -> p h d", d=DH),
                                             v[s][:, k, c0:c1], w[:, k, 1, h0:h1, 0, :], start=(n == 0), stop=(n == 5))
                            n += 1
                return last

            quarters = ((0, 0, 0), (64, 0, 1), (0, 1, 2), (64, 1, 2))

            def max_part(f, m):
                j, images = m // 2, m % 2
                s, rows = f.slot(2), slice(32 * (m // 2), 32 * (m // 2) + 32)
                if m == 0:
                    max_taken.wait(pe, f.plus(-1))
                    k_st1.wait(pe, f)
                    q_hi.wait(pe, f)
                else:
                    max_taken.wait(pe, f, m)
                if images:
                    for r, c, g in quarters:
                        last = pe.matmul(bank[7][r:r + 64, c * S:(c + 1) * S], q1[s][rows, g, TXT:SP], k1[s][rows, g, 0:S],
                                         start=True, stop=True)
                else:
                    for g in range(HG):
                        last = pe.matmul(bank[7][:, g * S:(g + 1) * S], q1[s][rows, g, 0:TXT], k1[s][rows, g, 0:S],
                                         start=True, stop=True)
                last.then_inc(max_scores.sem, 1)

            def scores(a, j):
                s, rows = a.slot(2), slice(32 * j, 32 * j + 32)
                if j == 0:
                    q_st2.wait(pe, a)
                    k_st2.wait(pe, a)
                    exp_a.wait(pe, a.plus(-1))
                else:
                    exp_a.wait(pe, a, j)
                for g in range(HG):
                    for n, (kk, qq) in enumerate(((k1, q1), (k2, q2))):
                        last = pe.matmul(bank[4][:, g * S:(g + 1) * S], kk[s][rows, g, 0:TXT], qq[s][rows, g, 0:S],
                                         start=(n == 0), stop=(n == 1))
                last.then_inc(sc_a.sem, 1)
                if j == 0:
                    exp_b.wait(pe, a.plus(-1))
                else:
                    exp_b.wait(pe, a, j)
                for r, c, g in quarters:
                    for n, (kk, qq) in enumerate(((k1, q1), (k2, q2))):
                        last = pe.matmul(bank[5][r:r + 64, c * S:(c + 1) * S], kk[s][rows, g, TXT:SP], qq[s][rows, g, 0:S],
                                         start=(n == 0), stop=(n == 1))
                last.then_inc(sc_b.sem, 1)

            def weigh(a, j):
                s, t = a.slot(2), j % 2
                if j == 0:
                    v_out.wait(pe, a)
                    o_norm.wait(pe, a.plus(-1))
                exp_a.wait(pe, a, j + 1)
                exp_b.wait(pe, a, j + 1)
                for g in range(HG):
                    h = HJ * g + j
                    dst = bank[6][32 * j:32 * j + 32, g * S:(g + 1) * S]
                    c = quarters[g][1]
                    pe.matmul(dst, V[s][:, 0, h, :], pa[t][:, g * S:(g + 1) * S], start=True, stop=False)
                    last = pe.matmul(dst, V[s][:, 1, h, :], pb[t][:, c * S:(c + 1) * S], start=False, stop=True)
                last.then_inc(pv.sem, 1)

            def step(l, f, a, p):
                if f.exists(B):
                    x_lo.wait(pe, f)
                    v_out.wait(pe, f.plus(-1))
                    project(bank[2], 1, f).then_inc(k_proj.sem, 1)
                    q_st2.wait(pe, f.plus(-1))
                    project(bank[3], 0, f).then_inc(q_proj.sem, 1)
                if a.exists(B):
                    scores(a, 0)
                if p.exists(B):
                    o_norm.wait(pe, p)
                    slots.wait(pe, p.plus(-1))
                    for rows, c0, c1, o in ((P, 0, TXT, 0), (NIMG, TXT, S, D)):
                        for g in range(HG):
                            last = pe.matmul(bank[1][0:rows, o:o + D], ot[:, g, c0:c1], wo[:, g, :],
                                             start=(g == 0), stop=(g == HG - 1))
                    last.then_inc(o_proj.sem, 1)
                if a.exists(B):
                    weigh(a, 0)
                    scores(a, 1)
                if f.exists(B):
                    k_st1.wait(pe, f)
                    project_values(f).then_inc(v_proj.sem, 1)
                    max_part(f, 0)
                if a.exists(B):
                    weigh(a, 1)
                if f.exists(B):
                    max_part(f, 1)
                if p.exists(B):
                    x2_norm.wait(pe, p)
                    h_sum.wait(pe, p)
                    for k in range(2):
                        for t, (c0, c1) in enumerate(((0, TXT), (TXT, SP))):
                            last = pe.transpose(bank[1][0:DK, k * SP + c0:k * SP + c1], xn2[0:c1 - c0, t, k * DK:(k + 1) * DK],
                                                ident[0:c1 - c0, 0:c1 - c0])
                    last.then_inc(x2_T.sem, 1)
                if a.exists(B):
                    scores(a, 2)
                if l.exists(B):
                    x_norm.wait(pe, l)
                    x_lo.wait(pe, l.plus(-1))
                    for k in range(2):
                        for t, (c0, c1) in enumerate(((0, TXT), (TXT, SP))):
                            last = pe.transpose(bank[0][0:DK, k * SP + c0:k * SP + c1], xn[0:c1 - c0, t, k * DK:(k + 1) * DK],
                                                ident[0:c1 - c0, 0:c1 - c0])
                    last.then_inc(x_T.sem, 1)
                if f.exists(B):
                    max_part(f, 2)
                if a.exists(B):
                    weigh(a, 2)
                if f.exists(B):
                    max_part(f, 3)
                if a.exists(B):
                    scores(a, 3)
                if f.exists(B):
                    max_part(f, 4)
                    max_part(f, 5)
                if p.exists(B):
                    x2_out.wait(pe, p)
                    for t in range(2):
                        for k in range(2):
                            last = pe.matmul(bank[1][:, t * E:(t + 1) * E], xT2[:, k, t * P:(t + 1) * P], ws[:, k, :],
                                             start=(k == 0), stop=(k == 1))
                    last.then_inc(logits.sem, 1)
                if a.exists(B):
                    weigh(a, 3)
                if f.exists(B):
                    max_part(f, 6)
                    max_part(f, 7)
                if p.exists(B):
                    onehot.wait(pe, p)
                    o = 2 * E
                    pe.matmul(bank[1][:, o:o + E], tri[:], ohb[:, 0, :], start=True, stop=True)
                    pe.matmul(bank[1][:, o + E:o + 2 * E], tri[:], ohb[:, 1, :], start=True, stop=False)
                    pe.matmul(bank[1][:, o + E:o + 2 * E], ones[:], ohb[:, 0, :], start=False, stop=True)
                    pe.matmul(bank[1][:, o + 2 * E:o + 3 * E], ones[:], ohb[:, 0, :], start=True, stop=False)
                    pe.matmul(bank[1][:, o + 2 * E:o + 3 * E], ones[:], ohb[:, 1, :], start=False, stop=True)\
                        .then_inc(ranks.sem, 1)
                if f.exists(B):
                    max_taken.wait(pe, f)
                    q_rest.wait(pe, f)
                    for g in range(HG):
                        r, c, _ = quarters[g]
                        pe.matmul(bank[3][:, g * S:g * S + TXT], mxa[:, g, :], neg_id[:], start=True, stop=True)
                        last = pe.matmul(bank[3][:, g * S + TXT:(g + 1) * S], mxb[:, c, :], neg_id[:, r:r + NIMG],
                                         start=True, stop=True)
                    last.then_inc(max_rows.sem, 1)

            attend_steps(pe, step)
            w_split.wait(pe, Turn(B // 2 - 1))
            pe.wait_ge(tiles, 1)
            slots.wait(pe, Turn(B - 1))
            o_norm.wait(pe, Turn(B - 1))

            def expert_of(t):
                return pe.value_load(tl[0:1, 1, bass.ds(t.lin(1), 1)] if t.r is not None
                                     else tl[0:1, 1, t.c:t.c + 1], min_val=0, max_val=E - 1)

            def estep(t, h, y):
                if t.exists(NT):
                    e_norm.wait(pe, t)
                    e_lo.wait(pe, t.plus(-1))
                    for k in range(2):
                        last = pe.transpose(bank[0][0:DK, k * P:(k + 1) * P], xe[:, k * DK:(k + 1) * DK], ident)
                    last.then_inc(e_T.sem, 1)
                if h.exists(NT):
                    s = h.slot(2)
                    e_lo.wait(pe, h)
                    ex = expert_of(h)
                    e_gelu.wait(pe, h.plus(-2))
                    for fc in range(FC):
                        n = 0
                        for k in range(2):
                            cols = bass.ds(ex * (2 * F) + (k * F + fc * P), P)
                            for w, v in ((w1_hi, xeh), (w1_lo, xeh), (w1_hi, xel)):
                                last = pe.matmul(bank[2 + 2 * s + fc // 3][:, fc % 3 * P:(fc % 3 + 1) * P], w[:, cols],
                                                 v[s][:, k, :], start=(n == 0), stop=(n == 5))
                                n += 1
                        if fc % 3 == 2:
                            last.then_inc(e_h.sem, 1)
                if y.exists(NT):
                    s = y.slot(2)
                    ex = expert_of(y)
                    e_res.wait(pe, y.plus(-2))
                    dst = bank[6 + s][:, 0:D]
                    row = bass.ds(ex * D, D)
                    pe.matmul(dst, one16[:], b2_hi[:, row], start=True, stop=False)
                    pe.matmul(dst, one16[:], b2_lo[:, row], start=False, stop=False)
                    for fc in range(FC):
                        if fc % 3 == 0:
                            e_hl.wait(pe, y, fc // 3 + 1)
                        cols = bass.ds(ex * (FC * D) + fc * D, D)
                        for n, (v, w) in enumerate(((hh, w2_hi), (hh, w2_lo), (hl, w2_hi))):
                            last = pe.matmul(dst, v[s][:, fc, :], w[:, cols], start=False,
                                             stop=(fc == FC - 1 and n == 2))
                    last.then_inc(e_y.sem, 1)

            expert_steps(pe, estep)


_INS = ["x", "x_txt", "L0_tok_ln1_g", "L0_tok_ln1_b", "L0_tok_W_lin", "L0_tok_b_lin", "L0_tok_ln2_g", "L0_tok_ln2_b",
        "L0_tok_pos_embedding", "L0_tok_cls_token", "L0_txt_atom_configs", "L0_txt_subshell_embeds",
        "L0_txt_occupancy_embeds", "L0_attn_w_qkv", "L0_attn_w_out", "L0_ffn_Ws", "L0_ffn_bs", "L0_ffn_W1", "L0_ffn_b1",
        "L0_ffn_W2", "L0_ffn_b2"]


def kernel(**inputs):
    import concourse.bacc as _bacc
    from concourse.bass_utils import run_bass_kernel_spmd as _run

    nc = _bacc.Bacc("TRN2", target_bir_lowering=False, num_devices=1)
    arrays, args = {}, []
    for name in _INS:
        a = np.ascontiguousarray(inputs[name])
        arrays[f"in_{name}"] = a
        args.append(nc.dram_tensor(f"in_{name}", a.shape, mybir.dt.from_np(a.dtype), kind="ExternalInput").ap())
    arrays["consts"] = shape_constants()
    args.append(nc.dram_tensor("consts", arrays["consts"].shape, F32, kind="ExternalInput").ap())
    args.append(nc.dram_tensor("out", (T, D), F32, kind="ExternalOutput").ap())
    build(nc, *args)
    r = _run(nc, [arrays], core_ids=[0])
    return r.results[0]["out"].reshape(B, S, D)
```

```python
from contextlib import ExitStack

import numpy as np

import concourse.bass as bass
from concourse import mybir

F32 = mybir.dt.float32
F16 = mybir.dt.float16
BF16 = mybir.dt.bfloat16
I32 = mybir.dt.int32
ALU = mybir.AluOpType
ACT = mybir.ActivationFunctionType
AX = mybir.AxisListType

P = 128
B, C, IMG, PATCH = 32, 3, 96, 16
G = IMG // PATCH
NPATCH = G * G
NIMG = NPATCH + 1
TXT = 128
S = NIMG + TXT
SP = TXT + 64
D = 192
DK = D // 2
H, DH = 12, 16
HG, HJ = 3, 4
NAT, NCFG = 119, 28
E, F = 8, 768
FC = F // P
T = B * S
OB = -(-HG * S // 32)
CAP = (T + P + 31) // 32 * 32
ROW = 196
C_MEAN, C_RSTD, C_PROB, C_ID = 192, 193, 194, 195
NT = T // P + E
EPS = 1e-5
QK_SCALE = 8.0
MAX_SCALE = 16.0
W_SCALE = 64.0
XS = 8
RS = 6
LG = 2 * D
PAD_ID = 1 << 20

K_ID, K_TRI, K_KLO, K_K2M, K_K2A, K_VALID, K_IDS, K_BASE, K_FIRST, K_TILE, K_PART, K_PADID, K_HALF = (
    0, 128, 256, 257, 258, 259, 261, 263, 271, 287, 287 + NT, 288 + NT, 289 + NT)
K_END = 291 + NT


def shape_constants():
    k = np.zeros((P, K_END), np.float32)
    p = np.arange(P)
    r = p % 32
    k[:, K_ID:K_ID + P] = np.eye(P)
    k[:, K_TRI:K_TRI + P] = p[:, None] < p[None, :]
    k[:, K_KLO] = -(r >= DH).astype(np.float32)
    k[:, K_K2M] = r < DH
    k[:, K_K2A] = MAX_SCALE * (r == DH)
    k[:, K_VALID] = 1
    k[:, K_VALID + 1] = p < NIMG
    k[:, K_IDS] = NIMG + p
    k[:, K_IDS + 1] = p
    k[:, K_BASE:K_BASE + E] = CAP * np.arange(E)
    k[:, K_FIRST:K_FIRST + 2 * E] = np.tile(E - np.arange(E), 2)
    k[:, K_TILE:K_TILE + NT] = np.arange(NT)
    k[:, K_PART] = p
    k[:, K_PADID] = PAD_ID
    k[:, K_HALF] = p < NIMG
    k[:, K_HALF + 1] = (p >= 64) & (p < 64 + NIMG)
    return k


def spread(ap, axis, n):
    shape = list(ap.shape)
    shape[axis] = n
    return ap.broadcast_to(shape)


class Turn:

    def __init__(self, c, r=None, n=1):
        self.c, self.r, self.n = c, r, n

    def plus(self, d):
        return Turn(self.c + d, self.r, self.n)

    def lin(self, a, k=0):
        return a * self.c + k if self.r is None else self.r * (a * self.n) + (a * self.c + k)

    def of(self, m):
        return self.c // m if self.r is None else self.r * (self.n // m) + self.c // m

    def slot(self, m):
        return self.c % m

    def exists(self, count):
        return self.r is not None or 0 <= self.c < count


class Event:

    def __init__(self, sem, per=1):
        self.sem, self.per = sem, per

    def wait(self, eng, item, k=None):
        if item.r is None and item.c < 0:
            return
        eng.wait_ge(self.sem, item.lin(self.per, self.per if k is None else k))


def build(nc, x, x_txt, ln1_g, ln1_b, W_lin, b_lin, ln2_g, ln2_b, pos, cls_tok, cfg, sub_e, occ_e,
          w_qkv, w_out, Ws, bs, W1, b1, W2, b2, consts, out):
    ctx = ExitStack()
    with ctx:
        def sb(name, shape, dt=F32):
            return ctx.enter_context(nc.sbuf_tensor(name, shape, dt))

        def sem(name):
            return ctx.enter_context(nc.semaphore(name))

        def ev(name, per=1):
            return Event(sem(name), per)

        bank = [ctx.enter_context(nc.psum_tensor(f"bank{i}", [P, 512], F32)) for i in range(8)]

        himg = nc.dram_tensor("himg", (B, NIMG, D), F32, kind="Internal").ap()
        atoms = nc.dram_tensor("atoms", (NAT, D), F32, kind="Internal").ap()
        routed = nc.dram_tensor("routed", (E * CAP + P, ROW), F32, kind="Internal").ap()

        con = sb("con", [P, K_END])
        neg_id = sb("neg_id", [P, P], BF16)
        tri = sb("tri", [P, P], BF16)
        ones = sb("ones", [P, P], BF16)
        one16 = sb("one16", [1, P], F16)
        halfs = sb("halfs", [P, 2 * G])
        ident = con[:, K_ID:K_ID + P]
        wqk_hi = sb("wqk_hi", [DK, 2, 2, HG * P], F16)
        wqk_lo = sb("wqk_lo", [DK, 2, 2, HG * P], F16)
        wo = sb("wo", [P, HG, D])
        ws = sb("ws", [DK, 2, E])
        bs_all = sb("bs_all", [P, 2, E])
        w2_hi = sb("w2_hi", [P, E * FC * D], F16)
        w2_lo = sb("w2_lo", [P, E * FC * D], F16)
        b1T = sb("b1T", [P, E * FC])
        b2_hi = sb("b2_hi", [1, E * D], F16)
        b2_lo = sb("b2_lo", [1, E * D], F16)
        wstage1 = sb("wstage1", [DK, F])
        wstage2 = sb("wstage2", [P, 3 * D])

        X = [sb(f"x{i}", [P, 2, D]) for i in range(XS)]
        txt_i = sb("txt_i", [P, B + 1], I32)
        txt_now = [sb(f"txt_now{i}", [P, 1], I32) for i in range(2)]
        padrow = sb("padrow", [P, ROW])
        st1 = sb("st1", [P, 2, 6])
        mv1 = sb("mv1", [P, 2, 2])
        var1 = sb("var1", [P, 2])
        rstd1 = sb("rstd1", [P, 2])
        neg1 = sb("neg1", [P, 2])
        shift1 = sb("shift1", [P, 2])
        xn = sb("xn", [P, 2, D])
        xh = [sb(f"xh{i}", [DK, 2, SP], F16) for i in range(2)]
        xl = [sb(f"xl{i}", [DK, 2, SP], F16) for i in range(2)]
        kh = sb("kh", [P, HG, S], F16)
        k1 = [sb(f"k1_{i}", [P, HG, SP], F16) for i in range(2)]
        k2 = [sb(f"k2_{i}", [P, HG, SP], F16) for i in range(2)]
        q1 = [sb(f"q1_{i}", [P, HG, SP], F16) for i in range(2)]
        q2 = [sb(f"q2_{i}", [P, HG, S], F16) for i in range(2)]
        qlo = sb("qlo", [P, HG, S], F16)
        V = [sb(f"v{i}", [P, 2, H, 32]) for i in range(2)]
        mxa = sb("mxa", [P, HG, P], BF16)
        mxb = sb("mxb", [P, 2, P], BF16)
        recip = sb("recip", [P, OB])
        ot = sb("ot", [P, HG, S])
        hrow = [sb(f"hrow{i}", [P, 2, ROW]) for i in range(2)]
        st2 = sb("st2", [P, 2, 6])
        mv2 = sb("mv2", [P, 2, 2])
        var2 = sb("var2", [P, 2])
        neg2 = sb("neg2", [P, 2])
        shift2 = sb("shift2", [P, 2])
        xn2 = sb("xn2", [P, 2, D])
        xT2 = sb("xT2", [DK, 2, 2 * P])
        lg = sb("lg", [P, 2, E])
        lgm = sb("lgm", [P, 2])
        lgd = sb("lgd", [P, 2, E])
        lge = sb("lge", [P, 2, E])
        esum = sb("esum", [P, 2])
        first = sb("first", [P, 2, E])
        firstm = sb("firstm", [P, 2])
        oh = sb("oh", [P, 2, E])
        ohb = sb("ohb", [P, 2, E], BF16)
        count = sb("count", [P, E])
        rank = sb("rank", [P, 2, E])
        slotf = sb("slotf", [P, 2])
        slot_i = [sb(f"slot_i{i}", [P, 2], I32) for i in range(2)]
        ids = sb("ids", [P, 2])

        embed_ctx = ExitStack()

        def sbe(name, shape, dt=F32):
            return embed_ctx.enter_context(nc.sbuf_tensor(name, shape, dt))

        IH = B // 2
        PR = IH * G
        xi = [sbe(f"xi{i}", [PR, C, PATCH * IMG]) for i in range(2)]
        sti = sbe("sti", [PR, 2 * G, C, 6])
        mvi = sbe("mvi", [PR, 2 * G, 2])
        vari = sbe("vari", [PR, 2 * G])
        rstdi = sbe("rstdi", [PR, 2 * G])
        xni = [sbe(f"xni{i}", [PR, C * 2, P]) for i in range(2)]
        xTi = [sbe(f"xTi{i}", [P, C * 2, PR]) for i in range(2)]
        wl = sbe("wl", [P, 2, C, D])
        wlg = sbe("wlg", [P, 2, C, D])
        g1 = sbe("g1", [P, 2, C])
        b1v = sbe("b1v", [P, 2, C])
        bl_all = sbe("bl_all", [P, D])
        bias_all = sbe("bias_all", [P, D])
        g2_all = sbe("g2_all", [P, D])
        b2_all = sbe("b2_all", [P, D])
        posr = sbe("posr", [PR, G * D])
        clsr = sbe("clsr", [B, D])
        posc = sbe("posc", [B, D])
        yi = sbe("yi", [PR, G, D])
        sty = sbe("sty", [PR, G, 6])
        mvy = sbe("mvy", [PR, G, 2])
        vary = sbe("vary", [PR, G])
        rstdy = sbe("rstdy", [PR, G])
        img = [sbe(f"img{i}", [PR, G, D]) for i in range(2)]
        cfg_s = sbe("cfg_s", [NAT, NCFG])
        cfg2 = sbe("cfg2", [NAT, 2, 32])
        cfgT = sbe("cfgT", [32, 2, NAT])
        emb = sbe("emb", [NCFG, 2, D])
        tab = sbe("tab", [NAT, D])

        wqkv = sbe("wqkv", [DK, 2, 2 * D])
        wdup = sbe("wdup", [DK, 2, 2 * H, 2, DH])
        b1r = sbe("b1r", [E * FC, P])
        b2r = sbe("b2r", [1, E * D])
        txt = sbe("txt", [B, P], I32)
        txt_f = sbe("txt_f", [B, P])
        txt_neg = sbe("txt_neg", [B, P])
        embed_ctx.close()

        pa = [sb(f"pa{j}", [P, HG * S]) for j in range(HJ)]
        pb = [sb(f"pb{j}", [P, 2 * S]) for j in range(HJ)]
        oT = sb("oT", [P, OB * 32])
        den = sb("den", [P, OB * 32])

        w1_hi = sb("w1_hi", [DK, E * 2 * F], F16)
        w1_lo = sb("w1_lo", [DK, E * 2 * F], F16)
        pad_f = sb("pad_f", [P, E])
        pad_i = sb("pad_i", [P, E], I32)
        cnt_f = sb("cnt_f", [1, E])
        cnt_i = sb("cnt_i", [1, E], I32)
        ntile = sb("ntile", [1, E])
        cum = sb("cum", [1, E])
        skip = sb("skip", [1, E])
        reached = sb("reached", [1, NT])
        tl_f = sb("tl_f", [1, 2, NT])
        tl = sb("tl", [1, 2, NT], I32)
        R = [sb(f"r{i}", [P, ROW]) for i in range(RS)]
        xe = [sb(f"xe{i}", [P, D]) for i in range(2)]
        xeh = [sb(f"xeh{i}", [DK, 2, P], F16) for i in range(2)]
        xel = [sb(f"xel{i}", [DK, 2, P], F16) for i in range(2)]
        hf = [sb(f"hf{i}", [P, FC, P]) for i in range(2)]
        hh = [sb(f"hh{i}", [P, FC, P], F16) for i in range(2)]
        hl = [sb(f"hl{i}", [P, FC, P], F16) for i in range(2)]
        res = [sb(f"res{i}", [P, D]) for i in range(3)]

        con_in = sem("con_in")
        patch_w_in = sem("patch_w_in")
        image_in = [sem(f"image_in{i}") for i in range(2)]
        atom_in = sem("atom_in")
        attn_w_in = sem("attn_w_in")
        route_w_in = sem("route_w_in")
        atoms_out = sem("atoms_out")
        himg_out = sem("himg_out")
        pool_zeroed = sem("pool_zeroed")
        pool_setup = sem("pool_setup")
        dve_setup = sem("dve_setup")
        pe_setup = sem("pe_setup")
        act_setup = sem("act_setup")
        dve_patch = sem("dve_patch")
        patch_stats = sem("patch_stats")
        patch_norm = sem("patch_norm")
        pe_patchT = sem("pe_patchT")
        act_patchT = sem("act_patchT")
        pe_patchY = sem("pe_patchY")
        patch_y = sem("patch_y")
        y_stats = sem("y_stats")
        img_ready = sem("img_ready")
        pool_patch = sem("pool_patch")
        img_step = sem("img_step")
        w_ready = sem("w_ready")
        list_step = sem("list_step")
        pool_apart, dve_apart = sem("pool_apart"), sem("dve_apart")

        xi_in = [sem(f"xi_in{i}") for i in range(XS)]
        xt_in = [sem(f"xt_in{i}") for i in range(XS)]
        w1_in, w2_in = ev("w1_in", 16), ev("w2_in", 16)
        w_split = ev("w_split", 6)
        ln_stats = ev("ln_stats", 4)
        ln_rstd = ev("ln_rstd", 4)
        x_norm = ev("x_norm")
        x_T = ev("x_T")
        x_hi = ev("x_hi")
        x_lo = ev("x_lo")
        k_proj, q_proj, v_proj = ev("k_proj"), ev("q_proj"), ev("v_proj")
        k_hi, q_hi, v_out = ev("k_hi"), ev("q_hi"), ev("v_out")
        k_st1, k_st2, q_rest, q_st2 = ev("k_st1"), ev("k_st2"), ev("q_rest"), ev("q_st2")
        max_scores = ev("max_scores", 8)
        max_taken = ev("max_taken", 8)
        max_rows = ev("max_rows")
        sc_a, sc_b = ev("sc_a", 4), ev("sc_b", 4)
        exp_a, exp_b = ev("exp_a", 4), ev("exp_b", 4)
        pv = ev("pv")
        o_norm = ev("o_norm", 4)
        o_proj = ev("o_proj")
        h_sum = ev("h_sum", 2)
        ln2_stats = ev("ln2_stats", 4)
        ln2_rstd = ev("ln2_rstd", 5)
        x2_norm = ev("x2_norm")
        x2_T = ev("x2_T")
        x2_out = ev("x2_out")
        logits = ev("logits")
        onehot = ev("onehot", 7)
        lg_exp = ev("lg_exp")
        prob = ev("prob", 3)
        ranks = ev("ranks")
        slots = ev("slots", 5)
        id_put = ev("id_put", 2)
        idx_put = ev("idx_put")
        scattered = [sem(f"scattered{i}") for i in range(2)]

        pads_i = sem("pads_i")
        pads_out = sem("pads_out")
        tiles = sem("tiles")
        r_in = [sem(f"r_in{i}") for i in range(RS)]
        e_norm, e_T, e_hi, e_lo = ev("e_norm"), ev("e_T"), ev("e_hi"), ev("e_lo")
        e_h = ev("e_h", 2)
        e_gelu = ev("e_gelu", 2)
        e_hh = ev("e_hh", 2)
        e_hl = ev("e_hl", 2)
        e_y = ev("e_y")
        e_res = ev("e_res")
        e_out = [sem(f"e_out{i}") for i in range(RS)]

        w1_pieces = W1.rearrange("e (k p) f -> (e k) p f", k=2)
        w2_pieces = W2.rearrange("e (c p) d -> p (e c) d", p=P)

        HEAD, TAIL, UN = XS, 6, XS

        def apart(eng, mark):
            eng.sem_inc(mark, 1)

        def attend_steps(eng, step):
            def at(i):
                step(*(i.plus(-d) for d in range(TAIL + 1)))
            for i in range(HEAD):
                at(Turn(i))
            with eng.Fori(HEAD // UN, B // UN) as r:
                for u in range(UN):
                    at(Turn(u, r, UN))
            for i in range(B, B + TAIL):
                at(Turn(i))

        def expert_steps(eng, step):
            def at(i):
                step(i, i.plus(-1), i.plus(-2))
            for i in range(RS):
                at(Turn(i))
            with eng.Fori(1, NT // RS) as r:
                for u in range(RS):
                    at(Turn(u, r, RS))
            for i in range(NT // RS * RS, NT + 2):
                at(Turn(i))

        block = ctx.enter_context(nc.Block())

        @block.sync
        def _(sp):
            sp.dma_start(con[:], consts).then_inc(con_in, 16)
            for h in range(2):
                for i in range(IH):
                    sp.dma_start(xi[h][i * G:(i + 1) * G, :, :],
                                 x[h * IH + i].rearrange("c (n r) w -> n c (r w)", n=G)).then_inc(image_in[h], 16)
            sp.dma_start(wqkv[:], w_qkv.rearrange("(k p) n -> p k n", k=2)[:, :, 0:2 * D]).then_inc(attn_w_in, 16)
            sp.wait_ge(pool_zeroed, 1)
            for j in range(HJ):
                sp.dma_start(wo[32 * j:32 * j + DH, :, :],
                             w_out.rearrange("(g j r) d -> j r g d", g=HG, j=HJ)[j]).then_inc(attn_w_in, 16)
            sp.dma_start(ws[:], Ws.rearrange("(k p) e -> p k e", k=2)).then_inc(route_w_in, 16)
            for t in range(2):
                sp.dma_start(bs_all[:, t, :], spread(bs.rearrange("(a e) -> a e", a=1), 0, P)).then_inc(route_w_in, 16)
            sp.dma_start(b1r[:], b1.rearrange("e (c p) -> (e c) p", p=P)).then_inc(route_w_in, 16)
            sp.dma_start(b2r[:], b2.rearrange("(a e) d -> a (e d)", a=1)).then_inc(route_w_in, 16)
            sp.wait_ge(dve_setup, 7)
            sp.dma_start(himg[:, 0, :], clsr[:]).then_inc(himg_out, 16)
            for h in range(2):
                sp.wait_ge(img_ready, h + 1)
                for i in range(IH):
                    sp.dma_start(himg[h * IH + i, 1:NIMG, :].rearrange("(n w) d -> n (w d)", n=G),
                                 img[h][i * G:(i + 1) * G, :, :].rearrange("p w d -> p (w d)")).then_inc(himg_out, 16)
            sp.wait_ge(himg_out, 16 * (1 + B))
            sp.dma_start(X[0][0:NIMG, 1, :], himg[0]).then_inc(xi_in[0], 16)

            def step(l, *later):
                if l.exists(B) and l.slot(2) == 0:
                    w_split.wait(sp, Turn(l.c // 2 - 1, l.r, l.n // 2))
                    sp.dma_start(wstage1[:], w1_pieces[l.of(2)]).then_inc(w1_in.sem, 16)
                    piece = l.of(2)
                    sp.dma_start(wstage2[:].rearrange("p (c d) -> p c d", d=D),
                                 w2_pieces[:, bass.ds(piece * 3, 3), :]).then_inc(w2_in.sem, 16)
                if l.exists(B) and not (l.r is None and l.c == 0):
                    h_sum.wait(sp, l.plus(-XS))
                    src = l.c if l.r is None else l.lin(1)
                    sp.dma_start(X[l.slot(XS)][0:NIMG, 1, :], himg[src]).then_inc(xi_in[l.slot(XS)], 16)

            attend_steps(sp, step)

            def estep(t, h, y):
                if t.exists(NT):
                    if t.r is None and t.c == 0:
                        for i in range(2):
                            sp.wait_ge(scattered[i], 32 * (B // 2))
                        sp.wait_ge(pads_out, 16 * (E + 1))
                        sp.wait_ge(tiles, 1)
                    if t.plus(-RS).exists(NT):
                        sp.wait_ge(e_out[t.slot(RS)], t.plus(-RS).of(RS) * 16 + 16)
                    row = sp.value_load(tl[0:1, 0, bass.ds(t.lin(1), 1)] if t.r is not None
                                        else tl[0:1, 0, t.c:t.c + 1], min_val=0, max_val=E * CAP)
                    sp.dma_start(R[t.slot(RS)][:], routed[bass.ds(row, P), :]).then_inc(r_in[t.slot(RS)], 16)

            expert_steps(sp, estep)

        @block.gpsimd
        def _(pool):
            pool.memset(wo[:], 0.0).then_inc(pool_zeroed, 1)
            pool.memset(halfs[:], -0.5)
            pool.memset(one16[:], 1.0)
            pool.memset(ones[:], 1.0)
            for i in range(XS):
                pool.memset(X[i][:, 1, :], 0.0)
            for i in range(2):
                for t in (k1[i], k2[i], q1[i], hrow[i], V[i]):
                    pool.memset(t[:], 0.0)
            pool.memset(mxa[:], 0.0)
            pool.memset(mxb[:], 0.0)
            pool.memset(xT2[:], 0.0)
            pool.memset(padrow[:], 0.0)
            pool.memset(cfg2[:], 0.0).then_inc(pool_zeroed, 1)
            pool.wait_ge(pool_zeroed, 2)
            pool.wait_ge(con_in, 16)
            for i in range(2):
                pool.memset(V[i][:, 0, :, DH:DH + 1], 1.0)
                for h in range(H):
                    g = h // HJ
                    pool.tensor_copy(V[i][:, 1, h, DH:DH + 1], con[:, K_HALF + g % 2:K_HALF + g % 2 + 1])
            pool.wait_ge(con_in, 16)
            pool.tensor_copy(padrow[:, C_ID:C_ID + 1].bitcast(I32), con[:, K_PADID:K_PADID + 1])
            pool.tensor_copy(count[:], con[:, K_BASE:K_BASE + E])
            pool.tensor_copy(ids[:], con[:, K_IDS:K_IDS + 2]).then_inc(pool_setup, 1)
            for h in range(2):
                pool.wait_ge(patch_stats, h + 1)
                v = slice(h * G, (h + 1) * G)
                pool.tensor_scalar(vari[:, v], mvi[:, v, 1], EPS, None, ALU.add).then_inc(pool_patch, 1)
                pool.wait_ge(pool_patch, 4 * h + 1)
                pool.tensor_tensor(rstdi[:, v], vari[:, v], halfs[0:PR, 0:G], ALU.pow).then_inc(pool_patch, 1)
                pool.wait_ge(y_stats, h + 1)
                pool.tensor_scalar(vary[:], mvy[:, :, 1], EPS, None, ALU.add).then_inc(pool_patch, 1)
                pool.wait_ge(pool_patch, 4 * h + 3)
                pool.tensor_tensor(rstdy[:], vary[:], halfs[0:PR, 0:G], ALU.pow).then_inc(pool_patch, 1)
            pool.wait_ge(atoms_out, 16)
            pool.wait_ge(dve_setup, 13)
            pool.indirect_dma_start(X[0][:, 0, :], None, atoms,
                                    bass.IndirectOffsetOnAxis(txt_i[:, 0:1], 0)).then_inc(xt_in[0], 16)

            def step(s, l, f, m, a, p, r):
                n = s.plus(1)
                if n.r is not None or n.c < B:
                    h_sum.wait(pool, n.plus(-XS))
                    o = n.plus(-2)
                    if o.r is not None or o.c >= 0:
                        pool.wait_ge(xt_in[o.slot(XS)], o.of(XS) * 16 + 16)
                    idx = txt_i[:, n.c:n.c + 1] if n.r is None else txt_i[:, bass.ds(n.lin(1), 1)]
                    apart(pool, pool_apart)
                    pool.tensor_copy(txt_now[n.slot(2)][:], idx).then_inc(idx_put.sem, 1)
                    idx_put.wait(pool, n.plus(-1))
                    apart(pool, pool_apart)
                    pool.indirect_dma_start(X[n.slot(XS)][:, 0, :], None, atoms,
                                            bass.IndirectOffsetOnAxis(txt_now[n.slot(2)][:], 0)).then_inc(xt_in[n.slot(XS)], 16)
                if s.r is None and s.c == 0:
                    pool.wait_ge(himg_out, 16 * (1 + B))
                    pool.wait_ge(w_ready, 12)
                if s.exists(B) and s.slot(2) == 0:
                    w = Turn(s.c // 2, s.r, s.n // 2)
                    if s.r is None:
                        d1, d2 = slice(w.c * F, w.c * F + F), slice(w.c * 3 * D, (w.c + 1) * 3 * D)
                    else:
                        d1, d2 = bass.ds(s.of(2) * F, F), bass.ds(s.of(2) * (3 * D), 3 * D)
                    w1_in.wait(pool, w)
                    apart(pool, pool_apart)
                    pool.tensor_scalar(wstage1[:], wstage1[:], W_SCALE, None, ALU.mult).then_inc(w_split.sem, 1)
                    w2_in.wait(pool, w)
                    apart(pool, pool_apart)
                    pool.tensor_scalar(wstage2[:], wstage2[:], W_SCALE, None, ALU.mult).then_inc(w_split.sem, 1)
                    w_split.wait(pool, w, 2)
                    apart(pool, pool_apart)
                    pool.tensor_copy(w1_hi[:, d1], wstage1[:]).then_inc(w_split.sem, 1)
                    pool.tensor_copy(w2_hi[:, d2], wstage2[:]).then_inc(w_split.sem, 1)
                if s.exists(B):
                    ln_stats.wait(pool, s)
                    ln_rstd.wait(pool, s.plus(-1))
                    x_norm.wait(pool, s.plus(-1))
                    apart(pool, pool_apart)
                    pool.tensor_scalar(var1[:], mv1[:, :, 1], EPS, None, ALU.add).then_inc(ln_rstd.sem, 1)
                    pool.tensor_scalar(neg1[:], mv1[:, :, 0], -1.0, None, ALU.mult).then_inc(ln_rstd.sem, 1)
                    ln_rstd.wait(pool, s, 1)
                    pool.tensor_tensor(rstd1[:], var1[:], halfs[:, 0:2], ALU.pow).then_inc(ln_rstd.sem, 1)
                if s.exists(B) and s.slot(2) == 0:
                    w_split.wait(pool, w, 4)
                    pool.tensor_tensor(w1_lo[:, d1], wstage1[:], w1_hi[:, d1], ALU.subtract).then_inc(w_split.sem, 1)
                    pool.tensor_tensor(w2_lo[:, d2], wstage2[:], w2_hi[:, d2], ALU.subtract).then_inc(w_split.sem, 1)
                if s.exists(B):
                    ln_rstd.wait(pool, s, 3)
                    pool.tensor_tensor(shift1[:], neg1[:], rstd1[:], ALU.mult).then_inc(ln_rstd.sem, 1)
                if p.exists(B):
                    c = p.slot(2)
                    ln2_stats.wait(pool, p)
                    ln2_rstd.wait(pool, p.plus(-1))
                    x2_norm.wait(pool, p.plus(-1))
                    apart(pool, pool_apart)
                    pool.tensor_scalar(var2[:], mv2[:, :, 1], EPS, None, ALU.add).then_inc(ln2_rstd.sem, 1)
                    pool.tensor_scalar(neg2[:], mv2[:, :, 0], -1.0, None, ALU.mult).then_inc(ln2_rstd.sem, 1)
                    pool.tensor_copy(hrow[c][:, :, C_MEAN], mv2[:, :, 0]).then_inc(ln2_rstd.sem, 1)
                    ln2_rstd.wait(pool, p, 1)
                    pool.tensor_tensor(hrow[c][:, :, C_RSTD], var2[:], halfs[:, 0:2], ALU.pow).then_inc(ln2_rstd.sem, 1)
                    ln2_rstd.wait(pool, p, 4)
                    pool.tensor_tensor(shift2[:], neg2[:], hrow[c][:, :, C_RSTD], ALU.mult).then_inc(ln2_rstd.sem, 1)
                if f.exists(B):
                    k_hi.wait(pool, f)
                    sc_b.wait(pool, f.plus(-2))
                    apart(pool, pool_apart)
                    pool.tensor_scalar(k2[f.slot(2)][:, :, 0:S], kh[:], con[:, K_K2M:K_K2M + 1], con[:, K_K2A:K_K2A + 1],
                                       ALU.mult, ALU.add).then_inc(k_st2.sem, 1)
                if r.exists(B):
                    c = r.slot(2)
                    id_put.wait(pool, r.plus(-1))
                    apart(pool, pool_apart)
                    pool.tensor_copy(hrow[c][:, :, C_ID].bitcast(I32), ids[:]).then_inc(id_put.sem, 1)
                    pool.tensor_scalar(ids[:], ids[:], float(S), None, ALU.add).then_inc(id_put.sem, 1)
                    id_put.wait(pool, r)
                    slots.wait(pool, r)
                    prob.wait(pool, r)
                    ln2_rstd.wait(pool, r)
                    apart(pool, pool_apart)
                    pool.indirect_dma_start(routed, bass.IndirectOffsetOnAxis(slot_i[c][:, 0:1], 0),
                                            hrow[c][:, 0, :], None).then_inc(scattered[c], 16)
                    pool.indirect_dma_start(routed, bass.IndirectOffsetOnAxis(slot_i[c][0:NIMG, 1:2], 0),
                                            hrow[c][0:NIMG, 1, :], None).then_inc(scattered[c], 16)

            attend_steps(pool, step)
            pool.wait_ge(pads_i, 2)
            for e in range(E):
                pool.indirect_dma_start(routed, bass.IndirectOffsetOnAxis(pad_i[:, e:e + 1], 0),
                                        padrow[:], None).then_inc(pads_out, 16)
            pool.dma_start(routed[E * CAP:E * CAP + P, :], padrow[:]).then_inc(pads_out, 16)

            def estep(t, h, y):
                if y.exists(NT):
                    e_res.wait(pool, y)
                    s = y.slot(RS)
                    apart(pool, pool_apart)
                    pool.indirect_dma_start(out, bass.IndirectOffsetOnAxis(R[s][:, C_ID:C_ID + 1].bitcast(I32), 0),
                                            res[y.slot(3)][:], None, bounds_check=T - 1, oob_is_err=False).then_inc(e_out[s], 16)

            expert_steps(pool, estep)
            pool.wait_ge(xt_in[0], 16 * (B // XS + 1))
            for s in range(RS):
                pool.wait_ge(e_out[s], 16 * ((NT - s + RS - 1) // RS))

        @block.scalar
        def _(act):
            act.dma_start(wl[:], W_lin.rearrange("(f p c) d -> p f c d", f=2, c=C)).then_inc(patch_w_in, 16)
            act.dma_start(g1[:], ln1_g.rearrange("(f p c) -> p f c", f=2, c=C)).then_inc(patch_w_in, 16)
            act.dma_start(b1v[:], ln1_b.rearrange("(f p c) -> p f c", f=2, c=C)).then_inc(patch_w_in, 16)
            for t, src in ((bl_all, b_lin), (g2_all, ln2_g), (b2_all, ln2_b)):
                act.dma_start(t[:], spread(src.rearrange("(a d) -> a d", a=1), 0, P)).then_inc(patch_w_in, 16)
            for i in range(IH):
                act.dma_start(posr[i * G:(i + 1) * G, :],
                              pos[0, 1:NIMG, :].rearrange("(n w) d -> n (w d)", n=G)).then_inc(patch_w_in, 16)
            act.dma_start(clsr[:], spread(cls_tok[0], 0, B)).then_inc(patch_w_in, 16)
            act.dma_start(posc[:], spread(pos[0, 0:1, :], 0, B)).then_inc(patch_w_in, 16)
            act.dma_start(cfg_s[:], cfg).then_inc(atom_in, 16)
            act.dma_start(emb[:, 0, :], sub_e).then_inc(atom_in, 16)
            act.dma_start(emb[:, 1, :], occ_e).then_inc(atom_in, 16)
            act.dma_start(txt[:], x_txt).then_inc(atom_in, 16)
            act.wait_ge(dve_setup, 6)
            act.wait_ge(dve_setup, 12)
            act.dma_start(atoms, tab[:]).then_inc(atoms_out, 16)
            for i in range(2 * G):
                act.wait_ge(pe_patchT, i + 1)
                if i >= 2:
                    act.wait_ge(pe_patchY, i - 1)
                for c in range(2):
                    last = act.activation(xTi[i % 2][:, 3 * c:3 * c + 3, :],
                                          bank[2 * (i % 2) + c][:, 0:3 * PR].rearrange("p (c n) -> p c n", c=3),
                                          ACT.Copy)
                last.then_inc(act_patchT, 1)

            def exps(a, j):
                if j == 0:
                    pv.wait(act, a.plus(-1))
                sc_a.wait(act, a, j + 1)
                act.activation(pa[j][:], bank[4][:, 0:HG * S], ACT.Exp,
                               scale=float(D) ** -0.5 / QK_SCALE ** 2).then_inc(exp_a.sem, 1)
                sc_b.wait(act, a, j + 1)
                act.activation(pb[j][:], bank[5][:, 0:2 * S], ACT.Exp,
                               scale=float(D) ** -0.5 / QK_SCALE ** 2).then_inc(exp_b.sem, 1)

            def step(s, l, f, m, a, p, r):
                if a.exists(B):
                    exps(a, 0)
                if r.exists(B):
                    x2_T.wait(act, r)
                    logits.wait(act, r.plus(-1))
                    act.activation(xT2[:, :, 0:SP], bank[0][0:DK, 0:2 * SP].rearrange("p (k n) -> p k n", k=2),
                                   ACT.Copy).then_inc(x2_out.sem, 1)
                if a.exists(B):
                    exps(a, 1)
                    exps(a, 2)
                if l.exists(B):
                    x_T.wait(act, l)
                    v_proj.wait(act, l.plus(-2))
                    act.activation(xh[l.slot(2)][:], bank[0][0:DK, 0:2 * SP].rearrange("p (k n) -> p k n", k=2),
                                   ACT.Copy).then_inc(x_hi.sem, 1)
                if r.exists(B):
                    onehot.wait(act, r, 3)
                    prob.wait(act, r.plus(-1), 1)
                    act.activation(lge[:], lgd[:], ACT.Exp).then_inc(lg_exp.sem, 1)
                if a.exists(B):
                    exps(a, 3)
                if f.exists(B):
                    k_proj.wait(act, f)
                    k_st1.wait(act, f.plus(-1))
                    k_st2.wait(act, f.plus(-1))
                    act.activation(kh[:].rearrange("p g n -> p (g n)"), bank[2][:, 0:HG * S], ACT.Copy).then_inc(k_hi.sem, 1)
                    q_proj.wait(act, f)
                    sc_b.wait(act, f.plus(-2))
                    act.activation(q1[f.slot(2)][:, :, 0:S], bank[3][:, 0:HG * S].rearrange("p (g n) -> p g n", g=HG),
                                   ACT.Copy).then_inc(q_hi.sem, 1)
                if s.exists(B):
                    ln_rstd.wait(act, s)
                    x_T.wait(act, s.plus(-1))
                    for t in range(2):
                        last = act.activation(xn[:, t, :], X[s.slot(XS)][:, t, :], ACT.Identity,
                                              bias=shift1[:, t:t + 1], scale=rstd1[:, t:t + 1])
                    last.then_inc(x_norm.sem, 1)
                if p.exists(B):
                    ln2_rstd.wait(act, p)
                    h_sum.wait(act, p)
                    x2_T.wait(act, p.plus(-1))
                    c = p.slot(2)
                    for t in range(2):
                        last = act.activation(xn2[:, t, :], hrow[c][:, t, 0:D], ACT.Identity,
                                              bias=shift2[:, t:t + 1], scale=hrow[c][:, t, C_RSTD:C_RSTD + 1])
                    last.then_inc(x2_norm.sem, 1)
                if f.exists(B):
                    v_proj.wait(act, f)
                    pv.wait(act, f.plus(-2))
                    pv_out = bank[2][:, 0:2 * D].rearrange("p (t h d) -> p t h d", t=2, h=H)
                    vs = V[f.slot(2)]
                    act.activation(vs[:, 0, :, 0:DH], pv_out[:, 0], ACT.Copy, scale=1.0 / QK_SCALE)
                    act.activation(vs[64:P, 1, HJ:2 * HJ, 0:DH], pv_out[64:P, 1, HJ:2 * HJ], ACT.Copy, scale=1.0 / QK_SCALE)
                    act.activation(vs[0:64, 1].rearrange("p (g j) d -> p g j d", j=HJ)[:, 0:HG:2, :, 0:DH],
                                   pv_out[0:64, 1].rearrange("p (g j) d -> p g j d", j=HJ)[:, 0:HG:2], ACT.Copy,
                                   scale=1.0 / QK_SCALE).then_inc(v_out.sem, 1)

            attend_steps(act, step)

            def estep(t, h, y):
                if t.exists(NT):
                    e_T.wait(act, t)
                    e_h.wait(act, t.plus(-2))
                    act.activation(xeh[t.slot(2)][:], bank[0][0:DK, 0:2 * P].rearrange("p (k n) -> p k n", k=2),
                                   ACT.Copy).then_inc(e_hi.sem, 1)
                if h.exists(NT):
                    s = h.slot(2)
                    ex = act.value_load(tl[0:1, 1, bass.ds(h.lin(1), 1)] if h.r is not None
                                        else tl[0:1, 1, h.c:h.c + 1], min_val=0, max_val=E - 1)
                    if h.exists(NT):
                        e_hl.wait(act, h.plus(-2))
                    for c in range(2):
                        e_h.wait(act, h, c + 1)
                        for m in range(3):
                            fc = 3 * c + m
                            last = act.activation(hf[s][:, fc, :], bank[2 + 2 * s + c][:, m * P:(m + 1) * P], ACT.Gelu,
                                                  bias=b1T[:, bass.ds(ex * FC + fc, 1)], scale=1.0 / W_SCALE)
                        last.then_inc(e_gelu.sem, 1)

            act.wait_ge(tiles, 1)
            expert_steps(act, estep)

        @block.vector
        def _(dve):
            dve.wait_ge(con_in, 16)
            dve.tensor_scalar(neg_id[:], ident, -1.0 / MAX_SCALE, None, ALU.mult).then_inc(dve_setup, 1)
            dve.tensor_copy(tri[:], con[:, K_TRI:K_TRI + P]).then_inc(dve_setup, 1)
            dve.wait_ge(atom_in, 64)
            dve.wait_ge(pool_zeroed, 2)
            dve.tensor_scalar(cfg2[:, 0, 0:NCFG], cfg_s[:], 0.0, None, ALU.not_equal).then_inc(dve_setup, 1)
            dve.tensor_scalar(cfg2[:, 1, 0:NCFG], cfg_s[:], -1.0, 0.0, ALU.add, ALU.max).then_inc(dve_setup, 1)
            dve.wait_ge(patch_w_in, 16 * (8 + IH))
            for f2 in range(2):
                for c in range(C):
                    last = dve.tensor_scalar(wlg[:, f2, c, :], wl[:, f2, c, :], g1[:, f2, c:c + 1], None, ALU.mult)
            last.then_inc(dve_setup, 1)
            dve.tensor_tensor(posr[:].rearrange("p (w d) -> p w d", d=D), posr[:].rearrange("p (w d) -> p w d", d=D),
                              spread(b2_all[0:PR, :].unsqueeze(1), 1, G), ALU.add).then_inc(dve_setup, 1)
            dve.tensor_tensor(clsr[:], clsr[:], posc[:], ALU.add).then_inc(dve_setup, 1)
            dve.tensor_scalar(txt_neg[:], txt[:], 0.0, float(NAT), ALU.is_lt, ALU.mult)
            dve.tensor_copy(txt_f[:], txt[:]).then_inc(dve_setup, 1)
            dve.wait_ge(dve_setup, 8)
            dve.tensor_tensor(txt_f[:], txt_f[:], txt_neg[:], ALU.add).then_inc(dve_patch, 1)
            dve.wait_ge(dve_patch, 1)
            dve.tensor_scalar(txt_f[:], txt_f[:], 0.0, float(NAT - 1), ALU.max, ALU.min).then_inc(dve_setup, 1)
            dve.wait_ge(pe_setup, 1)
            dve.tensor_tensor(bias_all[:], bank[7][:, 0:D], bl_all[:], ALU.add).then_inc(dve_setup, 1)
            dve.wait_ge(pe_setup, 2)
            dve.tensor_copy(cfgT[:], bank[6][0:32, 0:2 * NAT].rearrange("p (t n) -> p t n", t=2)).then_inc(dve_setup, 1)
            dve.wait_ge(pe_setup, 3)
            dve.tensor_copy(tab[:], bank[7][0:NAT, 0:D]).then_inc(dve_setup, 1)
            dve.memset(txt_i[:, B:B + 1], 0)
            dve.tensor_copy(txt_i[:, 0:B], bank[6][:, 256:256 + B]).then_inc(dve_setup, 1)
            for h in range(2):
                dve.wait_ge(image_in[h], 16 * IH)
                for w in range(G):
                    for c in range(C):
                        last = dve.bn_stats(sti[:, h * G + w, c, :],
                                            xi[h][:, c, :].rearrange("p (r w) -> p r w", r=PATCH)[:, :, w * PATCH:(w + 1) * PATCH])
                last.then_inc(dve_patch, 1)
                dve.wait_ge(dve_patch, 1 + 2 * h + 1)
                for w in range(G):
                    last = dve.bn_aggr(mvi[:, h * G + w, :], sti[:, h * G + w, :, :])
                last.then_inc(patch_stats, 1)
                dve.wait_ge(pool_patch, 4 * h + 2)
                dve.wait_ge(patch_stats, h + 1)

                def y_out(i):
                    dve.wait_ge(pe_patchY, i + 1)
                    dve.tensor_tensor(yi[:, i % G, :], bank[4 + i % 2][0:PR, 0:D], bias_all[0:PR, :],
                                      ALU.add).then_inc(patch_y, 1)

                if h == 0:
                    dve.wait_ge(dve_setup, 10)
                for w in range(G):
                    i = h * G + w
                    if i >= 2:
                        dve.wait_ge(pe_patchT, i - 1)
                    dve.tensor_scalar(xni[i % 2][:].rearrange("p c (r q) -> p c r q", q=PATCH),
                                      xi[h][:].rearrange("p c (r w) -> p c r w", r=PATCH)[:, :, :, w * PATCH:(w + 1) * PATCH]
                                      .rearrange("p c (f r) q -> p (c f) r q", f=2),
                                      mvi[:, i, 0:1], rstdi[:, i:i + 1], ALU.subtract, ALU.mult).then_inc(patch_norm, 1)
                    if w >= 1:
                        y_out(i - 1)
                y_out(h * G + G - 1)
                dve.wait_ge(patch_y, G * (h + 1))
                for w in range(G):
                    last = dve.bn_stats(sty[:, w, :], yi[:, w, :])
                last.then_inc(dve_patch, 1)
                dve.wait_ge(dve_patch, 1 + 2 * h + 2)
                for w in range(G):
                    last = dve.bn_aggr(mvy[:, w, :], sty[:, w, :])
                last.then_inc(y_stats, 1)
                dve.wait_ge(pool_patch, 4 * h + 4)
                dve.wait_ge(y_stats, h + 1)
                for w in range(G):
                    last = dve.tensor_scalar(img[h][:, w, :], yi[:, w, :], mvy[:, w, 0:1], rstdy[:, w:w + 1],
                                             ALU.subtract, ALU.mult)
                last.then_inc(img_step, 1)
                dve.wait_ge(img_step, 2 * h + 1)
                dve.tensor_tensor(img[h][:], img[h][:], spread(g2_all[0:PR, :].unsqueeze(1), 1, G),
                                  ALU.mult).then_inc(img_step, 1)
                dve.wait_ge(img_step, 2 * h + 2)
                dve.tensor_tensor(img[h][:], img[h][:], posr[:].rearrange("p (w d) -> p w d", d=D),
                                  ALU.add).then_inc(img_ready, 1)
            dve.wait_ge(attn_w_in, 16 * (1 + HJ))
            for k in range(2):
                for t in range(2):
                    dve.tensor_scalar(wdup[:, k, :, t, :], wqkv[:, k, :].rearrange("p (h d) -> p h d", d=DH),
                                      QK_SCALE, None, ALU.mult).then_inc(w_ready, 1)
            dve.wait_ge(w_ready, 4)
            wflat = wdup[:].rearrange("p k (q n) t d -> p k q (n t d)", q=2)
            for k in range(2):
                dve.tensor_copy(wqk_hi[:, k], wflat[:, k]).then_inc(w_ready, 1)
            dve.wait_ge(w_ready, 6)
            for k in range(2):
                dve.tensor_tensor(wqk_lo[:, k], wflat[:, k], wqk_hi[:, k], ALU.subtract).then_inc(w_ready, 1)
            dve.wait_ge(route_w_in, 80)
            dve.wait_ge(pe_setup, 4)
            dve.tensor_copy(b1T[:], bank[6][:, 0:E * FC]).then_inc(w_ready, 1)
            dve.tensor_scalar(b2r[:], b2r[:], W_SCALE, None, ALU.mult).then_inc(w_ready, 1)
            dve.wait_ge(w_ready, 10)
            dve.tensor_copy(b2_hi[:], b2r[:]).then_inc(w_ready, 1)
            dve.wait_ge(w_ready, 11)
            dve.tensor_tensor(b2_lo[:], b2r[:], b2_hi[:], ALU.subtract).then_inc(w_ready, 1)
            dve.wait_ge(pool_setup, 1)
            dve.memset(bank[6][:, HG * S:OB * 32], 1.0).then_inc(w_ready, 1)
            dve.wait_ge(w_ready, 13)

            def take_max(f, m):
                j, images = m // 2, m % 2
                if m == 0:
                    max_rows.wait(dve, f.plus(-1))
                max_scores.wait(dve, f, m + 1)
                if images:
                    dve.tensor_reduce(mxb[:, :, 32 * j + DH], bank[7][:, 0:2 * S].rearrange("p (g n) -> p g n", g=2),
                                      AX.X, ALU.max).then_inc(max_taken.sem, 1)
                else:
                    dve.tensor_reduce(mxa[:, :, 32 * j + DH], bank[7][:, 0:HG * S].rearrange("p (g n) -> p g n", g=HG),
                                      AX.X, ALU.max).then_inc(max_taken.sem, 1)

            def step(s, l, f, m, a, p, r):
                if p.exists(B):
                    pv.wait(dve, p)
                    o_norm.wait(dve, p.plus(-1))
                    apart(dve, dve_apart)
                    dve.transpose(oT[:], bank[6][:, 0:OB * 32]).then_inc(o_norm.sem, 1)
                if m.exists(B):
                    take_max(m, 0)
                if p.exists(B):
                    o_norm.wait(dve, p, 1)
                    dve.reciprocal(recip[:], oT[:].rearrange("p (b c) -> p b c", c=32)[:, :, DH]).then_inc(o_norm.sem, 1)
                if m.exists(B):
                    take_max(m, 1)
                if p.exists(B):
                    o_norm.wait(dve, p, 2)
                    apart(dve, dve_apart)
                    dve.transpose(den[:], spread(recip[:].unsqueeze(2), 2, 32)).then_inc(o_norm.sem, 1)
                if m.exists(B):
                    take_max(m, 2)
                if p.exists(B):
                    o_norm.wait(dve, p, 3)
                    o_proj.wait(dve, p.plus(-1))
                    dve.tensor_tensor(ot[:].rearrange("p g n -> p (g n)"), bank[6][:, 0:HG * S], den[:, 0:HG * S],
                                      ALU.mult).then_inc(o_norm.sem, 1)
                if m.exists(B):
                    take_max(m, 3)
                if s.exists(B):
                    n = s.slot(XS)
                    dve.wait_ge(xi_in[n], s.of(XS) * 16 + 16)
                    dve.wait_ge(xt_in[n], s.of(XS) * 16 + 16)
                    ln_stats.wait(dve, s.plus(-1))
                    for t in range(2):
                        dve.bn_stats(st1[:, t, :], X[n][:, t, :]).then_inc(ln_stats.sem, 1)
                if r.exists(B):
                    logits.wait(dve, r)
                    onehot.wait(dve, r.plus(-1))
                    dve.tensor_tensor(lg[:], bank[1][:, LG:LG + 2 * E].rearrange("p (t e) -> p t e", t=2), bs_all[:],
                                      ALU.add).then_inc(onehot.sem, 1)
                if m.exists(B):
                    take_max(m, 4)
                if r.exists(B):
                    onehot.wait(dve, r, 1)
                    dve.tensor_reduce(lgm[:], lg[:], AX.X, ALU.max).then_inc(onehot.sem, 1)
                if s.exists(B):
                    ln_stats.wait(dve, s, 2)
                    ln_rstd.wait(dve, s.plus(-1))
                    for t in range(2):
                        apart(dve, dve_apart)
                        dve.bn_aggr(mv1[:, t, :], st1[:, t, :]).then_inc(ln_stats.sem, 1)
                if r.exists(B):
                    onehot.wait(dve, r, 2)
                    lg_exp.wait(dve, r.plus(-1))
                    dve.tensor_tensor(lgd[:], lg[:], spread(lgm[:].unsqueeze(2), 2, E), ALU.subtract).then_inc(onehot.sem, 1)
                if m.exists(B):
                    take_max(m, 5)
                if r.exists(B):
                    onehot.wait(dve, r, 3)
                    dve.scalar_tensor_tensor(out=first[:], in0=lgd[:], scalar=0.0,
                                             in1=con[:, K_FIRST:K_FIRST + 2 * E].rearrange("p (t e) -> p t e", t=2),
                                             op0=ALU.is_equal, op1=ALU.mult).then_inc(onehot.sem, 1)
                if p.exists(B):
                    c = p.slot(2)
                    o_proj.wait(dve, p)
                    x2_norm.wait(dve, p.plus(-2))
                    if p.plus(-2).exists(B):
                        dve.wait_ge(scattered[c], p.plus(-2).of(2) * 32 + 32)
                    dve.tensor_tensor(hrow[c][:, 0, 0:D], bank[1][:, 0:D], X[p.slot(XS)][:, 0, :],
                                      ALU.add).then_inc(h_sum.sem, 1)
                    dve.tensor_tensor(hrow[c][0:NIMG, 1, 0:D], bank[1][0:NIMG, D:2 * D], X[p.slot(XS)][0:NIMG, 1, :],
                                      ALU.add).then_inc(h_sum.sem, 1)
                if r.exists(B):
                    onehot.wait(dve, r, 4)
                    dve.tensor_reduce(firstm[:], first[:], AX.X, ALU.max).then_inc(onehot.sem, 1)
                if p.exists(B):
                    ln2_stats.wait(dve, p.plus(-1))
                    for t in range(2):
                        h_sum.wait(dve, p, t + 1)
                        dve.bn_stats(st2[:, t, :], hrow[c][:, t, 0:D]).then_inc(ln2_stats.sem, 1)
                if r.exists(B):
                    onehot.wait(dve, r, 5)
                    dve.tensor_tensor(oh[:], first[:], spread(firstm[:].unsqueeze(2), 2, E), ALU.is_equal).then_inc(onehot.sem, 1)
                if p.exists(B):
                    ln2_rstd.wait(dve, p.plus(-1))
                    for t in range(2):
                        ln2_stats.wait(dve, p, t + 1)
                        apart(dve, dve_apart)
                        dve.bn_aggr(mv2[:, t, :], st2[:, t, :]).then_inc(ln2_stats.sem, 1)
                if r.exists(B):
                    onehot.wait(dve, r, 6)
                    dve.tensor_tensor(ohb[:], oh[:], spread(con[:, K_VALID:K_VALID + 2].unsqueeze(2), 2, E),
                                      ALU.mult).then_inc(onehot.sem, 1)
                if l.exists(B):
                    x_hi.wait(dve, l)
                    dve.tensor_tensor(xl[l.slot(2)][:], bank[0][0:DK, 0:2 * SP].rearrange("p (k n) -> p k n", k=2),
                                      xh[l.slot(2)][:], ALU.subtract).then_inc(x_lo.sem, 1)
                if m.exists(B):
                    take_max(m, 6)
                if r.exists(B):
                    lg_exp.wait(dve, r)
                    prob.wait(dve, r.plus(-1))
                    dve.tensor_reduce(esum[:], lge[:], AX.X, ALU.add).then_inc(prob.sem, 1)
                if m.exists(B):
                    take_max(m, 7)
                if r.exists(B):
                    prob.wait(dve, r, 1)
                    dve.tensor_scalar(esum[:], esum[:], W_SCALE, None, ALU.mult).then_inc(prob.sem, 1)
                if f.exists(B):
                    k_hi.wait(dve, f)
                    sc_b.wait(dve, f.plus(-2))
                    dve.scalar_tensor_tensor(out=k1[f.slot(2)][:, :, 0:S], in0=kh[:], scalar=con[:, K_KLO:K_KLO + 1],
                                             in1=bank[2][:, 0:HG * S].rearrange("p (g n) -> p g n", g=HG),
                                             op0=ALU.mult, op1=ALU.add).then_inc(k_st1.sem, 1)
                if m.exists(B):
                    max_rows.wait(dve, m)
                    q_rest.wait(dve, m)
                    sc_b.wait(dve, m.plus(-2))
                    dve.scalar_tensor_tensor(out=q2[m.slot(2)][:], in0=qlo[:], scalar=con[:, K_K2M:K_K2M + 1],
                                             in1=bank[7][:, 0:HG * S].rearrange("p (g n) -> p g n", g=HG),
                                             op0=ALU.mult, op1=ALU.add).then_inc(q_st2.sem, 1)
                if f.exists(B):
                    q_hi.wait(dve, f)
                    q_st2.wait(dve, f.plus(-1))
                    dve.tensor_tensor(qlo[:], bank[3][:, 0:HG * S].rearrange("p (g n) -> p g n", g=HG),
                                      q1[f.slot(2)][:, :, 0:S], ALU.subtract).then_inc(q_rest.sem, 1)
                if r.exists(B):
                    ranks.wait(dve, r)
                    slots.wait(dve, r.plus(-1))
                    rk = bank[1][:, LG + 2 * E:LG + 5 * E].rearrange("p (t e) -> p t e", t=3)
                    dve.tensor_tensor(rank[:], rk[:, 0:2, :], spread(count[:].unsqueeze(1), 1, 2), ALU.add).then_inc(slots.sem, 1)
                    prob.wait(dve, r, 2)
                    dve.reciprocal(hrow[r.slot(2)][:, :, C_PROB], esum[:]).then_inc(prob.sem, 1)
                    slots.wait(dve, r, 1)
                    dve.tensor_tensor(rank[:], rank[:], ohb[:], ALU.mult).then_inc(slots.sem, 1)
                    dve.tensor_tensor(count[:], count[:], rk[:, 2, :], ALU.add).then_inc(slots.sem, 1)
                    slots.wait(dve, r, 2)
                    dve.tensor_reduce(slotf[:], rank[:], AX.X, ALU.add).then_inc(slots.sem, 1)
                    slots.wait(dve, r, 4)
                    dve.tensor_copy(slot_i[r.slot(2)][:], slotf[:]).then_inc(slots.sem, 1)

            attend_steps(dve, step)

            last_b = Turn(B - 1)
            slots.wait(dve, last_b)
            dve.tensor_scalar(pad_f[:], count[:], con[:, K_PART:K_PART + 1], None, ALU.add).then_inc(pads_i, 1)
            dve.wait_ge(pads_i, 1)
            dve.tensor_copy(pad_i[:], pad_f[:]).then_inc(pads_i, 1)
            chain = [0]

            def link(ins):
                chain[0] += 1
                ins.then_inc(list_step, 1)
                dve.wait_ge(list_step, chain[0])

            link(dve.tensor_tensor(cnt_f[:], count[0:1, :], con[0:1, K_BASE:K_BASE + E], ALU.subtract))
            link(dve.tensor_scalar(cnt_i[:], cnt_f[:], float(P - 1), None, ALU.add))
            link(dve.tensor_scalar(cnt_i[:], cnt_i[:], P.bit_length() - 1, None, ALU.logical_shift_right))
            link(dve.tensor_copy(ntile[:], cnt_i[:]))
            link(dve.tensor_scalar(skip[:], ntile[:], -float(P), float(CAP), ALU.mult, ALU.add))
            link(dve.tensor_copy(cum[:], ntile[:]))
            for e in range(1, E):
                link(dve.tensor_tensor(cum[:, e:e + 1], cum[:, e:e + 1], cum[:, e - 1:e], ALU.add))
            link(dve.memset(tl_f[:, 1, :], 0.0))
            link(dve.tensor_scalar(tl_f[:, 0, :], con[0:1, K_TILE:K_TILE + NT], float(P), None, ALU.mult))
            for e in range(E):
                link(dve.tensor_scalar(reached[:], con[0:1, K_TILE:K_TILE + NT], cum[:, e:e + 1], None, ALU.is_ge))
                link(dve.tensor_tensor(tl_f[:, 1, :], tl_f[:, 1, :], reached[:], ALU.add))
                link(dve.scalar_tensor_tensor(out=tl_f[:, 0, :], in0=reached[:], scalar=skip[:, e:e + 1],
                                              in1=tl_f[:, 0, :], op0=ALU.mult, op1=ALU.add))
            link(dve.tensor_scalar(tl_f[:, 0, :], tl_f[:, 0, :], float(E * CAP), None, ALU.min))
            link(dve.tensor_scalar(tl_f[:, 1, :], tl_f[:, 1, :], float(E - 1), None, ALU.min))
            dve.tensor_copy(tl[:], tl_f[:]).then_inc(tiles, 1)

            def normalize(n):
                s = n.slot(RS)
                dve.wait_ge(r_in[s], n.of(RS) * 16 + 16)
                e_T.wait(dve, n.plus(-2))
                dve.tensor_scalar(xe[n.slot(2)][:], R[s][:, 0:D], R[s][:, C_MEAN:C_MEAN + 1],
                                  R[s][:, C_RSTD:C_RSTD + 1], ALU.subtract, ALU.mult).then_inc(e_norm.sem, 1)

            def estep(t, h, y):
                if t.exists(NT):
                    e_hi.wait(dve, t)
                    e_h.wait(dve, t.plus(-2))
                    dve.tensor_tensor(xel[t.slot(2)][:], bank[0][0:DK, 0:2 * P].rearrange("p (k n) -> p k n", k=2),
                                      xeh[t.slot(2)][:], ALU.subtract).then_inc(e_lo.sem, 1)
                if t.plus(1).exists(NT):
                    normalize(t.plus(1))
                if h.exists(NT):
                    s = h.slot(2)
                    for c in range(2):
                        e_gelu.wait(dve, h, c + 1)
                        e_y.wait(dve, h.plus(-2))
                        m = slice(3 * c, 3 * c + 3)
                        dve.tensor_copy(hh[s][:, m, :], hf[s][:, m, :]).then_inc(e_hh.sem, 1)
                        e_hh.wait(dve, h, c + 1)
                        dve.tensor_tensor(hl[s][:, m, :], hf[s][:, m, :], hh[s][:, m, :], ALU.subtract).then_inc(e_hl.sem, 1)
                if y.exists(NT):
                    s = y.slot(RS)
                    e_y.wait(dve, y)
                    o = y.plus(-3)
                    if o.exists(NT):
                        dve.wait_ge(e_out[o.slot(RS)], o.of(RS) * 16 + 16)
                    dve.scalar_tensor_tensor(out=res[y.slot(3)][:], in0=bank[6 + y.slot(2)][:, 0:D],
                                             scalar=R[s][:, C_PROB:C_PROB + 1], in1=R[s][:, 0:D],
                                             op0=ALU.mult, op1=ALU.add).then_inc(e_res.sem, 1)

            normalize(Turn(0))
            expert_steps(dve, estep)

        @block.tensor
        def _(pe):
            pe.wait_ge(con_in, 16)
            pe.wait_ge(patch_w_in, 16 * (8 + IH))
            n = 0
            for f2 in range(2):
                for c in range(C):
                    last = pe.matmul(bank[7][:, 0:D], spread(b1v[:, f2, c:c + 1], 1, P), wl[:, f2, c, :],
                                     start=(n == 0), stop=(n == 2 * C - 1))
                    n += 1
            last.then_inc(pe_setup, 1)
            pe.wait_ge(dve_setup, 4)
            for t in range(2):
                last = pe.transpose(bank[6][0:32, t * NAT:(t + 1) * NAT], cfg2[:, t, :], ident[0:NAT, 0:NAT])
            last.then_inc(pe_setup, 1)
            pe.wait_ge(dve_setup, 11)
            pe.transpose(bank[6][:, 256:256 + B], txt_f[:], ident[0:B, 0:B])
            for t in range(2):
                last = pe.matmul(bank[7][0:NAT, 0:D], cfgT[0:NCFG, t, :], emb[:, t, :], start=(t == 0), stop=(t == 1))
            last.then_inc(pe_setup, 1)
            def patch_transpose(i):
                pe.wait_ge(patch_norm, i + 1)
                if i >= 2:
                    pe.wait_ge(act_patchT, i - 1)
                for c in range(2 * C):
                    last = pe.transpose(bank[2 * (i % 2) + c // 3][:, (c % 3) * PR:(c % 3 + 1) * PR], xni[i % 2][:, c, :],
                                        ident[0:PR, 0:PR])
                last.then_inc(pe_patchT, 1)

            def patch_embed(k):
                pe.wait_ge(act_patchT, k + 1)
                if k >= 2:
                    pe.wait_ge(patch_y, k - 1)
                for c in range(2 * C):
                    last = pe.matmul(bank[4 + k % 2][0:PR, 0:D], xTi[k % 2][:, c, :], wlg[:, c % 2, c // 2, :],
                                     start=(c == 0), stop=(c == 2 * C - 1))
                last.then_inc(pe_patchY, 1)

            pe.wait_ge(dve_setup, 5)
            for h in range(2):
                patch_transpose(h * G)
                for w in range(1, G):
                    patch_transpose(h * G + w)
                    patch_embed(h * G + w - 1)
                patch_embed(h * G + G - 1)
            pe.wait_ge(route_w_in, 80)
            pe.wait_ge(dve_setup, 13)
            pe.transpose(bank[6][:, 0:E * FC], b1r[:], ident[0:E * FC, 0:E * FC]).then_inc(pe_setup, 1)
            pe.wait_ge(w_ready, 12)
            pe.wait_ge(attn_w_in, 16 * (1 + HJ))

            def project(dst, which, f):
                s = f.slot(2)
                for g in range(HG):
                    cols = slice(g * P, (g + 1) * P)
                    n = 0
                    for k in range(2):
                        for w, v in ((wqk_hi, xh), (wqk_lo, xh), (wqk_hi, xl)):
                            last = pe.matmul(dst[:, g * S:(g + 1) * S], w[:, k, which, cols], v[s][:, k, 0:S],
                                             start=(n == 0), stop=(n == 5))
                            n += 1
                return last

            def project_values(f):
                s = f.slot(2)
                wv_hi = wqk_hi[:].rearrange("p k q (h t d) -> p k q h t d", h=H, t=2)
                wv_lo = wqk_lo[:].rearrange("p k q (h t d) -> p k q h t d", h=H, t=2)
                for c0, c1, r0, r1, h0, h1, o in ((0, TXT, 0, P, 0, H, 0), (TXT, SP, 0, 64, 0, H, D),
                                                  (TXT, SP, 64, P, HJ, 2 * HJ, D)):
                    n = 0
                    for k in range(2):
                        for w, v in ((wv_hi, xh), (wv_lo, xh), (wv_hi, xl)):
                            last = pe.matmul(bank[2][r0:r1, o + h0 * DH:o + h1 * DH].rearrange("p (h d) -> p h d", d=DH),
                                             v[s][:, k, c0:c1], w[:, k, 1, h0:h1, 0, :], start=(n == 0), stop=(n == 5))
                            n += 1
                return last

            quarters = ((0, 0, 0), (64, 0, 1), (0, 1, 2), (64, 1, 2))

            def max_part(f, m):
                j, images = m // 2, m % 2
                s, rows = f.slot(2), slice(32 * (m // 2), 32 * (m // 2) + 32)
                if m == 0:
                    q_st2.wait(pe, f.plus(-1))
                    k_st1.wait(pe, f)
                    q_hi.wait(pe, f)
                else:
                    max_taken.wait(pe, f, m)
                if images:
                    for r, c, g in quarters:
                        last = pe.matmul(bank[7][r:r + 64, c * S:(c + 1) * S], q1[s][rows, g, TXT:SP], k1[s][rows, g, 0:S],
                                         start=True, stop=True)
                else:
                    for g in range(HG):
                        last = pe.matmul(bank[7][:, g * S:(g + 1) * S], q1[s][rows, g, 0:TXT], k1[s][rows, g, 0:S],
                                         start=True, stop=True)
                last.then_inc(max_scores.sem, 1)

            def scores(a, j):
                s, rows = a.slot(2), slice(32 * j, 32 * j + 32)
                if j == 0:
                    q_st2.wait(pe, a)
                    k_st2.wait(pe, a)
                    exp_a.wait(pe, a.plus(-1))
                else:
                    exp_a.wait(pe, a, j)
                for g in range(HG):
                    for n, (kk, qq) in enumerate(((k1, q1), (k2, q2))):
                        last = pe.matmul(bank[4][:, g * S:(g + 1) * S], kk[s][rows, g, 0:TXT], qq[s][rows, g, 0:S],
                                         start=(n == 0), stop=(n == 1))
                last.then_inc(sc_a.sem, 1)
                if j == 0:
                    exp_b.wait(pe, a.plus(-1))
                else:
                    exp_b.wait(pe, a, j)
                for r, c, g in quarters:
                    for n, (kk, qq) in enumerate(((k1, q1), (k2, q2))):
                        last = pe.matmul(bank[5][r:r + 64, c * S:(c + 1) * S], kk[s][rows, g, TXT:SP], qq[s][rows, g, 0:S],
                                         start=(n == 0), stop=(n == 1))
                last.then_inc(sc_b.sem, 1)

            def weigh(a):
                s = a.slot(2)
                v_out.wait(pe, a)
                o_norm.wait(pe, a.plus(-1))
                exp_a.wait(pe, a)
                exp_b.wait(pe, a)
                for g in range(HG):
                    c = quarters[g][1]
                    for t, (w, cols) in enumerate(((pa, g), (pb, c))):
                        for j in range(HJ):
                            last = pe.matmul(bank[6][32 * j:32 * j + 32, g * S:(g + 1) * S], V[s][:, t, HJ * g + j, :],
                                             w[j][:, cols * S:(cols + 1) * S], start=(t == 0), stop=(t == 1))
                last.then_inc(pv.sem, 1)

            def transpose_rows(rows):
                for k in range(2):
                    for t, (c0, c1) in enumerate(((0, TXT), (TXT, SP))):
                        last = pe.transpose(bank[0][0:DK, k * SP + c0:k * SP + c1], rows[0:c1 - c0, t, k * DK:(k + 1) * DK],
                                            ident[0:c1 - c0, 0:c1 - c0])
                return last

            def step(s, l, f, m, a, p, r):
                if m.exists(B):
                    max_part(m, 0)
                if a.exists(B):
                    scores(a, 0)
                if m.exists(B):
                    max_part(m, 1)
                if r.exists(B):
                    x2_norm.wait(pe, r)
                    if l.plus(-1).exists(B):
                        x_lo.wait(pe, l.plus(-1))
                    x2_out.wait(pe, r.plus(-1))
                    transpose_rows(xn2).then_inc(x2_T.sem, 1)
                if m.exists(B):
                    max_part(m, 2)
                if a.exists(B):
                    scores(a, 1)
                if m.exists(B):
                    max_part(m, 3)
                if r.exists(B):
                    x2_out.wait(pe, r)
                    slots.wait(pe, r.plus(-1))
                    h_sum.wait(pe, r)
                    for t in range(2):
                        for k in range(2):
                            last = pe.matmul(bank[1][:, LG + t * E:LG + (t + 1) * E], xT2[:, k, t * P:(t + 1) * P],
                                             ws[:, k, :], start=(k == 0), stop=(k == 1))
                    last.then_inc(logits.sem, 1)
                if m.exists(B):
                    max_part(m, 4)
                if a.exists(B):
                    scores(a, 2)
                if m.exists(B):
                    max_part(m, 5)
                if p.exists(B):
                    o_norm.wait(pe, p)
                    onehot.wait(pe, r, 1)
                    for rows, c0, c1, o in ((P, 0, TXT, 0), (NIMG, TXT, S, D)):
                        for g in range(HG):
                            last = pe.matmul(bank[1][0:rows, o:o + D], ot[:, g, c0:c1], wo[:, g, :],
                                             start=(g == 0), stop=(g == HG - 1))
                    last.then_inc(o_proj.sem, 1)
                if l.exists(B):
                    x_norm.wait(pe, l)
                    x_lo.wait(pe, l.plus(-1))
                    x2_out.wait(pe, r)
                    transpose_rows(xn).then_inc(x_T.sem, 1)
                if m.exists(B):
                    max_part(m, 6)
                if a.exists(B):
                    scores(a, 3)
                if m.exists(B):
                    max_part(m, 7)
                if f.exists(B):
                    x_lo.wait(pe, f)
                    v_out.wait(pe, f.plus(-1))
                    project(bank[2], 1, f).then_inc(k_proj.sem, 1)
                if m.exists(B):
                    max_taken.wait(pe, m)
                    for g in range(HG):
                        e, c, _ = quarters[g]
                        pe.matmul(bank[7][:, g * S:g * S + TXT], mxa[:, g, :], neg_id[:], start=True, stop=True)
                        last = pe.matmul(bank[7][:, g * S + TXT:(g + 1) * S], mxb[:, c, :], neg_id[:, e:e + NIMG],
                                         start=True, stop=True)
                    last.then_inc(max_rows.sem, 1)
                if f.exists(B):
                    q_rest.wait(pe, f.plus(-1))
                    project(bank[3], 0, f).then_inc(q_proj.sem, 1)
                if r.exists(B):
                    onehot.wait(pe, r)
                    if p.exists(B):
                        h_sum.wait(pe, p)
                    o = LG + 2 * E
                    pe.matmul(bank[1][:, o:o + E], tri[:], ohb[:, 0, :], start=True, stop=True)
                    pe.matmul(bank[1][:, o + E:o + 2 * E], tri[:], ohb[:, 1, :], start=True, stop=False)
                    pe.matmul(bank[1][:, o + E:o + 2 * E], ones[:], ohb[:, 0, :], start=False, stop=True)
                    pe.matmul(bank[1][:, o + 2 * E:o + 3 * E], ones[:], ohb[:, 0, :], start=True, stop=False)
                    pe.matmul(bank[1][:, o + 2 * E:o + 3 * E], ones[:], ohb[:, 1, :], start=False, stop=True)\
                        .then_inc(ranks.sem, 1)
                if a.exists(B):
                    weigh(a)
                if f.exists(B):
                    k_st1.wait(pe, f)
                    project_values(f).then_inc(v_proj.sem, 1)

            attend_steps(pe, step)
            w_split.wait(pe, Turn(B // 2 - 1))
            pe.wait_ge(tiles, 1)
            slots.wait(pe, Turn(B - 1))
            o_norm.wait(pe, Turn(B - 1))

            def expert_of(t):
                return pe.value_load(tl[0:1, 1, bass.ds(t.lin(1), 1)] if t.r is not None
                                     else tl[0:1, 1, t.c:t.c + 1], min_val=0, max_val=E - 1)

            def estep(t, h, y):
                if t.exists(NT):
                    e_norm.wait(pe, t)
                    e_lo.wait(pe, t.plus(-1))
                    for k in range(2):
                        last = pe.transpose(bank[0][0:DK, k * P:(k + 1) * P], xe[t.slot(2)][:, k * DK:(k + 1) * DK], ident)
                    last.then_inc(e_T.sem, 1)
                if h.exists(NT):
                    s = h.slot(2)
                    e_lo.wait(pe, h)
                    ex = expert_of(h)
                    e_gelu.wait(pe, h.plus(-2))
                    for fc in range(FC):
                        n = 0
                        for k in range(2):
                            cols = bass.ds(ex * (2 * F) + (k * F + fc * P), P)
                            for w, v in ((w1_hi, xeh), (w1_lo, xeh), (w1_hi, xel)):
                                last = pe.matmul(bank[2 + 2 * s + fc // 3][:, fc % 3 * P:(fc % 3 + 1) * P], w[:, cols],
                                                 v[s][:, k, :], start=(n == 0), stop=(n == 5))
                                n += 1
                        if fc % 3 == 2:
                            last.then_inc(e_h.sem, 1)
                if y.exists(NT):
                    s = y.slot(2)
                    ex = expert_of(y)
                    e_res.wait(pe, y.plus(-2))
                    dst = bank[6 + s][:, 0:D]
                    row = bass.ds(ex * D, D)
                    pe.matmul(dst, one16[:], b2_hi[:, row], start=True, stop=False)
                    pe.matmul(dst, one16[:], b2_lo[:, row], start=False, stop=False)
                    for fc in range(FC):
                        if fc % 3 == 0:
                            e_hl.wait(pe, y, fc // 3 + 1)
                        cols = bass.ds(ex * (FC * D) + fc * D, D)
                        for n, (v, w) in enumerate(((hh, w2_hi), (hh, w2_lo), (hl, w2_hi))):
                            last = pe.matmul(dst, v[s][:, fc, :], w[:, cols], start=False,
                                             stop=(fc == FC - 1 and n == 2))
                    last.then_inc(e_y.sem, 1)

            expert_steps(pe, estep)


_INS = ["x", "x_txt", "L0_tok_ln1_g", "L0_tok_ln1_b", "L0_tok_W_lin", "L0_tok_b_lin", "L0_tok_ln2_g", "L0_tok_ln2_b",
        "L0_tok_pos_embedding", "L0_tok_cls_token", "L0_txt_atom_configs", "L0_txt_subshell_embeds",
        "L0_txt_occupancy_embeds", "L0_attn_w_qkv", "L0_attn_w_out", "L0_ffn_Ws", "L0_ffn_bs", "L0_ffn_W1", "L0_ffn_b1",
        "L0_ffn_W2", "L0_ffn_b2"]


def kernel(**inputs):
    import concourse.bacc as _bacc
    from concourse.bass_utils import run_bass_kernel_spmd as _run

    nc = _bacc.Bacc("TRN2", target_bir_lowering=False, num_devices=1)
    arrays, args = {}, []
    for name in _INS:
        a = np.ascontiguousarray(inputs[name])
        arrays[f"in_{name}"] = a
        args.append(nc.dram_tensor(f"in_{name}", a.shape, mybir.dt.from_np(a.dtype), kind="ExternalInput").ap())
    arrays["consts"] = shape_constants()
    args.append(nc.dram_tensor("consts", arrays["consts"].shape, F32, kind="ExternalInput").ap())
    args.append(nc.dram_tensor("out", (T, D), F32, kind="ExternalOutput").ap())
    build(nc, *args)
    r = _run(nc, [arrays], core_ids=[0])
    return r.results[0]["out"].reshape(B, S, D)
```

```python
from contextlib import ExitStack

import numpy as np

import concourse.bass as bass
from concourse import mybir

F32 = mybir.dt.float32
F16 = mybir.dt.float16
U8 = mybir.dt.uint8
BF16 = mybir.dt.bfloat16
I32 = mybir.dt.int32
ALU = mybir.AluOpType
ACT = mybir.ActivationFunctionType
AX = mybir.AxisListType

P = 128
B, C, IMG, PATCH = 32, 3, 96, 16
G = IMG // PATCH
NPATCH = G * G
NIMG = NPATCH + 1
TXT = 128
S = NIMG + TXT
SP = TXT + 64
D = 192
DK = D // 2
H, DH = 12, 16
HG, HJ = 3, 4
NAT, NCFG = 119, 28
E, F = 8, 768
FC = F // P
T = B * S
OB = -(-HG * S // 32)
CAP = (T + P + 31) // 32 * 32
ROW = 196
C_MEAN, C_RSTD, C_PROB, C_ID = 192, 193, 194, 195
RS = 6
NT = T // P + E
NW = NT // RS + 1
WB = (E - 1).bit_length()
EPS = 1e-5
QK_SCALE = 8.0
MAX_SCALE = 16.0
W_SCALE = 64.0
XS = 8
LG = 2 * D
PAD_ID = 1 << 20

K_ID, K_TRI, K_KLO, K_K2M, K_K2A, K_VALID, K_IDS, K_BASE, K_FIRST, K_TILE, K_PART, K_PADID, K_HALF = (
    0, 128, 256, 257, 258, 259, 261, 263, 271, 287, 287 + NT, 288 + NT, 289 + NT)
K_END = 291 + NT


def shape_constants():
    k = np.zeros((P, K_END), np.float32)
    p = np.arange(P)
    r = p % 32
    k[:, K_ID:K_ID + P] = np.eye(P)
    k[:, K_TRI:K_TRI + P] = p[:, None] < p[None, :]
    k[:, K_KLO] = -(r >= DH).astype(np.float32)
    k[:, K_K2M] = r < DH
    k[:, K_K2A] = MAX_SCALE * (r == DH)
    k[:, K_VALID] = 1
    k[:, K_VALID + 1] = p < NIMG
    k[:, K_IDS] = NIMG + p
    k[:, K_IDS + 1] = p
    k[:, K_BASE:K_BASE + E] = CAP * np.arange(E)
    k[:, K_FIRST:K_FIRST + 2 * E] = np.tile(E - np.arange(E), 2)
    k[:, K_TILE:K_TILE + NT] = np.arange(NT)
    k[:, K_PART] = p
    k[:, K_PADID] = PAD_ID
    k[:, K_HALF] = p < NIMG
    k[:, K_HALF + 1] = (p >= 64) & (p < 64 + NIMG)
    return k


def spread(ap, axis, n):
    shape = list(ap.shape)
    shape[axis] = n
    return ap.broadcast_to(shape)


class Turn:

    def __init__(self, c, r=None, n=1):
        self.c, self.r, self.n = c, r, n

    def plus(self, d):
        return Turn(self.c + d, self.r, self.n)

    def lin(self, a, k=0):
        return a * self.c + k if self.r is None else self.r * (a * self.n) + (a * self.c + k)

    def of(self, m):
        return self.c // m if self.r is None else self.r * (self.n // m) + self.c // m

    def slot(self, m):
        return self.c % m

    def exists(self, count):
        return self.r is not None or 0 <= self.c < count


class Event:

    def __init__(self, sem, per=1):
        self.sem, self.per = sem, per

    def wait(self, eng, item, k=None):
        if item.r is None and item.c < 0:
            return
        eng.wait_ge(self.sem, item.lin(self.per, self.per if k is None else k))


def build(nc, x, x_txt, ln1_g, ln1_b, W_lin, b_lin, ln2_g, ln2_b, pos, cls_tok, cfg, sub_e, occ_e,
          w_qkv, w_out, Ws, bs, W1, b1, W2, b2, consts, out):
    ctx = ExitStack()
    with ctx:
        def sb(name, shape, dt=F32):
            return ctx.enter_context(nc.sbuf_tensor(name, shape, dt))

        def sem(name):
            return ctx.enter_context(nc.semaphore(name))

        def ev(name, per=1):
            return Event(sem(name), per)

        bank = [ctx.enter_context(nc.psum_tensor(f"bank{i}", [P, 512], F32)) for i in range(8)]

        himg = nc.dram_tensor("himg", (B, NIMG, D), F32, kind="Internal").ap()
        atoms = nc.dram_tensor("atoms", (NAT, D), F32, kind="Internal").ap()
        routed = nc.dram_tensor("routed", (E * CAP + P, ROW), F32, kind="Internal").ap()

        con = sb("con", [P, K_END])
        neg_id = sb("neg_id", [P, P], BF16)
        tri = sb("tri", [P, P], BF16)
        ones = sb("ones", [P, P], BF16)
        one16 = sb("one16", [1, P], F16)
        halfs = sb("halfs", [P, 2 * G])
        ident = con[:, K_ID:K_ID + P]
        wqk_hi = sb("wqk_hi", [DK, 2, 2, HG * P], F16)
        wqk_lo = sb("wqk_lo", [DK, 2, 2, HG * P], F16)
        wo = sb("wo", [P, HG, D])
        wo_hi = sb("wo_hi", [P, HG, D], F16)
        wo_lo = sb("wo_lo", [P, HG, D], F16)
        ws = sb("ws", [DK, 2, E])
        ws_hi = sb("ws_hi", [DK, 2, E], F16)
        ws_lo = sb("ws_lo", [DK, 2, E], F16)
        bs_all = sb("bs_all", [P, 2, E])
        w2_hi = sb("w2_hi", [P, E * FC * D], F16)
        w2_lo = sb("w2_lo", [P, E * FC * D], F16)
        b1T = sb("b1T", [P, E * FC])
        b2_hi = sb("b2_hi", [1, E * D], F16)
        b2_lo = sb("b2_lo", [1, E * D], F16)
        wstage1 = sb("wstage1", [DK, F])
        wstage2 = sb("wstage2", [P, 3 * D])

        X = [sb(f"x{i}", [P, 2, D]) for i in range(XS)]
        txt_i = sb("txt_i", [P, B + 1], I32)
        txt_now = [sb(f"txt_now{i}", [P, 1], I32) for i in range(2)]
        padrow = sb("padrow", [P, ROW])
        st1 = sb("st1", [P, 2, 6])
        mv1 = sb("mv1", [P, 2, 2])
        var1 = sb("var1", [P, 2])
        rstd1 = sb("rstd1", [P, 2])
        neg1 = sb("neg1", [P, 2])
        shift1 = sb("shift1", [P, 2])
        xn = sb("xn", [P, 2, D])
        xh = [sb(f"xh{i}", [DK, 2, SP], F16) for i in range(2)]
        xl = [sb(f"xl{i}", [DK, 2, SP], F16) for i in range(2)]
        kh = sb("kh", [P, HG, S], F16)
        k1 = [sb(f"k1_{i}", [P, HG, SP], F16) for i in range(2)]
        k2 = [sb(f"k2_{i}", [P, HG, SP], F16) for i in range(2)]
        q1 = [sb(f"q1_{i}", [P, HG, SP], F16) for i in range(2)]
        qlo = [sb(f"qlo{i}", [P, HG, S], F16) for i in range(2)]
        V = [sb(f"v{i}", [P, 2, H, 32]) for i in range(2)]
        mxa = sb("mxa", [P, HG, P], BF16)
        mxb = sb("mxb", [P, 2, P], BF16)
        recip = sb("recip", [P, OB])
        hrow = [sb(f"hrow{i}", [P, 2, ROW]) for i in range(2)]
        st2 = sb("st2", [P, 2, 6])
        mv2 = sb("mv2", [P, 2, 2])
        var2 = sb("var2", [P, 2])
        neg2 = sb("neg2", [P, 2])
        shift2 = sb("shift2", [P, 2])
        xn2 = sb("xn2", [P, 2, D])
        x2h = sb("x2h", [DK, 2, 2 * P], F16)
        x2l = sb("x2l", [DK, 2, 2 * P], F16)
        lg = sb("lg", [P, 2, E])
        lgm = sb("lgm", [P, 2])
        lgd = sb("lgd", [P, 2, E])
        lge = sb("lge", [P, 2, E])
        esum = sb("esum", [P, 2])
        first = sb("first", [P, 2, E])
        firstm = sb("firstm", [P, 2])
        oh = sb("oh", [P, 2, E])
        ohb = sb("ohb", [P, 2, E], BF16)
        count = sb("count", [P, E])
        rank = sb("rank", [P, 2, E])
        slotf = sb("slotf", [P, 2])
        slot_i = [sb(f"slot_i{i}", [P, 2], I32) for i in range(2)]
        ids = sb("ids", [P, 2])

        embed_ctx = ExitStack()

        def sbe(name, shape, dt=F32):
            return embed_ctx.enter_context(nc.sbuf_tensor(name, shape, dt))

        IH = B // 2
        PR = IH * G
        xi = [sbe(f"xi{i}", [PR, C, PATCH * IMG]) for i in range(2)]
        sti = sbe("sti", [PR, 2 * G, C, 6])
        mvi = sbe("mvi", [PR, 2 * G, 2])
        vari = sbe("vari", [PR, 2 * G])
        rstdi = sbe("rstdi", [PR, 2 * G])
        xni = [sbe(f"xni{i}", [PR, C * 2, P]) for i in range(2)]
        xTi = [sbe(f"xTi{i}", [P, C * 2, PR]) for i in range(2)]
        wl = sbe("wl", [P, 2, C, D])
        wlg = sbe("wlg", [P, 2, C, D])
        g1 = sbe("g1", [P, 2, C])
        b1v = sbe("b1v", [P, 2, C])
        bl_all = sbe("bl_all", [P, D])
        bias_all = sbe("bias_all", [P, D])
        g2_all = sbe("g2_all", [P, D])
        b2_all = sbe("b2_all", [P, D])
        posr = sbe("posr", [PR, G * D])
        clsr = sbe("clsr", [B, D])
        posc = sbe("posc", [B, D])
        yi = [sbe(f"yi{i}", [PR, G, D]) for i in range(2)]
        sty = sbe("sty", [PR, G, 6])
        mvy = sbe("mvy", [PR, G, 2])
        vary = sbe("vary", [PR, G])
        rstdy = sbe("rstdy", [PR, G])
        img = [sbe(f"img{i}", [PR, G, D]) for i in range(2)]
        cfg_s = sbe("cfg_s", [NAT, NCFG])
        cfg2 = sbe("cfg2", [NAT, 2, 32])
        cfgT = sbe("cfgT", [32, 2, NAT])
        emb = sbe("emb", [NCFG, 2, D])
        tab = sbe("tab", [NAT, D])

        wqkv = sbe("wqkv", [DK, 2, 2 * D])
        wdup = sbe("wdup", [DK, 2, 2 * H, 2, DH])
        b1r = sbe("b1r", [E * FC, P])
        b2r = sbe("b2r", [1, E * D])
        txt = sbe("txt", [B, P], I32)
        txt_f = sbe("txt_f", [B, P])
        txt_neg = sbe("txt_neg", [B, P])
        embed_ctx.close()

        pa = [sb(f"pa{j}", [P, HG * S]) for j in range(HJ)]
        pb = [sb(f"pb{j}", [P, 2 * S]) for j in range(HJ)]
        ot = sb("ot", [P, HG, S])
        oth = sb("oth", [P, HG, S], F16)
        otl = sb("otl", [P, HG, S], F16)
        q2 = [sb(f"q2_{i}", [P, HG, S], F16) for i in range(2)]
        oT = sb("oT", [P, OB * 32])
        den = sb("den", [P, OB * 32])

        w1_hi = sb("w1_hi", [DK, E * 2 * F], F16)
        w1_lo = sb("w1_lo", [DK, E * 2 * F], F16)
        pad_i = sb("pad_i", [1, E], I32)
        cnt_f = sb("cnt_f", [1, E])
        cnt_i = sb("cnt_i", [1, E], I32)
        ntile = sb("ntile", [1, E])
        cum = sb("cum", [1, 4, E])
        skip = sb("skip", [1, E])
        reached = sb("reached", [1, NT, E])
        tl_f = sb("tl_f", [1, 2, NT])
        tl = sb("tl", [1, NT], I32)
        queue = sb("queue", [1, NW + 1, RS])
        words_f = sb("words_f", [1, NW])
        words = sb("words", [1, NW], I32)
        R = [sb(f"r{i}", [P, ROW]) for i in range(RS)]
        xe = [sb(f"xe{i}", [P, D]) for i in range(2)]
        xeh = [sb(f"xeh{i}", [DK, 2, P], F16) for i in range(2)]
        xel = [sb(f"xel{i}", [DK, 2, P], F16) for i in range(2)]
        hf = [sb(f"hf{i}", [P, FC, P]) for i in range(2)]
        hh = [sb(f"hh{i}", [P, FC, P], F16) for i in range(2)]
        hl = [sb(f"hl{i}", [P, FC, P], F16) for i in range(2)]
        res = [sb(f"res{i}", [P, D]) for i in range(3)]

        con_in = sem("con_in")
        qkv_in = sem("qkv_in")
        patch_w_in = sem("patch_w_in")
        image_in = [sem(f"image_in{i}") for i in range(2)]
        atom_in = sem("atom_in")
        place_in = sem("place_in")
        wo_in = sem("wo_in")
        route_w_in = sem("route_w_in")
        atoms_out = sem("atoms_out")
        himg_out = [sem(f"himg_out{i}") for i in range(2)]
        pool_zeroed = sem("pool_zeroed")
        pool_setup = sem("pool_setup")
        const_ready = sem("const_ready")
        cfg_ready = sem("cfg_ready")
        idx_step = sem("idx_step")
        patch_w_ready = sem("patch_w_ready")
        cls_ready = sem("cls_ready")
        pos_ready = sem("pos_ready")
        pe_bias, bias_ready = sem("pe_bias"), sem("bias_ready")
        pe_cfgT, cfgT_ready = sem("pe_cfgT"), sem("cfgT_ready")
        pe_table, table_ready = sem("pe_table"), sem("table_ready")
        pe_b1T, late_ready = sem("pe_b1T"), sem("late_ready")
        b2_round, b2_split = sem("b2_round"), sem("b2_split")
        patch_bn = sem("patch_bn")
        patch_stats = sem("patch_stats")
        patch_rstd = sem("patch_rstd")
        patch_norm = sem("patch_norm")
        pe_patchT = sem("pe_patchT")
        act_patchT = sem("act_patchT")
        pe_patchY = sem("pe_patchY")
        patch_y = sem("patch_y")
        y_bn = sem("y_bn")
        y_stats = sem("y_stats")
        y_rstd = sem("y_rstd")
        y_mid = sem("y_mid")
        y_scaled = sem("y_scaled")
        img_ready = sem("img_ready")
        w_ready = sem("w_ready")
        list_step = sem("list_step")
        pool_apart, dve_apart = sem("pool_apart"), sem("dve_apart")

        xi_in = [sem(f"xi_in{i}") for i in range(XS)]
        xt_in = [sem(f"xt_in{i}") for i in range(XS)]
        w1_in, w2_in = ev("w1_in", 16), ev("w2_in", 16)
        w1_scaled, w2_scaled = ev("w1_scaled", 2), ev("w2_scaled", 2)
        w1_split, w2_split = ev("w1_split"), ev("w2_split")
        ln_stats = ev("ln_stats", 4)
        ln_rstd = ev("ln_rstd", 4)
        x_norm = ev("x_norm")
        x_T = ev("x_T")
        x_hi = ev("x_hi")
        x_lo = ev("x_lo")
        k_proj, q_proj, v_proj = ev("k_proj"), ev("q_proj"), ev("v_proj")
        k_hi, q_hi, v_out = ev("k_hi"), ev("q_hi"), ev("v_out")
        k_st1, k_st2, q_rest, q_st2 = ev("k_st1"), ev("k_st2"), ev("q_rest"), ev("q_st2")
        max_scores = ev("max_scores", 8)
        max_taken = ev("max_taken", 8)
        max_rows = ev("max_rows")
        sc_a, sc_b = ev("sc_a", 4), ev("sc_b", 4)
        exp_a, exp_b = ev("exp_a", 4), ev("exp_b", 4)
        pv = ev("pv")
        o_norm = ev("o_norm", 4)
        o_hi, o_lo = ev("o_hi"), ev("o_lo")
        o_proj = ev("o_proj")
        h_sum = ev("h_sum", 2)
        ln2_stats = ev("ln2_stats", 4)
        ln2_rstd = ev("ln2_rstd", 5)
        x2_norm = ev("x2_norm")
        x2_T = ev("x2_T")
        x2_hi, x2_lo = ev("x2_hi"), ev("x2_lo")
        logits = ev("logits")
        onehot = ev("onehot", 7)
        lg_exp = ev("lg_exp")
        prob = ev("prob", 3)
        ranks = ev("ranks")
        slots = ev("slots", 5)
        id_put = ev("id_put", 2)
        idx_put = ev("idx_put")
        scattered = [sem(f"scattered{i}") for i in range(2)]

        pads_i = sem("pads_i")
        pads_out = [sem(f"pads_out{i}") for i in range(3)]
        words_ready = sem("words_ready")
        tiles = sem("tiles")
        r_in = [sem(f"r_in{i}") for i in range(RS)]
        e_norm, e_T, e_hi, e_lo = ev("e_norm"), ev("e_T"), ev("e_hi"), ev("e_lo")
        e_h = ev("e_h", 2)
        e_gelu = ev("e_gelu", 2)
        e_hh = ev("e_hh", 2)
        e_hl = ev("e_hl", 2)
        e_y = ev("e_y")
        e_res = ev("e_res")
        e_out = [sem(f"e_out{i}") for i in range(RS)]

        w1_pieces = W1.rearrange("e (k p) f -> (e k) p f", k=2)
        w2_pieces = W2.rearrange("e (c p) d -> p (e c) d", p=P)

        HEAD, TAIL, UN = XS, 6, XS

        def apart(eng, mark):
            eng.sem_inc(mark, 1)

        def attend_steps(eng, step, embed_tail=None):
            def at(i):
                step(*(i.plus(-d) for d in range(TAIL + 1)))
            for i in range(HEAD):
                at(Turn(i))
                if embed_tail:
                    embed_tail(i)
            with eng.Fori(HEAD // UN, B // UN) as r:
                for u in range(UN):
                    at(Turn(u, r, UN))
            for i in range(B, B + TAIL):
                at(Turn(i))

        def expert_steps(eng, step):
            def at(i):
                step(i, i.plus(-1), i.plus(-2))
            for i in range(RS):
                at(Turn(i))
            with eng.Fori(1, NT // RS) as r:
                for u in range(RS):
                    at(Turn(u, r, RS))
            for i in range(NT // RS * RS, NT + 2):
                at(Turn(i))

        def expert_reader(eng):
            known = {}

            def expert_of(t, item):
                word = t.c // RS, t.r is None
                if word not in known:
                    known[word] = eng.value_load(words[0:1, t.c // RS:t.c // RS + 1] if t.r is None
                                                 else words[0:1, bass.ds(t.of(RS), 1)],
                                                 min_val=0, max_val=(1 << (WB * (RS + 1))) - 1)
                u = item.c - t.c // RS * RS + 2
                if (word, u) not in known:
                    known[word, u] = (known[word] >> (WB * u)) & (E - 1)
                return known[word, u]

            return expert_of

        def pad_tiles(eng, half):
            eng.wait_ge(pads_i, 1)
            eng.wait_ge(pool_setup, 1)
            for e in range(half * E // 2, (half + 1) * E // 2):
                row = eng.value_load(pad_i[0:1, e:e + 1], min_val=0, max_val=E * CAP - P)
                eng.dma_start(routed[bass.ds(row, P), :], padrow[:]).then_inc(pads_out[half], 16)

        def weight_piece(s):
            w = Turn(s.c // 2, s.r, s.n // 2)
            if s.r is None:
                return w, slice(w.c * F, w.c * F + F), slice(w.c * 3 * D, (w.c + 1) * 3 * D)
            return w, bass.ds(w.lin(F), F), bass.ds(w.lin(3 * D), 3 * D)

        block = ctx.enter_context(nc.Block())

        @block.sync
        def _(sp):
            sp.dma_start(con[:], consts).then_inc(con_in, 16)
            sp.dma_start(wqkv[:], w_qkv.rearrange("(k p) n -> p k n", k=2)[:, :, 0:2 * D]).then_inc(qkv_in, 16)
            for h in range(2):
                for c in range(C):
                    sp.dma_start(xi[h][:, c, :], x[h * IH:(h + 1) * IH, c].rearrange("i (n r) w -> i n (r w)", n=G))\
                        .then_inc(image_in[h], 16)
            sp.wait_ge(pool_zeroed, 1)
            for j in range(HJ):
                sp.dma_start(wo[32 * j:32 * j + DH, :, :],
                             w_out.rearrange("(g j r) d -> j r g d", g=HG, j=HJ)[j]).then_inc(wo_in, 16)
            sp.dma_start(ws[:], Ws.rearrange("(k p) e -> p k e", k=2)).then_inc(route_w_in, 16)
            for t in range(2):
                sp.dma_start(bs_all[:, t, :], spread(bs.rearrange("(a e) -> a e", a=1), 0, P)).then_inc(route_w_in, 16)
            sp.dma_start(b1r[:], b1.rearrange("e (c p) -> (e c) p", p=P)).then_inc(route_w_in, 16)
            sp.dma_start(b2r[:], b2.rearrange("(a e) d -> a (e d)", a=1)).then_inc(route_w_in, 16)
            sp.wait_ge(table_ready, 1)
            sp.dma_start(atoms, tab[:]).then_inc(atoms_out, 16)
            sp.wait_ge(cls_ready, 1)
            sp.dma_start(himg[:, 0, :], clsr[:]).then_inc(himg_out[0], 16)

            def images_out(h):
                sp.wait_ge(img_ready, 2 + h)
                sp.dma_start(himg[h * IH:(h + 1) * IH, 1:NIMG, :].rearrange("i (n w) d -> i n (w d)", n=G),
                             img[h][:].rearrange("p w d -> p (w d)")).then_inc(himg_out[h], 16)

            images_out(0)
            sp.wait_ge(himg_out[0], 32)
            sp.dma_start(X[0][0:NIMG, 1, :], himg[0]).then_inc(xi_in[0], 16)

            def embed_tail(i):
                if i == 4:
                    images_out(1)
                if i == HEAD - 1:
                    sp.wait_ge(himg_out[1], 16)

            def step(l, _l, _f, _m, a, *later):
                if a.exists(B):
                    w, _, _ = weight_piece(a)
                    piece = w.c if w.r is None else w.lin(1)
                    if a.slot(2) == 0:
                        w1_split.wait(sp, w.plus(-1))
                        sp.dma_start(wstage1[:], w1_pieces[piece]).then_inc(w1_in.sem, 16)
                    else:
                        w2_split.wait(sp, w.plus(-1))
                        sp.dma_start(wstage2[:].rearrange("p (c d) -> p c d", d=D),
                                     w2_pieces[:, bass.ds(piece * 3, 3), :]).then_inc(w2_in.sem, 16)
                if l.exists(B) and not (l.r is None and l.c == 0):
                    h_sum.wait(sp, l.plus(-XS))
                    src = l.c if l.r is None else l.lin(1)
                    sp.dma_start(X[l.slot(XS)][0:NIMG, 1, :], himg[src]).then_inc(xi_in[l.slot(XS)], 16)

            attend_steps(sp, step, embed_tail)
            pad_tiles(sp, 0)

            def estep(t, h, y):
                if t.exists(NT):
                    if t.r is None and t.c == 0:
                        for i in range(2):
                            sp.wait_ge(scattered[i], 32 * (B // 2))
                        for i, n in enumerate((E // 2, E // 2, 1)):
                            sp.wait_ge(pads_out[i], 16 * n)
                        sp.wait_ge(tiles, 1)
                    if t.plus(-RS).exists(NT):
                        sp.wait_ge(e_out[t.slot(RS)], t.plus(-RS).of(RS) * 16 + 16)
                    row = sp.value_load(tl[0:1, bass.ds(t.lin(1), 1)] if t.r is not None
                                        else tl[0:1, t.c:t.c + 1], min_val=0, max_val=E * CAP)
                    sp.dma_start(R[t.slot(RS)][:], routed[bass.ds(row, P), :]).then_inc(r_in[t.slot(RS)], 16)

            expert_steps(sp, estep)

        @block.gpsimd
        def _(pool):
            pool.memset(wo[:], 0.0).then_inc(pool_zeroed, 1)
            pool.memset(halfs[:], -0.5)
            pool.memset(one16[:], 1.0)
            pool.memset(ones[:], 1.0)
            for i in range(XS):
                pool.memset(X[i][:, 1, :], 0.0)
            for i in range(2):
                for t in (k1[i], k2[i], q1[i], hrow[i], V[i]):
                    pool.memset(t[:], 0.0)
            pool.memset(mxa[:], 0.0)
            pool.memset(mxb[:], 0.0)
            pool.memset(x2h[:], 0.0)
            pool.memset(x2l[:], 0.0)
            pool.memset(padrow[:], 0.0)
            pool.memset(cfg2[:], 0.0).then_inc(pool_zeroed, 1)
            pool.wait_ge(pool_zeroed, 2)
            pool.wait_ge(con_in, 16)
            for i in range(2):
                pool.memset(V[i][:, 0, :, DH:DH + 1], 1.0)
                for h in range(H):
                    g = h // HJ
                    pool.tensor_copy(V[i][:, 1, h, DH:DH + 1], con[:, K_HALF + g % 2:K_HALF + g % 2 + 1])
            pool.wait_ge(con_in, 16)
            pool.tensor_copy(padrow[:, C_ID:C_ID + 1].bitcast(I32), con[:, K_PADID:K_PADID + 1])
            pool.tensor_copy(count[:], con[:, K_BASE:K_BASE + E])
            pool.tensor_copy(ids[:], con[:, K_IDS:K_IDS + 2]).then_inc(pool_setup, 1)

            def y_deviation(h):
                pool.wait_ge(y_stats, h + 1)
                if h:
                    pool.wait_ge(img_ready, 2)
                pool.tensor_scalar(vary[:], mvy[:, :, 1], EPS, None, ALU.add).then_inc(y_rstd, 1)
                pool.wait_ge(y_rstd, 2 * h + 1)
                pool.tensor_tensor(rstdy[:], vary[:], halfs[0:PR, 0:G], ALU.pow).then_inc(y_rstd, 1)
                pool.wait_ge(y_rstd, 2 * h + 2)

            def y_scale(h, w):
                pool.wait_ge(y_mid, G * h + w + 1)
                pool.tensor_scalar(img[h][:, w, :], yi[h][:, w, :], rstdy[:, w:w + 1], None, ALU.mult).then_inc(y_scaled, 1)

            def y_place(h, ws):
                pool.wait_ge(y_scaled, G * h + ws.stop)
                pool.tensor_tensor(img[h][:, ws, :], img[h][:, ws, :],
                                   posr[:, ws.start * D:ws.stop * D].rearrange("p (w d) -> p w d", d=D),
                                   ALU.add).then_inc(img_ready, 1)

            for i in range(2 * G):
                pool.wait_ge(patch_stats, i + 1)
                pool.tensor_scalar(vari[:, i:i + 1], mvi[:, i:i + 1, 1], EPS, None, ALU.add).then_inc(patch_rstd, 1)
                pool.wait_ge(patch_rstd, 2 * i + 1)
                pool.tensor_tensor(rstdi[:, i:i + 1], vari[:, i:i + 1], halfs[0:PR, 0:1], ALU.pow).then_inc(patch_rstd, 1)
                if i == 3:
                    pool.wait_ge(place_in, 16 * 5)
                    pool.tensor_tensor(posr[:].rearrange("p (w d) -> p w d", d=D),
                                       posr[:].rearrange("p (w d) -> p w d", d=D),
                                       spread(b2_all[0:PR, :].unsqueeze(1), 1, G), ALU.add).then_inc(pos_ready, 1)
                if i == 8:
                    pool.wait_ge(pos_ready, 1)
                if i == 6:
                    pool.wait_ge(atoms_out, 16)
                    pool.wait_ge(table_ready, 2)
                    pool.indirect_dma_start(X[0][:, 0, :], None, atoms,
                                            bass.IndirectOffsetOnAxis(txt_i[:, 0:1], 0)).then_inc(xt_in[0], 16)
                if i == 7:
                    pool.wait_ge(b2_round, 2)
                    pool.tensor_tensor(b2_lo[:], b2r[:], b2_hi[:], ALU.subtract).then_inc(b2_split, 1)
                if i == 9:
                    y_deviation(0)
                if i >= 9:
                    y_scale(0, 2 * (i - 9))
                    y_scale(0, 2 * (i - 9) + 1)
                if i == 10:
                    y_place(0, slice(0, 4))
            y_place(0, slice(4, G))

            def embed_tail(i):
                if i == 2:
                    y_deviation(1)
                    for w in range(G):
                        y_scale(1, w)
                if i == 3:
                    y_place(1, slice(0, G))

            def step(s, l, f, m, a, p, r):
                if p.exists(B):
                    o_hi.wait(pool, p)
                    pool.tensor_tensor(otl[:], ot[:], oth[:], ALU.subtract).then_inc(o_lo.sem, 1)
                n = s.plus(1)
                if n.r is not None or n.c < B:
                    h_sum.wait(pool, n.plus(-XS))
                    o = n.plus(-2)
                    if o.r is not None or o.c >= 0:
                        pool.wait_ge(xt_in[o.slot(XS)], o.of(XS) * 16 + 16)
                    idx = txt_i[:, n.c:n.c + 1] if n.r is None else txt_i[:, bass.ds(n.lin(1), 1)]
                    apart(pool, pool_apart)
                    pool.tensor_copy(txt_now[n.slot(2)][:], idx).then_inc(idx_put.sem, 1)
                    idx_put.wait(pool, n.plus(-1))
                    apart(pool, pool_apart)
                    pool.indirect_dma_start(X[n.slot(XS)][:, 0, :], None, atoms,
                                            bass.IndirectOffsetOnAxis(txt_now[n.slot(2)][:], 0)).then_inc(xt_in[n.slot(XS)], 16)
                if a.exists(B) and a.slot(2) == 1:
                    w, cols, _ = weight_piece(a)
                    w1_scaled.wait(pool, w)
                    pool.tensor_tensor(w1_lo[:, cols], wstage1[:], w1_hi[:, cols], ALU.subtract).then_inc(w1_split.sem, 1)
                if p.exists(B) and p.slot(2) == 1:
                    w, _, cols = weight_piece(p)
                    w2_scaled.wait(pool, w)
                    pool.tensor_tensor(w2_lo[:, cols], wstage2[:], w2_hi[:, cols], ALU.subtract).then_inc(w2_split.sem, 1)
                if s.exists(B):
                    ln_stats.wait(pool, s)
                    ln_rstd.wait(pool, s.plus(-1))
                    x_norm.wait(pool, s.plus(-1))
                    apart(pool, pool_apart)
                    pool.tensor_scalar(var1[:], mv1[:, :, 1], EPS, None, ALU.add).then_inc(ln_rstd.sem, 1)
                    pool.tensor_scalar(neg1[:], mv1[:, :, 0], -1.0, None, ALU.mult).then_inc(ln_rstd.sem, 1)
                    ln_rstd.wait(pool, s, 1)
                    pool.tensor_tensor(rstd1[:], var1[:], halfs[:, 0:2], ALU.pow).then_inc(ln_rstd.sem, 1)
                    ln_rstd.wait(pool, s, 3)
                    pool.tensor_tensor(shift1[:], neg1[:], rstd1[:], ALU.mult).then_inc(ln_rstd.sem, 1)
                if f.exists(B):
                    k_hi.wait(pool, f)
                    sc_b.wait(pool, f.plus(-2))
                    apart(pool, pool_apart)
                    pool.tensor_scalar(k2[f.slot(2)][:, :, 0:S], kh[:], con[:, K_K2M:K_K2M + 1], con[:, K_K2A:K_K2A + 1],
                                       ALU.mult, ALU.add).then_inc(k_st2.sem, 1)
                if p.exists(B):
                    c = p.slot(2)
                    ln2_stats.wait(pool, p)
                    ln2_rstd.wait(pool, p.plus(-1))
                    x2_norm.wait(pool, p.plus(-1))
                    apart(pool, pool_apart)
                    pool.tensor_scalar(var2[:], mv2[:, :, 1], EPS, None, ALU.add).then_inc(ln2_rstd.sem, 1)
                    pool.tensor_scalar(neg2[:], mv2[:, :, 0], -1.0, None, ALU.mult).then_inc(ln2_rstd.sem, 1)
                    pool.tensor_copy(hrow[c][:, :, C_MEAN], mv2[:, :, 0]).then_inc(ln2_rstd.sem, 1)
                    ln2_rstd.wait(pool, p, 1)
                    pool.tensor_tensor(hrow[c][:, :, C_RSTD], var2[:], halfs[:, 0:2], ALU.pow).then_inc(ln2_rstd.sem, 1)
                    ln2_rstd.wait(pool, p, 4)
                    pool.tensor_tensor(shift2[:], neg2[:], hrow[c][:, :, C_RSTD], ALU.mult).then_inc(ln2_rstd.sem, 1)
                if r.exists(B):
                    c = r.slot(2)
                    id_put.wait(pool, r.plus(-1))
                    apart(pool, pool_apart)
                    pool.tensor_copy(hrow[c][:, :, C_ID].bitcast(I32), ids[:]).then_inc(id_put.sem, 1)
                    pool.tensor_scalar(ids[:], ids[:], float(S), None, ALU.add).then_inc(id_put.sem, 1)
                    id_put.wait(pool, r)
                    slots.wait(pool, r)
                    prob.wait(pool, r)
                    ln2_rstd.wait(pool, r)
                    apart(pool, pool_apart)
                    pool.indirect_dma_start(routed, bass.IndirectOffsetOnAxis(slot_i[c][:, 0:1], 0),
                                            hrow[c][:, 0, :], None).then_inc(scattered[c], 16)
                    pool.indirect_dma_start(routed, bass.IndirectOffsetOnAxis(slot_i[c][0:NIMG, 1:2], 0),
                                            hrow[c][0:NIMG, 1, :], None).then_inc(scattered[c], 16)

            attend_steps(pool, step, embed_tail)
            pool.dma_start(routed[E * CAP:E * CAP + P, :], padrow[:]).then_inc(pads_out[2], 16)

            def estep(t, h, y):
                if y.exists(NT):
                    e_res.wait(pool, y)
                    s = y.slot(RS)
                    apart(pool, pool_apart)
                    pool.indirect_dma_start(out, bass.IndirectOffsetOnAxis(R[s][:, C_ID:C_ID + 1].bitcast(I32), 0),
                                            res[y.slot(3)][:], None, bounds_check=T - 1, oob_is_err=False).then_inc(e_out[s], 16)

            expert_steps(pool, estep)
            pool.wait_ge(xt_in[0], 16 * (B // XS + 1))
            for s in range(RS):
                pool.wait_ge(e_out[s], 16 * ((NT - s + RS - 1) // RS))

        @block.scalar
        def _(act):
            act.dma_start(wl[:], W_lin.rearrange("(f p c) d -> p f c d", f=2, c=C)).then_inc(patch_w_in, 16)
            act.dma_start(g1[:], ln1_g.rearrange("(f p c) -> p f c", f=2, c=C)).then_inc(patch_w_in, 16)
            act.dma_start(b1v[:], ln1_b.rearrange("(f p c) -> p f c", f=2, c=C)).then_inc(patch_w_in, 16)
            act.dma_start(bl_all[:], spread(b_lin.rearrange("(a d) -> a d", a=1), 0, P)).then_inc(patch_w_in, 16)
            act.dma_start(cfg_s[:], cfg).then_inc(atom_in, 16)
            act.dma_start(emb[:, 0, :], sub_e).then_inc(atom_in, 16)
            act.dma_start(emb[:, 1, :], occ_e).then_inc(atom_in, 16)
            act.dma_start(txt[:], x_txt).then_inc(atom_in, 16)
            for t, src in ((g2_all, ln2_g), (b2_all, ln2_b)):
                act.dma_start(t[:], spread(src.rearrange("(a d) -> a d", a=1), 0, P)).then_inc(place_in, 16)
            act.dma_start(posr[:], spread(pos[0, 1:NIMG, :].rearrange("(a n w) d -> a n (w d)", a=1, n=G), 0, IH))\
                .then_inc(place_in, 16)
            act.dma_start(clsr[:], spread(cls_tok[0], 0, B)).then_inc(place_in, 16)
            act.dma_start(posc[:], spread(pos[0, 0:1, :], 0, B)).then_inc(place_in, 16)
            for i in range(2 * G):
                act.wait_ge(pe_patchT, i + 1)
                if i >= 2:
                    act.wait_ge(pe_patchY, i - 1)
                for c in range(2):
                    last = act.activation(xTi[i % 2][:, 3 * c:3 * c + 3, :],
                                          bank[2 * (i % 2) + c][:, 0:3 * PR].rearrange("p (c n) -> p c n", c=3),
                                          ACT.Copy)
                last.then_inc(act_patchT, 1)
                if i == 4:
                    act.wait_ge(route_w_in, 80)
                    act.activation(b2_hi[:], b2r[:], ACT.Copy, scale=W_SCALE).then_inc(b2_round, 1)
                if i == 5:
                    act.wait_ge(b2_round, 1)
                    act.activation(b2r[:], b2r[:], ACT.Copy, scale=W_SCALE).then_inc(b2_round, 1)

            def exps(a, j):
                if j == 0:
                    pv.wait(act, a.plus(-1))
                sc_a.wait(act, a, j + 1)
                act.activation(pa[j][:], bank[4][:, 0:HG * S], ACT.Exp,
                               scale=float(D) ** -0.5 / QK_SCALE ** 2).then_inc(exp_a.sem, 1)
                sc_b.wait(act, a, j + 1)
                act.activation(pb[j][:], bank[5][:, 0:2 * S], ACT.Exp,
                               scale=float(D) ** -0.5 / QK_SCALE ** 2).then_inc(exp_b.sem, 1)

            def values(f):
                v_proj.wait(act, f)
                pv.wait(act, f.plus(-2))
                pv_out = bank[2][:, 0:2 * D].rearrange("p (t h d) -> p t h d", t=2, h=H)
                vs = V[f.slot(2)]
                act.activation(vs[:, 0, :, 0:DH], pv_out[:, 0], ACT.Copy, scale=1.0 / QK_SCALE)
                act.activation(vs[64:P, 1, HJ:2 * HJ, 0:DH], pv_out[64:P, 1, HJ:2 * HJ], ACT.Copy, scale=1.0 / QK_SCALE)
                act.activation(vs[0:64, 1].rearrange("p (g j) d -> p g j d", j=HJ)[:, 0:HG:2, :, 0:DH],
                               pv_out[0:64, 1].rearrange("p (g j) d -> p g j d", j=HJ)[:, 0:HG:2], ACT.Copy,
                               scale=1.0 / QK_SCALE).then_inc(v_out.sem, 1)

            def step(s, l, f, m, a, p, r):
                if a.exists(B):
                    exps(a, 0)
                if m.exists(B):
                    values(m)
                if a.exists(B):
                    exps(a, 1)
                if p.exists(B):
                    o_norm.wait(act, p)
                    o_proj.wait(act, p.plus(-1))
                    act.activation(oth[:], ot[:], ACT.Copy).then_inc(o_hi.sem, 1)
                if r.exists(B):
                    x2_T.wait(act, r)
                    logits.wait(act, r.plus(-1))
                    act.activation(x2h[:, :, 0:SP], bank[3][0:DK, 0:2 * SP].rearrange("p (k n) -> p k n", k=2),
                                   ACT.Copy).then_inc(x2_hi.sem, 1)
                if a.exists(B):
                    exps(a, 2)
                if l.exists(B):
                    x_T.wait(act, l)
                    v_proj.wait(act, l.plus(-2))
                    act.activation(xh[l.slot(2)][:], bank[3][0:DK, 0:2 * SP].rearrange("p (k n) -> p k n", k=2),
                                   ACT.Copy).then_inc(x_hi.sem, 1)
                if f.exists(B):
                    k_proj.wait(act, f)
                    k_st1.wait(act, f.plus(-1))
                    k_st2.wait(act, f.plus(-1))
                    act.activation(kh[:].rearrange("p g n -> p (g n)"), bank[2][:, 0:HG * S], ACT.Copy).then_inc(k_hi.sem, 1)
                if a.exists(B):
                    exps(a, 3)
                if r.exists(B):
                    onehot.wait(act, r, 3)
                    prob.wait(act, r.plus(-1), 1)
                    act.activation(lge[:], lgd[:], ACT.Exp).then_inc(lg_exp.sem, 1)
                if a.exists(B):
                    if a.r is None and a.c == 0:
                        act.wait_ge(himg_out[1], 16)
                        act.wait_ge(b2_split, 1)
                    w, d1, d2 = weight_piece(a)
                    loaded, stage, hi, cols, scaled = ((w1_in, wstage1, w1_hi, d1, w1_scaled),
                                                       (w2_in, wstage2, w2_hi, d2, w2_scaled))[a.slot(2)]
                    loaded.wait(act, w)
                    act.activation(hi[:, cols], stage[:], ACT.Copy, scale=W_SCALE).then_inc(scaled.sem, 1)
                    scaled.wait(act, w, 1)
                    act.activation(stage[:], stage[:], ACT.Copy, scale=W_SCALE).then_inc(scaled.sem, 1)
                if s.exists(B):
                    ln_rstd.wait(act, s)
                    x_T.wait(act, s.plus(-1))
                    for t in range(2):
                        last = act.activation(xn[:, t, :], X[s.slot(XS)][:, t, :], ACT.Identity,
                                              bias=shift1[:, t:t + 1], scale=rstd1[:, t:t + 1])
                    last.then_inc(x_norm.sem, 1)
                if f.exists(B):
                    q_proj.wait(act, f)
                    sc_b.wait(act, f.plus(-2))
                    act.activation(q1[f.slot(2)][:, :, 0:S], bank[3][:, 0:HG * S].rearrange("p (g n) -> p g n", g=HG),
                                   ACT.Copy).then_inc(q_hi.sem, 1)
                if p.exists(B):
                    ln2_rstd.wait(act, p)
                    h_sum.wait(act, p)
                    x2_T.wait(act, p.plus(-1))
                    c = p.slot(2)
                    for t in range(2):
                        last = act.activation(xn2[:, t, :], hrow[c][:, t, 0:D], ACT.Identity,
                                              bias=shift2[:, t:t + 1], scale=hrow[c][:, t, C_RSTD:C_RSTD + 1])
                    last.then_inc(x2_norm.sem, 1)

            attend_steps(act, step)
            pad_tiles(act, 1)

            expert_of = expert_reader(act)

            def estep(t, h, y):
                if t.exists(NT):
                    e_T.wait(act, t)
                    e_h.wait(act, t.plus(-2))
                    act.activation(xeh[t.slot(2)][:], bank[0][0:DK, 0:2 * P].rearrange("p (k n) -> p k n", k=2),
                                   ACT.Copy).then_inc(e_hi.sem, 1)
                if h.exists(NT):
                    s = h.slot(2)
                    ex = expert_of(t, h)
                    e_hl.wait(act, h.plus(-2))
                    for c in range(2):
                        e_h.wait(act, h, c + 1)
                        for m in range(3):
                            fc = 3 * c + m
                            last = act.activation(hf[s][:, fc, :], bank[2 + 2 * s + c][:, m * P:(m + 1) * P], ACT.Gelu,
                                                  bias=b1T[:, bass.ds(ex * FC + fc, 1)], scale=1.0 / W_SCALE)
                        last.then_inc(e_gelu.sem, 1)

            act.wait_ge(words_ready, 1)
            expert_steps(act, estep)

        @block.vector
        def _(dve):
            dve.wait_ge(con_in, 16)
            dve.tensor_scalar(neg_id[:], ident, -1.0 / MAX_SCALE, None, ALU.mult)
            dve.tensor_copy(tri[:], con[:, K_TRI:K_TRI + P]).then_inc(const_ready, 1)
            dve.wait_ge(qkv_in, 16)
            for k in range(2):
                for t in range(2):
                    last = dve.tensor_scalar(wdup[:, k, :, t, :], wqkv[:, k, :].rearrange("p (h d) -> p h d", d=DH),
                                             QK_SCALE, None, ALU.mult)
            last.then_inc(w_ready, 1)
            dve.wait_ge(w_ready, 1)
            wflat = wdup[:].rearrange("p k (q n) t d -> p k q (n t d)", q=2)
            for k in range(2):
                last = dve.tensor_copy(wqk_hi[:, k], wflat[:, k])
            last.then_inc(w_ready, 1)
            dve.wait_ge(w_ready, 2)
            for k in range(2):
                last = dve.tensor_tensor(wqk_lo[:, k], wflat[:, k], wqk_hi[:, k], ALU.subtract)
            last.then_inc(w_ready, 1)
            def stats_of_patches(i):
                h, w = divmod(i, G)
                if w == 0:
                    dve.wait_ge(image_in[h], 16 * C)
                for c in range(C):
                    last = dve.bn_stats(sti[:, i, c, :],
                                        xi[h][:, c, :].rearrange("p (r w) -> p r w", r=PATCH)[:, :, w * PATCH:(w + 1) * PATCH])
                last.then_inc(patch_bn, 1)
                dve.wait_ge(patch_bn, i + 1)
                dve.bn_aggr(mvi[:, i, :], sti[:, i, :, :]).then_inc(patch_stats, 1)

            def normalize_patches(i):
                h, w = divmod(i, G)
                dve.wait_ge(patch_rstd, 2 * i + 2)
                dve.wait_ge(patch_stats, i + 1)
                if i >= 2:
                    dve.wait_ge(pe_patchT, i - 1)
                dve.tensor_scalar(xni[i % 2][:].rearrange("p c (r q) -> p c r q", q=PATCH),
                                  xi[h][:].rearrange("p c (r w) -> p c r w", r=PATCH)[:, :, :, w * PATCH:(w + 1) * PATCH]
                                  .rearrange("p c (f r) q -> p (c f) r q", f=2),
                                  mvi[:, i, 0:1], rstdi[:, i:i + 1], ALU.subtract, ALU.mult).then_inc(patch_norm, 1)

            def y_out(i):
                dve.wait_ge(pe_patchY, i + 1)
                dve.tensor_tensor(yi[i // G][:, i % G, :], bank[4 + i % 2][0:PR, 0:D], bias_all[0:PR, :],
                                  ALU.add).then_inc(patch_y, 1)

            def stats_of_y(h):
                dve.wait_ge(patch_y, G * (h + 1))
                for w in range(G):
                    last = dve.bn_stats(sty[:, w, :], yi[h][:, w, :])
                last.then_inc(y_bn, 1)

            def aggregate_y(h):
                dve.wait_ge(y_bn, h + 1)
                if h:
                    dve.wait_ge(y_rstd, 1)
                    dve.wait_ge(y_mid, G)
                for w in range(G):
                    last = dve.bn_aggr(mvy[:, w, :], sty[:, w, :])
                last.then_inc(y_stats, 1)
                dve.wait_ge(y_stats, h + 1)

            def y_middle(h, w):
                dve.scalar_tensor_tensor(out=yi[h][:, w, :], in0=yi[h][:, w, :], scalar=mvy[:, w, 0:1],
                                         in1=g2_all[0:PR, :], op0=ALU.subtract, op1=ALU.mult).then_inc(y_mid, 1)

            stats_of_patches(0)
            dve.wait_ge(patch_w_in, 16 * 4)
            for f2 in range(2):
                for c in range(C):
                    last = dve.tensor_scalar(wlg[:, f2, c, :], wl[:, f2, c, :], g1[:, f2, c:c + 1], None, ALU.mult)
            last.then_inc(patch_w_ready, 1)
            dve.wait_ge(atom_in, 64)
            dve.wait_ge(pool_zeroed, 2)
            dve.tensor_scalar(cfg2[:, 0, 0:NCFG], cfg_s[:], 0.0, None, ALU.not_equal)
            dve.tensor_scalar(cfg2[:, 1, 0:NCFG], cfg_s[:], -1.0, 0.0, ALU.add, ALU.max).then_inc(cfg_ready, 1)
            dve.tensor_scalar(txt_neg[:], txt[:], 0.0, float(NAT), ALU.is_lt, ALU.mult)
            dve.tensor_copy(txt_f[:], txt[:]).then_inc(idx_step, 1)
            dve.wait_ge(idx_step, 1)
            dve.tensor_tensor(txt_f[:], txt_f[:], txt_neg[:], ALU.add).then_inc(idx_step, 1)
            dve.wait_ge(idx_step, 2)
            dve.tensor_scalar(txt_f[:], txt_f[:], 0.0, float(NAT - 1), ALU.max, ALU.min).then_inc(idx_step, 1)
            dve.wait_ge(pe_cfgT, 1)
            dve.tensor_copy(cfgT[:], bank[6][0:32, 0:2 * NAT].rearrange("p (t n) -> p t n", t=2)).then_inc(cfgT_ready, 1)
            for i in range(2 * G):
                if i + 1 < 2 * G:
                    stats_of_patches(i + 1)
                normalize_patches(i)
                if i == 0:
                    dve.wait_ge(pe_bias, 1)
                    dve.tensor_tensor(bias_all[:], bank[7][:, 0:D], bl_all[:], ALU.add).then_inc(bias_ready, 1)
                    dve.memset(txt_i[:, B:B + 1], 0)
                if i == 1:
                    dve.wait_ge(pe_table, 1)
                    dve.wait_ge(bias_ready, 1)
                    dve.tensor_copy(tab[:], bank[7][0:NAT, 0:D]).then_inc(table_ready, 1)
                    dve.tensor_copy(txt_i[:, 0:B], bank[6][:, 256:256 + B]).then_inc(table_ready, 1)
                if i >= 2:
                    y_out(i - 2)
                if i == 3:
                    dve.wait_ge(place_in, 16 * 5)
                    dve.tensor_tensor(clsr[:], clsr[:], posc[:], ALU.add).then_inc(cls_ready, 1)
                if i == 4:
                    dve.wait_ge(route_w_in, 80)
                    dve.wait_ge(pe_b1T, 1)
                    dve.tensor_copy(b1T[:], bank[6][:, 0:E * FC])
                    dve.memset(bank[6][:, HG * S:OB * 32], 1.0)
                    dve.wait_ge(wo_in, 16 * HJ)
                    dve.tensor_scalar(wo[:], wo[:], W_SCALE, None, ALU.mult)
                    dve.tensor_scalar(ws[:], ws[:], W_SCALE, None, ALU.mult).then_inc(late_ready, 1)
                if i == 5:
                    dve.wait_ge(late_ready, 1)
                    dve.tensor_copy(wo_hi[:], wo[:])
                    dve.tensor_copy(ws_hi[:], ws[:]).then_inc(late_ready, 1)
                if i == 6:
                    dve.wait_ge(late_ready, 2)
                    dve.tensor_tensor(wo_lo[:], wo[:], wo_hi[:], ALU.subtract)
                    dve.tensor_tensor(ws_lo[:], ws[:], ws_hi[:], ALU.subtract).then_inc(late_ready, 1)
                if i == 7:
                    stats_of_y(0)
                if i == 8:
                    aggregate_y(0)
                if 8 <= i < 11:
                    y_middle(0, 2 * (i - 8))
                    y_middle(0, 2 * (i - 8) + 1)
            y_out(2 * G - 2)
            y_out(2 * G - 1)
            dve.wait_ge(pool_setup, 1)

            def embed_tail(i):
                if i == 1:
                    stats_of_y(1)
                    aggregate_y(1)
                    for w in range(G):
                        y_middle(1, w)

            def take_max(f, m):
                j, images = m // 2, m % 2
                if m == 0:
                    max_rows.wait(dve, f.plus(-1))
                max_scores.wait(dve, f, m + 1)
                if images:
                    dve.tensor_reduce(mxb[:, :, 32 * j + DH], bank[0][:, 0:2 * S].rearrange("p (g n) -> p g n", g=2),
                                      AX.X, ALU.max).then_inc(max_taken.sem, 1)
                else:
                    dve.tensor_reduce(mxa[:, :, 32 * j + DH], bank[7][:, 0:HG * S].rearrange("p (g n) -> p g n", g=HG),
                                      AX.X, ALU.max).then_inc(max_taken.sem, 1)

            def step(s, l, f, m, a, p, r):
                if m.exists(B):
                    take_max(m, 0)
                if s.exists(B):
                    n = s.slot(XS)
                    dve.wait_ge(xi_in[n], s.of(XS) * 16 + 16)
                    dve.wait_ge(xt_in[n], s.of(XS) * 16 + 16)
                    ln_stats.wait(dve, s.plus(-1))
                    for t in range(2):
                        dve.bn_stats(st1[:, t, :], X[n][:, t, :]).then_inc(ln_stats.sem, 1)
                if m.exists(B):
                    take_max(m, 1)
                if r.exists(B):
                    x2_hi.wait(dve, r)
                    dve.tensor_tensor(x2l[:, :, 0:SP], bank[3][0:DK, 0:2 * SP].rearrange("p (k n) -> p k n", k=2),
                                      x2h[:, :, 0:SP], ALU.subtract).then_inc(x2_lo.sem, 1)
                if m.exists(B):
                    take_max(m, 2)
                if s.exists(B):
                    ln_stats.wait(dve, s, 2)
                    ln_rstd.wait(dve, s.plus(-1))
                    for t in range(2):
                        apart(dve, dve_apart)
                        dve.bn_aggr(mv1[:, t, :], st1[:, t, :]).then_inc(ln_stats.sem, 1)
                if m.exists(B):
                    take_max(m, 3)
                if r.exists(B):
                    logits.wait(dve, r)
                    onehot.wait(dve, r.plus(-1))
                    dve.scalar_tensor_tensor(out=lg[:], in0=bank[1][:, LG:LG + 2 * E].rearrange("p (t e) -> p t e", t=2),
                                             scalar=1.0 / W_SCALE, in1=bs_all[:], op0=ALU.mult,
                                             op1=ALU.add).then_inc(onehot.sem, 1)
                if l.exists(B):
                    x_hi.wait(dve, l)
                    dve.tensor_tensor(xl[l.slot(2)][:], bank[3][0:DK, 0:2 * SP].rearrange("p (k n) -> p k n", k=2),
                                      xh[l.slot(2)][:], ALU.subtract).then_inc(x_lo.sem, 1)
                if m.exists(B):
                    take_max(m, 4)
                if r.exists(B):
                    onehot.wait(dve, r, 1)
                    dve.tensor_reduce(lgm[:], lg[:], AX.X, ALU.max).then_inc(onehot.sem, 1)
                if m.exists(B):
                    take_max(m, 5)
                if r.exists(B):
                    onehot.wait(dve, r, 2)
                    lg_exp.wait(dve, r.plus(-1))
                    dve.tensor_tensor(lgd[:], lg[:], spread(lgm[:].unsqueeze(2), 2, E), ALU.subtract).then_inc(onehot.sem, 1)
                if f.exists(B):
                    k_hi.wait(dve, f)
                    sc_b.wait(dve, f.plus(-2))
                    dve.scalar_tensor_tensor(out=k1[f.slot(2)][:, :, 0:S], in0=kh[:], scalar=con[:, K_KLO:K_KLO + 1],
                                             in1=bank[2][:, 0:HG * S].rearrange("p (g n) -> p g n", g=HG),
                                             op0=ALU.mult, op1=ALU.add).then_inc(k_st1.sem, 1)
                if r.exists(B):
                    onehot.wait(dve, r, 3)
                    dve.scalar_tensor_tensor(out=first[:], in0=lgd[:], scalar=0.0,
                                             in1=con[:, K_FIRST:K_FIRST + 2 * E].rearrange("p (t e) -> p t e", t=2),
                                             op0=ALU.is_equal, op1=ALU.mult).then_inc(onehot.sem, 1)
                if p.exists(B):
                    c = p.slot(2)
                    o_proj.wait(dve, p)
                    x2_norm.wait(dve, p.plus(-2))
                    if p.plus(-2).exists(B):
                        dve.wait_ge(scattered[c], p.plus(-2).of(2) * 32 + 32)
                    for t, rows in enumerate((P, NIMG)):
                        dve.scalar_tensor_tensor(out=hrow[c][0:rows, t, 0:D], in0=bank[1][0:rows, t * D:(t + 1) * D],
                                                 scalar=1.0 / W_SCALE, in1=X[p.slot(XS)][0:rows, t, :], op0=ALU.mult,
                                                 op1=ALU.add).then_inc(h_sum.sem, 1)
                if r.exists(B):
                    onehot.wait(dve, r, 4)
                    dve.tensor_reduce(firstm[:], first[:], AX.X, ALU.max).then_inc(onehot.sem, 1)
                if m.exists(B):
                    take_max(m, 6)
                if r.exists(B):
                    onehot.wait(dve, r, 5)
                    dve.tensor_tensor(oh[:], first[:], spread(firstm[:].unsqueeze(2), 2, E), ALU.is_equal).then_inc(onehot.sem, 1)
                if m.exists(B):
                    take_max(m, 7)
                if p.exists(B):
                    ln2_stats.wait(dve, p.plus(-1))
                    for t in range(2):
                        h_sum.wait(dve, p, t + 1)
                        dve.bn_stats(st2[:, t, :], hrow[c][:, t, 0:D]).then_inc(ln2_stats.sem, 1)
                if r.exists(B):
                    onehot.wait(dve, r, 6)
                    dve.tensor_tensor(ohb[:], oh[:], spread(con[:, K_VALID:K_VALID + 2].unsqueeze(2), 2, E),
                                      ALU.mult).then_inc(onehot.sem, 1)
                if r.exists(B):
                    lg_exp.wait(dve, r)
                    prob.wait(dve, r.plus(-1))
                    dve.tensor_reduce(esum[:], lge[:], AX.X, ALU.add).then_inc(prob.sem, 1)
                if p.exists(B):
                    ln2_rstd.wait(dve, p.plus(-1))
                    for t in range(2):
                        ln2_stats.wait(dve, p, t + 1)
                        apart(dve, dve_apart)
                        dve.bn_aggr(mv2[:, t, :], st2[:, t, :]).then_inc(ln2_stats.sem, 1)
                if r.exists(B):
                    prob.wait(dve, r, 1)
                    dve.tensor_scalar(esum[:], esum[:], W_SCALE, None, ALU.mult).then_inc(prob.sem, 1)
                if m.exists(B):
                    max_rows.wait(dve, m)
                    q_rest.wait(dve, m)
                    sc_b.wait(dve, m.plus(-2))
                    dve.scalar_tensor_tensor(out=q2[m.slot(2)][:], in0=qlo[m.slot(2)][:], scalar=con[:, K_K2M:K_K2M + 1],
                                             in1=bank[7][:, 0:HG * S].rearrange("p (g n) -> p g n", g=HG),
                                             op0=ALU.mult, op1=ALU.add).then_inc(q_st2.sem, 1)
                if a.exists(B):
                    pv.wait(dve, a)
                    o_norm.wait(dve, a.plus(-1))
                    apart(dve, dve_apart)
                    dve.transpose(oT[:], bank[6][:, 0:OB * 32]).then_inc(o_norm.sem, 1)
                if r.exists(B):
                    ranks.wait(dve, r)
                    slots.wait(dve, r.plus(-1))
                    rk = bank[1][:, LG + 2 * E:LG + 5 * E].rearrange("p (t e) -> p t e", t=3)
                    dve.tensor_tensor(rank[:], rk[:, 0:2, :], spread(count[:].unsqueeze(1), 1, 2), ALU.add).then_inc(slots.sem, 1)
                    prob.wait(dve, r, 2)
                    dve.reciprocal(hrow[r.slot(2)][:, :, C_PROB], esum[:]).then_inc(prob.sem, 1)
                if a.exists(B):
                    o_norm.wait(dve, a, 1)
                    dve.reciprocal(recip[:], oT[:].rearrange("p (b c) -> p b c", c=32)[:, :, DH]).then_inc(o_norm.sem, 1)
                if r.exists(B):
                    slots.wait(dve, r, 1)
                    dve.tensor_tensor(rank[:], rank[:], ohb[:], ALU.mult).then_inc(slots.sem, 1)
                    dve.tensor_tensor(count[:], count[:], rk[:, 2, :], ALU.add).then_inc(slots.sem, 1)
                if a.exists(B):
                    o_norm.wait(dve, a, 2)
                    apart(dve, dve_apart)
                    dve.transpose(den[:], spread(recip[:].unsqueeze(2), 2, 32)).then_inc(o_norm.sem, 1)
                if r.exists(B):
                    slots.wait(dve, r, 2)
                    dve.tensor_reduce(slotf[:], rank[:], AX.X, ALU.add).then_inc(slots.sem, 1)
                if f.exists(B):
                    q_hi.wait(dve, f)
                    q_st2.wait(dve, f.plus(-2))
                    dve.tensor_tensor(qlo[f.slot(2)][:], bank[3][:, 0:HG * S].rearrange("p (g n) -> p g n", g=HG),
                                      q1[f.slot(2)][:, :, 0:S], ALU.subtract).then_inc(q_rest.sem, 1)
                if r.exists(B):
                    slots.wait(dve, r, 4)
                    dve.tensor_copy(slot_i[r.slot(2)][:], slotf[:]).then_inc(slots.sem, 1)
                if a.exists(B):
                    o_norm.wait(dve, a, 3)
                    o_lo.wait(dve, a.plus(-1))
                    dve.tensor_tensor(ot[:].rearrange("p g n -> p (g n)"), bank[6][:, 0:HG * S], den[:, 0:HG * S],
                                      ALU.mult).then_inc(o_norm.sem, 1)

            attend_steps(dve, step, embed_tail)

            last_b = Turn(B - 1)
            slots.wait(dve, last_b)
            dve.tensor_copy(pad_i[:], count[0:1, :]).then_inc(pads_i, 1)
            chain = [0]

            def link(ins):
                chain[0] += 1
                ins.then_inc(list_step, 1)
                dve.wait_ge(list_step, chain[0])

            link(dve.tensor_tensor(cnt_f[:], count[0:1, :], con[0:1, K_BASE:K_BASE + E], ALU.subtract))
            link(dve.tensor_scalar(cnt_i[:], cnt_f[:], float(P - 1), None, ALU.add))
            link(dve.tensor_scalar(cnt_i[:], cnt_i[:], P.bit_length() - 1, None, ALU.logical_shift_right))
            link(dve.tensor_copy(ntile[:], cnt_i[:]))
            link(dve.tensor_scalar(skip[:], ntile[:], -float(P), float(CAP), ALU.mult, ALU.add))
            link(dve.tensor_copy(cum[:, 0, :], ntile[:]))
            for n, d in enumerate((1, 2, 4)):
                link(dve.tensor_copy(cum[:, n + 1, 0:d], cum[:, n, 0:d]))
                link(dve.tensor_tensor(cum[:, n + 1, d:E], cum[:, n, d:E], cum[:, n, 0:E - d], ALU.add))
            tile_no = con[0:1, K_TILE:K_TILE + NT]
            link(dve.tensor_tensor(reached[:], spread(tile_no.unsqueeze(2), 2, E), spread(cum[:, 3, :].unsqueeze(1), 1, NT),
                                   ALU.is_ge))
            link(dve.tensor_reduce(tl_f[:, 1, :], reached[:], AX.X, ALU.add))
            link(dve.tensor_tensor(reached[:], reached[:], spread(skip[:].unsqueeze(1), 1, NT), ALU.mult))
            link(dve.tensor_reduce(tl_f[:, 0, :], reached[:], AX.X, ALU.add))
            link(dve.scalar_tensor_tensor(out=tl_f[:, 0, :], in0=tile_no, scalar=float(P), in1=tl_f[:, 0, :],
                                          op0=ALU.mult, op1=ALU.add))
            link(dve.tensor_scalar(tl_f[:, 0, :], tl_f[:, 0, :], float(E * CAP), None, ALU.min))
            link(dve.tensor_scalar(tl_f[:, 1, :], tl_f[:, 1, :], float(E - 1), None, ALU.min))
            dve.tensor_copy(tl[:], tl_f[:, 0, :]).then_inc(tiles, 1)
            link(dve.memset(queue[:], 0.0))
            link(dve.tensor_copy(queue[:].rearrange("a r u -> a (r u)")[:, 2:2 + NT], tl_f[:, 1, :]))
            link(dve.tensor_copy(words_f[:], queue[:, 0:NW, 0]))
            for u in range(1, RS + 1):
                link(dve.scalar_tensor_tensor(out=words_f[:], in0=queue[:, u // RS:u // RS + NW, u % RS],
                                              scalar=float(1 << (WB * u)), in1=words_f[:], op0=ALU.mult, op1=ALU.add))
            dve.tensor_copy(words[:], words_f[:]).then_inc(words_ready, 1)

            def normalize(n):
                s = n.slot(RS)
                dve.wait_ge(r_in[s], n.of(RS) * 16 + 16)
                e_T.wait(dve, n.plus(-2))
                dve.tensor_scalar(xe[n.slot(2)][:], R[s][:, 0:D], R[s][:, C_MEAN:C_MEAN + 1],
                                  R[s][:, C_RSTD:C_RSTD + 1], ALU.subtract, ALU.mult).then_inc(e_norm.sem, 1)

            def estep(t, h, y):
                if t.exists(NT):
                    e_hi.wait(dve, t)
                    e_h.wait(dve, t.plus(-2))
                    dve.tensor_tensor(xel[t.slot(2)][:], bank[0][0:DK, 0:2 * P].rearrange("p (k n) -> p k n", k=2),
                                      xeh[t.slot(2)][:], ALU.subtract).then_inc(e_lo.sem, 1)
                if t.plus(1).exists(NT):
                    normalize(t.plus(1))
                if h.exists(NT):
                    s = h.slot(2)
                    for c in range(2):
                        e_gelu.wait(dve, h, c + 1)
                        e_y.wait(dve, h.plus(-2))
                        m = slice(3 * c, 3 * c + 3)
                        dve.tensor_copy(hh[s][:, m, :], hf[s][:, m, :]).then_inc(e_hh.sem, 1)
                        e_hh.wait(dve, h, c + 1)
                        dve.tensor_tensor(hl[s][:, m, :], hf[s][:, m, :], hh[s][:, m, :], ALU.subtract).then_inc(e_hl.sem, 1)
                if y.exists(NT):
                    s = y.slot(RS)
                    e_y.wait(dve, y)
                    o = y.plus(-3)
                    if o.exists(NT):
                        dve.wait_ge(e_out[o.slot(RS)], o.of(RS) * 16 + 16)
                    dve.scalar_tensor_tensor(out=res[y.slot(3)][:], in0=bank[6 + y.slot(2)][:, 0:D],
                                             scalar=R[s][:, C_PROB:C_PROB + 1], in1=R[s][:, 0:D],
                                             op0=ALU.mult, op1=ALU.add).then_inc(e_res.sem, 1)

            normalize(Turn(0))
            expert_steps(dve, estep)

        @block.tensor
        def _(pe):
            pe.wait_ge(con_in, 16)
            pe.wait_ge(patch_w_in, 16 * 4)
            n = 0
            for f2 in range(2):
                for c in range(C):
                    last = pe.matmul(bank[7][:, 0:D], spread(b1v[:, f2, c:c + 1], 1, P), wl[:, f2, c, :],
                                     start=(n == 0), stop=(n == 2 * C - 1))
                    n += 1
            last.then_inc(pe_bias, 1)
            pe.wait_ge(cfg_ready, 1)
            for t in range(2):
                last = pe.transpose(bank[6][0:32, t * NAT:(t + 1) * NAT], cfg2[:, t, :], ident[0:NAT, 0:NAT])
            last.then_inc(pe_cfgT, 1)

            def table_of_atoms():
                pe.wait_ge(cfgT_ready, 1)
                pe.wait_ge(idx_step, 3)
                pe.transpose(bank[6][:, 256:256 + B], txt_f[:], ident[0:B, 0:B])
                pe.wait_ge(bias_ready, 1)
                for t in range(2):
                    last = pe.matmul(bank[7][0:NAT, 0:D], cfgT[0:NCFG, t, :], emb[:, t, :], start=(t == 0), stop=(t == 1))
                last.then_inc(pe_table, 1)

            def patch_transpose(i):
                pe.wait_ge(patch_norm, i + 1)
                if i >= 2:
                    pe.wait_ge(act_patchT, i - 1)
                for c in range(2 * C):
                    last = pe.transpose(bank[2 * (i % 2) + c // 3][:, (c % 3) * PR:(c % 3 + 1) * PR], xni[i % 2][:, c, :],
                                        ident[0:PR, 0:PR])
                last.then_inc(pe_patchT, 1)

            def patch_embed(k):
                pe.wait_ge(act_patchT, k + 1)
                if k >= 2:
                    pe.wait_ge(patch_y, k - 1)
                for c in range(2 * C):
                    last = pe.matmul(bank[4 + k % 2][0:PR, 0:D], xTi[k % 2][:, c, :], wlg[:, c % 2, c // 2, :],
                                     start=(c == 0), stop=(c == 2 * C - 1))
                last.then_inc(pe_patchY, 1)

            pe.wait_ge(patch_w_ready, 1)
            patch_transpose(0)
            table_of_atoms()
            for i in range(1, 2 * G):
                patch_transpose(i)
                patch_embed(i - 1)
                if i == 3:
                    pe.wait_ge(route_w_in, 80)
                    pe.wait_ge(table_ready, 2)
                    pe.transpose(bank[6][:, 0:E * FC], b1r[:], ident[0:E * FC, 0:E * FC]).then_inc(pe_b1T, 1)
            patch_embed(2 * G - 1)
            pe.wait_ge(late_ready, 3)
            pe.wait_ge(w_ready, 3)
            pe.wait_ge(const_ready, 1)

            def project(dst, which, f, groups):
                s = f.slot(2)
                for g in groups:
                    cols = slice(g * P, (g + 1) * P)
                    n = 0
                    for k in range(2):
                        for w, v in ((wqk_hi, xh), (wqk_lo, xh), (wqk_hi, xl)):
                            last = pe.matmul(dst[:, g * S:(g + 1) * S], w[:, k, which, cols], v[s][:, k, 0:S],
                                             start=(n == 0), stop=(n == 5))
                            n += 1
                return last

            def project_values(f):
                s = f.slot(2)
                wv_hi = wqk_hi[:].rearrange("p k q (h t d) -> p k q h t d", h=H, t=2)
                wv_lo = wqk_lo[:].rearrange("p k q (h t d) -> p k q h t d", h=H, t=2)
                for c0, c1, r0, r1, h0, h1, o in ((0, TXT, 0, P, 0, H, 0), (TXT, SP, 0, 64, 0, H, D),
                                                  (TXT, SP, 64, P, HJ, 2 * HJ, D)):
                    n = 0
                    for k in range(2):
                        for w, v in ((wv_hi, xh), (wv_lo, xh), (wv_hi, xl)):
                            last = pe.matmul(bank[2][r0:r1, o + h0 * DH:o + h1 * DH].rearrange("p (h d) -> p h d", d=DH),
                                             v[s][:, k, c0:c1], w[:, k, 1, h0:h1, 0, :], start=(n == 0), stop=(n == 5))
                            n += 1
                return last

            quarters = ((0, 0, 0), (64, 0, 1), (0, 1, 2), (64, 1, 2))

            def max_part(f, m):
                j, images = m // 2, m % 2
                s, rows = f.slot(2), slice(32 * (m // 2), 32 * (m // 2) + 32)
                if m == 0:
                    q_st2.wait(pe, f.plus(-1))
                    k_st1.wait(pe, f)
                    q_hi.wait(pe, f)
                elif m == 1:
                    max_taken.wait(pe, f.plus(-1))
                else:
                    max_taken.wait(pe, f, m - 1)
                if images:
                    for r, c, g in quarters:
                        last = pe.matmul(bank[0][r:r + 64, c * S:(c + 1) * S], q1[s][rows, g, TXT:SP], k1[s][rows, g, 0:S],
                                         start=True, stop=True)
                else:
                    for g in range(HG):
                        last = pe.matmul(bank[7][:, g * S:(g + 1) * S], q1[s][rows, g, 0:TXT], k1[s][rows, g, 0:S],
                                         start=True, stop=True)
                last.then_inc(max_scores.sem, 1)

            def scores(a, j):
                s, rows = a.slot(2), slice(32 * j, 32 * j + 32)
                if j == 0:
                    q_st2.wait(pe, a)
                    k_st2.wait(pe, a)
                    exp_a.wait(pe, a.plus(-1))
                else:
                    exp_a.wait(pe, a, j)
                for g in range(HG):
                    for n, (kk, qq) in enumerate(((k1, q1), (k2, q2))):
                        last = pe.matmul(bank[4][:, g * S:(g + 1) * S], kk[s][rows, g, 0:TXT], qq[s][rows, g, 0:S],
                                         start=(n == 0), stop=(n == 1))
                last.then_inc(sc_a.sem, 1)
                if j == 0:
                    exp_b.wait(pe, a.plus(-1))
                else:
                    exp_b.wait(pe, a, j)
                for r, c, g in quarters:
                    for n, (kk, qq) in enumerate(((k1, q1), (k2, q2))):
                        last = pe.matmul(bank[5][r:r + 64, c * S:(c + 1) * S], kk[s][rows, g, TXT:SP], qq[s][rows, g, 0:S],
                                         start=(n == 0), stop=(n == 1))
                last.then_inc(sc_b.sem, 1)

            def weigh(a):
                s = a.slot(2)
                v_out.wait(pe, a)
                o_norm.wait(pe, a.plus(-1))
                exp_a.wait(pe, a)
                exp_b.wait(pe, a)
                for g in range(HG):
                    c = quarters[g][1]
                    for t, (w, cols) in enumerate(((pa, g), (pb, c))):
                        for j in range(HJ):
                            last = pe.matmul(bank[6][32 * j:32 * j + 32, g * S:(g + 1) * S], V[s][:, t, HJ * g + j, :],
                                             w[j][:, cols * S:(cols + 1) * S], start=(t == 0), stop=(t == 1))
                last.then_inc(pv.sem, 1)

            def transpose_rows(rows):
                for k in range(2):
                    for t, (c0, c1) in enumerate(((0, TXT), (TXT, SP))):
                        last = pe.transpose(bank[3][0:DK, k * SP + c0:k * SP + c1], rows[0:c1 - c0, t, k * DK:(k + 1) * DK],
                                            ident[0:c1 - c0, 0:c1 - c0])
                return last

            def output_projection(t):
                rows, c0, c1, o = ((P, 0, TXT, 0), (NIMG, TXT, S, D))[t]
                n = 0
                for g in range(HG):
                    for v, w in ((oth, wo_hi), (oth, wo_lo), (otl, wo_hi)):
                        last = pe.matmul(bank[1][0:rows, o:o + D], v[:, g, c0:c1], w[:, g, :],
                                         start=(n == 0), stop=(n == 3 * HG - 1))
                        n += 1
                return last

            def step(s, l, f, m, a, p, r):
                if a.exists(B):
                    scores(a, 0)
                if m.exists(B):
                    k_st1.wait(pe, m)
                    project_values(m).then_inc(v_proj.sem, 1)
                if m.exists(B):
                    max_part(m, 0)
                if a.exists(B):
                    scores(a, 1)
                if r.exists(B):
                    x2_norm.wait(pe, r)
                    if f.plus(-1).exists(B):
                        q_rest.wait(pe, f.plus(-1))
                    x2_lo.wait(pe, r.plus(-1))
                    transpose_rows(xn2).then_inc(x2_T.sem, 1)
                if m.exists(B):
                    max_part(m, 1)
                if f.exists(B):
                    x_lo.wait(pe, f)
                    v_out.wait(pe, f.plus(-1))
                    project(bank[2], 1, f, (0, 1))
                if m.exists(B):
                    max_part(m, 2)
                if a.exists(B):
                    scores(a, 2)
                if m.exists(B):
                    max_part(m, 3)
                if r.exists(B):
                    x2_lo.wait(pe, r)
                    h_sum.wait(pe, r)
                    slots.wait(pe, r.plus(-1))
                    for t in range(2):
                        for k in range(2):
                            for n, (x2, w) in enumerate(((x2h, ws_hi), (x2h, ws_lo), (x2l, ws_hi), (x2l, ws_lo))):
                                last = pe.matmul(bank[1][:, LG + t * E:LG + (t + 1) * E], x2[:, k, t * P:(t + 1) * P],
                                                 w[:, k, :], start=(k == 0 and n == 0), stop=(k == 1 and n == 3))
                    last.then_inc(logits.sem, 1)
                if l.exists(B):
                    x_norm.wait(pe, l)
                    q_rest.wait(pe, l.plus(-2))
                    x_lo.wait(pe, l.plus(-1))
                    x2_lo.wait(pe, r)
                    transpose_rows(xn).then_inc(x_T.sem, 1)
                if m.exists(B):
                    max_part(m, 4)
                if f.exists(B):
                    project(bank[2], 1, f, (2,)).then_inc(k_proj.sem, 1)
                if m.exists(B):
                    max_part(m, 5)
                if a.exists(B):
                    scores(a, 3)
                if p.exists(B):
                    o_lo.wait(pe, p)
                    onehot.wait(pe, r, 1)
                    slots.wait(pe, p.plus(-2))
                    output_projection(0)
                if p.exists(B):
                    output_projection(1).then_inc(o_proj.sem, 1)
                if m.exists(B):
                    max_part(m, 6)
                if m.exists(B):
                    max_part(m, 7)
                if a.exists(B):
                    weigh(a)
                if m.exists(B):
                    max_taken.wait(pe, m)
                    for g in range(HG):
                        e, c, _ = quarters[g]
                        pe.matmul(bank[7][:, g * S:g * S + TXT], mxa[:, g, :], neg_id[:], start=True, stop=True)
                        last = pe.matmul(bank[7][:, g * S + TXT:(g + 1) * S], mxb[:, c, :], neg_id[:, e:e + NIMG],
                                         start=True, stop=True)
                    last.then_inc(max_rows.sem, 1)
                if r.exists(B):
                    onehot.wait(pe, r)
                    if p.exists(B):
                        h_sum.wait(pe, p)
                    o = LG + 2 * E
                    pe.matmul(bank[1][:, o:o + E], tri[:], ohb[:, 0, :], start=True, stop=True)
                    pe.matmul(bank[1][:, o + E:o + 2 * E], tri[:], ohb[:, 1, :], start=True, stop=False)
                    pe.matmul(bank[1][:, o + E:o + 2 * E], ones[:], ohb[:, 0, :], start=False, stop=True)
                    pe.matmul(bank[1][:, o + 2 * E:o + 3 * E], ones[:], ohb[:, 0, :], start=True, stop=False)
                    pe.matmul(bank[1][:, o + 2 * E:o + 3 * E], ones[:], ohb[:, 1, :], start=False, stop=True)\
                        .then_inc(ranks.sem, 1)
                if f.exists(B):
                    if l.exists(B):
                        x_lo.wait(pe, l)
                    x2_lo.wait(pe, r)
                    project(bank[3], 0, f, range(HG)).then_inc(q_proj.sem, 1)

            attend_steps(pe, step)
            w1_split.wait(pe, Turn(B // 2 - 1))
            w2_split.wait(pe, Turn(B // 2 - 1))
            pe.wait_ge(words_ready, 1)
            slots.wait(pe, Turn(B - 1))
            o_norm.wait(pe, Turn(B - 1))

            expert_of = expert_reader(pe)
            AHEAD = 2

            def expert_slices(weights, ex, size, parts, stationary):
                for i in range(0, len(parts), AHEAD):
                    group = [[w[:].bitcast(U8)[:, bass.ds(ex * (size * 2) + c0 * 2, n * 2)].bitcast(F16) for w in weights]
                             for c0, n in parts[i:i + AHEAD]]
                    for halves in group:
                        for w in halves:
                            pe.lower_ap(w, for_matmul_weights=stationary)
                    yield from group

            def estep(t, h, y):
                if t.exists(NT):
                    e_norm.wait(pe, t)
                    e_lo.wait(pe, t.plus(-1))
                    for k in range(2):
                        last = pe.transpose(bank[0][0:DK, k * P:(k + 1) * P], xe[t.slot(2)][:, k * DK:(k + 1) * DK], ident)
                    last.then_inc(e_T.sem, 1)
                if h.exists(NT):
                    s = h.slot(2)
                    e_lo.wait(pe, h)
                    ex = expert_of(t, h)
                    e_gelu.wait(pe, h.plus(-2))
                    we = expert_slices((w1_hi, w1_lo), ex, 2 * F,
                                       [(k * F + fc * P, P) for fc in range(FC) for k in range(2)], stationary=True)
                    for fc in range(FC):
                        n = 0
                        for k in range(2):
                            we_hi, we_lo = next(we)
                            for w, v in ((we_hi, xeh), (we_lo, xeh), (we_hi, xel)):
                                last = pe.matmul(bank[2 + 2 * s + fc // 3][:, fc % 3 * P:(fc % 3 + 1) * P],
                                                 w, v[s][:, k, :], start=(n == 0), stop=(n == 5))
                                n += 1
                        if fc % 3 == 2:
                            last.then_inc(e_h.sem, 1)
                if y.exists(NT):
                    s = y.slot(2)
                    ex = expert_of(t, y)
                    e_res.wait(pe, y.plus(-2))
                    dst = bank[6 + s][:, 0:D]
                    row = bass.ds(ex * D, D)
                    we = expert_slices((w2_hi, w2_lo), ex, FC * D, [(fc * D, D) for fc in range(FC)],
                                       stationary=False)
                    pe.matmul(dst, one16[:], b2_hi[:, row], start=True, stop=False)
                    pe.matmul(dst, one16[:], b2_lo[:, row], start=False, stop=False)
                    for fc in range(FC):
                        if fc % 3 == 0:
                            e_hl.wait(pe, y, fc // 3 + 1)
                        we_hi, we_lo = next(we)
                        for n, (v, w) in enumerate(((hh, we_hi), (hh, we_lo), (hl, we_hi))):
                            last = pe.matmul(dst, v[s][:, fc, :], w, start=False,
                                             stop=(fc == FC - 1 and n == 2))
                    last.then_inc(e_y.sem, 1)

            expert_steps(pe, estep)


_INS = ["x", "x_txt", "L0_tok_ln1_g", "L0_tok_ln1_b", "L0_tok_W_lin", "L0_tok_b_lin", "L0_tok_ln2_g", "L0_tok_ln2_b",
        "L0_tok_pos_embedding", "L0_tok_cls_token", "L0_txt_atom_configs", "L0_txt_subshell_embeds",
        "L0_txt_occupancy_embeds", "L0_attn_w_qkv", "L0_attn_w_out", "L0_ffn_Ws", "L0_ffn_bs", "L0_ffn_W1", "L0_ffn_b1",
        "L0_ffn_W2", "L0_ffn_b2"]


def kernel(**inputs):
    import concourse.bacc as _bacc
    from concourse.bass_utils import run_bass_kernel_spmd as _run

    nc = _bacc.Bacc("TRN2", target_bir_lowering=False, num_devices=1)
    arrays, args = {}, []
    for name in _INS:
        a = np.ascontiguousarray(inputs[name])
        arrays[f"in_{name}"] = a
        args.append(nc.dram_tensor(f"in_{name}", a.shape, mybir.dt.from_np(a.dtype), kind="ExternalInput").ap())
    arrays["consts"] = shape_constants()
    args.append(nc.dram_tensor("consts", arrays["consts"].shape, F32, kind="ExternalInput").ap())
    args.append(nc.dram_tensor("out", (T, D), F32, kind="ExternalOutput").ap())
    build(nc, *args)
    r = _run(nc, [arrays], core_ids=[0])
    return r.results[0]["out"].reshape(B, S, D)
```
